# Optimizing a Trainium2 kernel written in Bass

```python
import numpy as np
import jax
import jax.numpy as jnp

def _softmax(x, axis=-1):
    return jax.nn.softmax(x, axis=axis)

def _gelu(x):
    return jax.nn.gelu(x, approximate=True)

def _silu(x):
    return jax.nn.silu(x)

def _sigmoid(x):
    return jax.nn.sigmoid(x)

def _layernorm(x, axis=-1, eps=1e-05):
    m = jnp.mean(x, axis=axis, keepdims=True)
    v = jnp.var(x, axis=axis, keepdims=True)
    return (x - m) / jnp.sqrt(v + eps)

def _scatter_add(tgt, idx, src, axis=0):
    return tgt.at[idx].add(src)

def _segment_sum(src, seg, n):
    return jax.ops.segment_sum(src, seg, n)
kernel_name = 'mk_macaron_d2_jaxref_r8_5faf2a'

def setup_inputs(seed: int=0):
    np.random.seed(seed)
    _w = jnp.asarray

    def _L0_attn_setup():
        import jax, jax.numpy as jnp
        import numpy as np
        D_MODEL, N_HEADS = (128, 16)
        D_H = D_MODEL // N_HEADS
        D_HR = D_H // 2
        D_LATENT = 32
        THETA = 10000.0

        def rope(x, theta=THETA):
            S, d = (x.shape[-2], x.shape[-1])
            inv = theta ** (-jnp.arange(0, d, 2, dtype=jnp.float32) / d)
            ang = jnp.arange(S, dtype=jnp.float32)[:, None] * inv
            cos, sin = (jnp.cos(ang), jnp.sin(ang))
            x1, x2 = (x[..., 0::2], x[..., 1::2])
            r1 = x1 * cos - x2 * sin
            r2 = x1 * sin + x2 * cos
            return jnp.stack([r1, r2], axis=-1).reshape(x.shape)
        key = jax.random.key(seed)
        ks = jax.random.split(key, 9)
        s = lambda fan_in: 1.0 / np.sqrt(fan_in)
        return {'x': jax.random.normal(ks[0], (4, 256, D_MODEL), jnp.float32), 'W_DQ': jax.random.normal(ks[1], (D_MODEL, D_LATENT), jnp.float32) * s(D_MODEL), 'W_UQ': jax.random.normal(ks[2], (D_LATENT, N_HEADS * D_H), jnp.float32) * s(D_LATENT), 'W_QR': jax.random.normal(ks[3], (D_LATENT, N_HEADS * D_HR), jnp.float32) * s(D_LATENT), 'W_DKV': jax.random.normal(ks[4], (D_MODEL, D_LATENT), jnp.float32) * s(D_MODEL), 'W_UK': jax.random.normal(ks[5], (D_LATENT, N_HEADS * D_H), jnp.float32) * s(D_LATENT), 'W_UV': jax.random.normal(ks[6], (D_LATENT, N_HEADS * D_H), jnp.float32) * s(D_LATENT), 'W_KR': jax.random.normal(ks[7], (D_MODEL, D_HR), jnp.float32) * s(D_MODEL), 'W_O': jax.random.normal(ks[8], (N_HEADS * D_H, D_MODEL), jnp.float32) * s(N_HEADS * D_H)}
    _L0_attn_in = _L0_attn_setup()

    def _L0_ffn_setup():
        import jax, jax.numpy as jnp
        import numpy as np
        NUM_EXPERTS = 8
        TOP_K = 2

        def _swiglu(x, w1, w2, w3):
            return jax.nn.silu(x @ w1) * (x @ w3) @ w2
        key = jax.random.key(seed)
        ks = jax.random.split(key, 9)
        B, S, D, H, E = (1, 128, 128, 128, NUM_EXPERTS)
        std = 0.02
        return {'x': jax.random.normal(ks[0], (B, S, D), jnp.float32), 'router_w': jax.random.normal(ks[1], (D, E), jnp.float32) * std, 'expert_bias': jnp.zeros((E,), jnp.float32), 'w1': jax.random.normal(ks[2], (E, D, H), jnp.float32) * std, 'w2': jax.random.normal(ks[3], (E, H, D), jnp.float32) * std, 'w3': jax.random.normal(ks[4], (E, D, H), jnp.float32) * std, 'sw1': jax.random.normal(ks[5], (D, H), jnp.float32) * std, 'sw2': jax.random.normal(ks[6], (H, D), jnp.float32) * std, 'sw3': jax.random.normal(ks[7], (D, H), jnp.float32) * std}
    _L0_ffn_in = _L0_ffn_setup()

    def _L1_attn_setup():
        import jax, jax.numpy as jnp
        import numpy as np
        SHIFTS = (-32, -16, -4, -1, 1, 4, 16, 32)
        LN_EPS = 1e-05
        key = jax.random.key(seed)
        k_x, k_g, k_v, k_gm, k_bt = jax.random.split(key, 5)
        B, L, D = (4, 512, 128)
        n = len(SHIFTS) + 1
        scale = 1.0 / np.sqrt(D)
        x = jax.random.normal(k_x, (B, L, D), dtype=jnp.float32)
        gate_W = jax.random.normal(k_g, (n * D, D), dtype=jnp.float32) * scale
        value_W = jax.random.normal(k_v, (D, D), dtype=jnp.float32) * scale
        gamma = jnp.ones((D,), dtype=jnp.float32)
        beta = jnp.zeros((D,), dtype=jnp.float32)
        return {'x': x, 'gate_W': gate_W, 'value_W': value_W, 'gamma': gamma, 'beta': beta}
    _L1_attn_in = _L1_attn_setup()

    def _L1_ffn_setup():
        import jax, jax.numpy as jnp
        import numpy as np
        DIM = 128
        DEPTH = 7
        PAR = 8
        N_NODES = 2 ** (DEPTH + 1) - 1
        WIDTH = PAR * N_NODES
        key = jax.random.key(seed)
        k1, k2, k3, k4 = jax.random.split(key, 4)
        init_k = float(np.sqrt(1.0 / DIM))
        init_k2 = float(np.sqrt(1.0 / ((DEPTH + 1) * PAR)))
        oldx = jax.random.normal(k1, (4, 256, DIM), dtype=jnp.float32)
        W_in = jax.random.uniform(k2, (WIDTH, DIM), jnp.float32, -init_k, init_k)
        b_in = jax.random.uniform(k3, (WIDTH,), jnp.float32, -init_k, init_k)
        W_out = jax.random.uniform(k4, (DIM, WIDTH), jnp.float32, -init_k2, init_k2)
        return {'oldx': oldx, 'W_in': W_in, 'b_in': b_in, 'W_out': W_out}
    _L1_ffn_in = _L1_ffn_setup()
    _d = {'L0_attn_x': _L0_attn_in['x'], 'L0_attn_W_DQ': _L0_attn_in['W_DQ'], 'L0_attn_W_UQ': _L0_attn_in['W_UQ'], 'L0_attn_W_QR': _L0_attn_in['W_QR'], 'L0_attn_W_DKV': _L0_attn_in['W_DKV'], 'L0_attn_W_UK': _L0_attn_in['W_UK'], 'L0_attn_W_UV': _L0_attn_in['W_UV'], 'L0_attn_W_KR': _L0_attn_in['W_KR'], 'L0_attn_W_O': _L0_attn_in['W_O'], 'L0_ffn_router_w': _L0_ffn_in['router_w'], 'L0_ffn_expert_bias': _L0_ffn_in['expert_bias'], 'L0_ffn_w1': _L0_ffn_in['w1'], 'L0_ffn_w2': _L0_ffn_in['w2'], 'L0_ffn_w3': _L0_ffn_in['w3'], 'L0_ffn_sw1': _L0_ffn_in['sw1'], 'L0_ffn_sw2': _L0_ffn_in['sw2'], 'L0_ffn_sw3': _L0_ffn_in['sw3'], 'L1_attn_gate_W': _L1_attn_in['gate_W'], 'L1_attn_value_W': _L1_attn_in['value_W'], 'L1_attn_gamma': _L1_attn_in['gamma'], 'L1_attn_beta': _L1_attn_in['beta'], 'L1_ffn_W_in': _L1_ffn_in['W_in'], 'L1_ffn_b_in': _L1_ffn_in['b_in'], 'L1_ffn_W_out': _L1_ffn_in['W_out']}
    _x0 = _d['L0_attn_x']
    _d['L0_attn_x'] = jax.random.normal(jax.random.fold_in(jax.random.key(seed), 1), (4, 512, 128), dtype=_x0.dtype)
    del _x0
    return _d

def reference(L0_attn_x, L0_attn_W_DQ, L0_attn_W_UQ, L0_attn_W_QR, L0_attn_W_DKV, L0_attn_W_UK, L0_attn_W_UV, L0_attn_W_KR, L0_attn_W_O, L0_ffn_router_w, L0_ffn_expert_bias, L0_ffn_w1, L0_ffn_w2, L0_ffn_w3, L0_ffn_sw1, L0_ffn_sw2, L0_ffn_sw3, L1_attn_gate_W, L1_attn_value_W, L1_attn_gamma, L1_attn_beta, L1_ffn_W_in, L1_ffn_b_in, L1_ffn_W_out):

    def _L0_attn_ref(x, W_DQ, W_UQ, W_QR, W_DKV, W_UK, W_UV, W_KR, W_O):
        import jax, jax.numpy as jnp
        import numpy as np
        D_MODEL, N_HEADS = (128, 16)
        D_H = D_MODEL // N_HEADS
        D_HR = D_H // 2
        D_LATENT = 32
        THETA = 10000.0

        def rope(x, theta=THETA):
            S, d = (x.shape[-2], x.shape[-1])
            inv = theta ** (-jnp.arange(0, d, 2, dtype=jnp.float32) / d)
            ang = jnp.arange(S, dtype=jnp.float32)[:, None] * inv
            cos, sin = (jnp.cos(ang), jnp.sin(ang))
            x1, x2 = (x[..., 0::2], x[..., 1::2])
            r1 = x1 * cos - x2 * sin
            r2 = x1 * sin + x2 * cos
            return jnp.stack([r1, r2], axis=-1).reshape(x.shape)
        B, S, _ = x.shape
        d_qk = D_H + D_HR
        c_q = x @ W_DQ
        Qc = (c_q @ W_UQ).reshape(B, S, N_HEADS, D_H).transpose(0, 2, 1, 3)
        Qr = (c_q @ W_QR).reshape(B, S, N_HEADS, D_HR).transpose(0, 2, 1, 3)
        Qr = rope(Qr)
        c_kv = x @ W_DKV
        Kc = (c_kv @ W_UK).reshape(B, S, N_HEADS, D_H).transpose(0, 2, 1, 3)
        Kr = rope((x @ W_KR)[:, None, :, :])
        Kr = jnp.broadcast_to(Kr, (B, N_HEADS, S, D_HR))
        V = (c_kv @ W_UV).reshape(B, S, N_HEADS, D_H).transpose(0, 2, 1, 3)
        Q = jnp.concatenate([Qc, Qr], axis=-1)
        K = jnp.concatenate([Kc, Kr], axis=-1)
        scores = jnp.einsum('bhqd,bhkd->bhqk', Q, K)
        scores = jnp.clip(scores, -80.0, 80.0)
        causal = jnp.tril(jnp.ones((S, S), dtype=bool))
        scores = jnp.where(causal, scores, -jnp.inf)
        weights = jax.nn.softmax(scores / jnp.sqrt(jnp.float32(d_qk)), axis=-1)
        attn = jnp.einsum('bhqk,bhkd->bhqd', weights, V)
        attn = attn.transpose(0, 2, 1, 3).reshape(B, S, N_HEADS * D_H)
        return attn @ W_O

    def _L0_ffn_ref(x, router_w, expert_bias, w1, w2, w3, sw1, sw2, sw3):
        import jax, jax.numpy as jnp
        import numpy as np
        NUM_EXPERTS = 8
        TOP_K = 2

        def _swiglu(x, w1, w2, w3):
            return jax.nn.silu(x @ w1) * (x @ w3) @ w2
        B, S, D = x.shape
        E, K = (NUM_EXPERTS, TOP_K)
        N = B * S
        x_flat = x.reshape(N, D)
        logits = x_flat @ router_w
        scores = jax.nn.softmax(logits.astype(jnp.float32), axis=-1)
        _, sel = jax.lax.top_k(scores + expert_bias[None, :], K)
        top_scores = jnp.take_along_axis(scores, sel, axis=-1)
        flat_exp = sel.reshape(-1)
        order = jnp.argsort(flat_exp)
        exp_sorted = flat_exp[order]
        routed_input = x_flat[order // K]
        routed_output = jnp.zeros_like(routed_input)
        for e in range(E):
            mask = (exp_sorted == e)[:, None]
            y_e = _swiglu(routed_input, w1[e], w2[e], w3[e])
            routed_output = routed_output + jnp.where(mask, y_e, 0.0)
        unsorted = jnp.zeros((N * K, D), routed_output.dtype).at[order].set(routed_output)
        unsorted = unsorted.reshape(N, K, D)
        out_experts = jnp.einsum('nk,nkd->nd', top_scores, unsorted)
        shared_out = _swiglu(x_flat, sw1, sw2, sw3)
        return (shared_out + out_experts).reshape(B, S, D)

    def _L1_attn_ref(x, gate_W, value_W, gamma, beta):
        import jax, jax.numpy as jnp
        import numpy as np
        SHIFTS = (-32, -16, -4, -1, 1, 4, 16, 32)
        LN_EPS = 1e-05
        B, L, D = x.shape
        n = len(SHIFTS) + 1
        v = jnp.einsum('bld,ed->ble', x, value_W)
        stacked = jnp.stack([v] + [jnp.roll(v, -s, axis=1) for s in SHIFTS], axis=2)
        gates = jax.nn.sigmoid(jnp.einsum('bld,ed->ble', x, gate_W))
        gates = gates.reshape(B, L, n, D)
        out = jnp.sum(stacked * gates, axis=2)
        mu = jnp.mean(out, axis=-1, keepdims=True)
        var = jnp.mean(jnp.square(out - mu), axis=-1, keepdims=True)
        return (out - mu) * jax.lax.rsqrt(var + LN_EPS) * gamma + beta

    def _L1_ffn_ref(oldx, W_in, b_in, W_out):
        import jax, jax.numpy as jnp
        import numpy as np
        DIM = 128
        DEPTH = 7
        PAR = 8
        N_NODES = 2 ** (DEPTH + 1) - 1
        WIDTH = PAR * N_NODES
        x = oldx.reshape(-1, DIM)
        B = x.shape[0]
        logits = x @ W_in.T + b_in
        decisions = (logits > 0).astype(jnp.int32).reshape(B, PAR, N_NODES)
        acts = jax.nn.silu(logits).reshape(B, PAR, N_NODES)
        current = jnp.zeros((B, PAR), dtype=jnp.int32)
        dmap = jax.nn.one_hot(current, N_NODES, dtype=acts.dtype)
        for d in range(DEPTH):
            cur_platform = 2 ** d - 1
            next_platform = 2 ** (d + 1) - 1
            moves = jnp.take_along_axis(decisions, current[..., None], axis=2)[..., 0]
            current = (current - cur_platform) * 2 + moves + next_platform
            dmap = dmap + jax.nn.one_hot(current, N_NODES, dtype=acts.dtype)
        masked = acts * jax.lax.stop_gradient(dmap)
        out = masked.reshape(B, WIDTH) @ W_out.T
        return out.reshape(oldx.shape)
    x = L0_attn_x
    x = x + 0.5 * _L0_ffn_ref(_layernorm(x, axis=-1), L0_ffn_router_w, L0_ffn_expert_bias, L0_ffn_w1, L0_ffn_w2, L0_ffn_w3, L0_ffn_sw1, L0_ffn_sw2, L0_ffn_sw3)
    x = x + _L0_attn_ref(_layernorm(x, axis=-1), L0_attn_W_DQ, L0_attn_W_UQ, L0_attn_W_QR, L0_attn_W_DKV, L0_attn_W_UK, L0_attn_W_UV, L0_attn_W_KR, L0_attn_W_O)
    x = x + 0.5 * _L0_ffn_ref(_layernorm(x, axis=-1), L0_ffn_router_w, L0_ffn_expert_bias, L0_ffn_w1, L0_ffn_w2, L0_ffn_w3, L0_ffn_sw1, L0_ffn_sw2, L0_ffn_sw3)
    x = x + 0.5 * _L1_ffn_ref(_layernorm(x, axis=-1), L1_ffn_W_in, L1_ffn_b_in, L1_ffn_W_out)
    x = x + _L1_attn_ref(_layernorm(x, axis=-1), L1_attn_gate_W, L1_attn_value_W, L1_attn_gamma, L1_attn_beta)
    x = x + 0.5 * _L1_ffn_ref(_layernorm(x, axis=-1), L1_ffn_W_in, L1_ffn_b_in, L1_ffn_W_out)
    return x

_drawn_inputs = setup_inputs


def setup_inputs(seed=0):
    import zlib

    import numpy as np

    out = dict(_drawn_inputs(seed))
    spreads = {'L0_ffn_expert_bias': (0.0, 0.8), 'L1_attn_gamma': (1.0, 0.2), 'L1_attn_beta': (0.0, 0.1)}
    factors = {'L0_ffn_router_w': 8.0,
     'L0_ffn_w1': 8.0,
     'L0_ffn_w2': 8.0,
     'L0_ffn_w3': 8.0,
     'L0_ffn_sw1': 4.369,
     'L0_ffn_sw2': 4.492,
     'L0_ffn_sw3': 4.307}
    for name, (base, spread) in spreads.items():
        noise = np.random.default_rng([zlib.crc32(name.encode()), seed]).standard_normal(out[name].shape)
        drawn = base * np.exp(spread * noise) if base else spread * noise
        out[name] = jnp.asarray(drawn.astype(out[name].dtype))
    for name, factor in factors.items():
        out[name] = (out[name] * factor).astype(out[name].dtype)
    return out
```

```python
from contextlib import ExitStack

import numpy as np

import concourse.bass as bass
from concourse import mybir

F32 = mybir.dt.float32
F32R = mybir.dt.float32r
BF16 = mybir.dt.bfloat16
ALU = mybir.AluOpType
ACT = mybir.ActivationFunctionType
AX = mybir.AxisListType

P = 128
NB = 4
L = 512
TT = L // P
NE = 8
NX = NE + 1
NH = 16
NPAIR = NH // 2
DL = 32
DH, DR = 8, 4
TREES = 8
DEPTH = 7
NCH = 2 * TREES
SHIFTS = (0, -32, -16, -4, -1, 1, 4, 16, 32)
PADV = 32
EPS = 1e-5
QK_SCALE = float(1.0 / np.sqrt(np.float32(DH + DR)))
P_LOW = float(np.exp(-80.0 * QK_SCALE))
P_HIGH = float(np.exp(80.0 * QK_SCALE))
N_PHASES = 6
PHASES = ("moe0", "attn", "moe1", "tree0", "mix", "tree1")


def shape_constants():
    ident = np.eye(P, dtype=np.float32)
    sel = np.zeros((P, NE, P), np.float32)
    for e in range(NE):
        sel[e, e] = 1.0
        sel[NE + e, e] = 1.0
    before = np.broadcast_to(np.tril(np.ones((NE, NE), np.float32), -1).reshape(1, -1), (P, NE * NE))
    path = np.zeros((P, 2, P), np.float32)
    target = np.full((P, 2), 99.0, np.float32)
    for n in range(2 ** (DEPTH + 1) - 1):
        c, i = (0, n) if n < 127 else (1, n - 127)
        target[i, c] = 0.0
        m = n
        while m > 0:
            parent = (m - 1) // 2
            right = m == 2 * parent + 2
            path[parent, c, i] = -1.0 if right else 1.0
            target[i, c] -= 1.0 if right else 0.0
            m = parent
    inv = np.float32(10000.0) ** (-np.arange(0, DR, 2, dtype=np.float32) / np.float32(DR))
    ang = np.arange(L, dtype=np.float32)[:, None] * inv.astype(np.float32)
    cos = np.repeat(np.cos(ang).astype(np.float32), 2, axis=1).T
    sin = np.repeat(np.sin(ang).astype(np.float32), 2, axis=1).T * np.array([-1, 1, -1, 1], np.float32)[:, None]
    rope_k = np.ones((P, L), np.float32)
    for r in (3 * DL, 3 * DL + 8):
        rope_k[r:r + 4] = cos
        rope_k[r + 4:r + 8] = sin
    rope_q = np.ones((P, L), np.float32)
    for half in (0, 64):
        for blk in range(3):
            r = half + 16 * blk + DH
            rope_q[r:r + 4] = cos
            rope_q[r + 4:r + 8] = sin
    low = np.zeros((P, 5), np.float32)
    low[DL:2 * DL, 0] = -1
    low[DL:2 * DL, 1] = -1
    low[3 * DL + 8:3 * DL + 16, 1] = -1
    low[2 * DL:3 * DL, 2] = -1
    for half in (0, 64):
        low[half + 16:half + 32, 3] = -1
        low[half + 32:half + 48, 4] = -1
    k, q = np.arange(P)[:, None], np.arange(P)[None, :]
    cap = np.where(k <= q, np.float32(P_HIGH), np.float32(0)).astype(np.float32)
    cap = np.stack([cap, cap], axis=1)
    return [("ident", ident), ("sel", sel.reshape(P, -1)), ("before", np.ascontiguousarray(before)),
            ("path", path.reshape(P, -1)), ("target", target), ("rope_k", rope_k), ("rope_q", rope_q),
            ("low", low), ("cap", cap.reshape(P, -1))]


def lay_out(x):
    g = {k: np.asarray(v) for k, v in x.items()}
    f = np.float32
    out = {}
    out["x"] = g["L0_attn_x"]
    up = np.zeros((P, NX, 2, P), f)
    down = np.zeros((P, NX, P), f)
    up[:, 0, 0], up[:, 0, 1], down[:, 0] = g["L0_ffn_sw1"], g["L0_ffn_sw3"], g["L0_ffn_sw2"]
    up[:, 1:, 0] = g["L0_ffn_w1"].transpose(1, 0, 2)
    up[:, 1:, 1] = g["L0_ffn_w3"].transpose(1, 0, 2)
    down[:, 1:] = g["L0_ffn_w2"].transpose(1, 0, 2)
    out["up"], out["down"] = up.reshape(P, -1), down.reshape(P, -1)
    router = np.zeros((P, P), f)
    router[:, :NE] = g["L0_ffn_router_w"]
    out["router"] = router
    out["ebias"] = np.tile(g["L0_ffn_expert_bias"][None, :], (P, 1))
    kr = g["L0_attn_W_KR"]
    swap = [1, 0, 3, 2]
    wc = np.zeros((P, 2, P), f)
    for i in range(3):
        wc[:, 0, DL * i:DL * i + DL] = g["L0_attn_W_DQ"]
        wc[:, 1, DL * i:DL * i + DL] = g["L0_attn_W_DKV"]
    for r in (3 * DL, 3 * DL + 8):
        wc[:, 1, r:r + 4] = kr
        wc[:, 1, r + 4:r + 8] = kr[:, swap]
    out["latent"] = wc.reshape(P, -1)
    uq = g["L0_attn_W_UQ"].reshape(DL, NH, DH)
    qr = g["L0_attn_W_QR"].reshape(DL, NH, DR)
    uk = g["L0_attn_W_UK"].reshape(DL, NH, DH)
    wq = np.zeros((P, NPAIR, 2, 4, 16), f)
    wk = np.zeros((P, NPAIR, 2, 4, 16), f)
    wv = np.zeros((P, P), f)
    for i in range(3):
        r = slice(DL * i, DL * i + DL)
        wv[r] = g["L0_attn_W_UV"]
        for h in range(NH):
            for blk in range(3):
                wq[r, h // 2, h % 2, blk, 0:8] = uq[:, h]
                wq[r, h // 2, h % 2, blk, 8:12] = qr[:, h]
                wq[r, h // 2, h % 2, blk, 12:16] = qr[:, h][:, swap]
                wk[r, h // 2, h % 2, blk, 0:8] = uk[:, h]
    for r in range(16):
        wk[3 * DL + r, :, :, 0:3, 8 + r % 4] = 1.0
        wk[3 * DL + r, :, :, 0:3, 12 + r % 4] = 1.0
    out["pairs"] = np.concatenate([wq.reshape(P, -1), wk.reshape(P, -1), wv], axis=1)
    out["wo"] = g["L0_attn_W_O"]
    win = g["L1_ffn_W_in"].reshape(TREES, 255, P)
    b = g["L1_ffn_b_in"].reshape(TREES, 255)
    wout = g["L1_ffn_W_out"].reshape(P, TREES, 255)
    tin = np.zeros((P, TREES, 2, P), f)
    tout = np.zeros((P, TREES, 2, P), f)
    tb = np.zeros((P, TREES, 2), f)
    for c, (a, n) in enumerate(((0, 127), (127, 128))):
        tin[:, :, c, :n] = win[:, a:a + n].transpose(2, 0, 1)
        tout[:n, :, c, :] = wout[:, :, a:a + n].transpose(2, 1, 0)
        tb[:n, :, c] = b[:, a:a + n].T
    out["tin"], out["tout"], out["tb"] = tin.reshape(P, -1), tout.reshape(P, -1), tb.reshape(P, -1)
    mw = np.zeros((P, 10, P), f)
    mw[:, 0] = g["L1_attn_value_W"].T
    mw[:, 1:] = g["L1_attn_gate_W"].reshape(9, P, P).transpose(2, 0, 1)
    out["mixw"] = mw.reshape(P, -1)
    out["gb"] = np.tile(np.concatenate([g["L1_attn_gamma"], g["L1_attn_beta"]])[None, :], (P, 1))
    for name, a in shape_constants():
        out[name] = a
    return {k: np.ascontiguousarray(v) for k, v in out.items()}


def macaron(nc, d, out, n_phases=6):
    with ExitStack() as ctx:
        def sb(name, shape, dt=F32):
            return ctx.enter_context(nc.sbuf_tensor(name, shape, dt))

        def sem(name):
            return ctx.enter_context(nc.semaphore(name))

        X = sb("X", [P, NB * TT, P])
        xhi = sb("xhi", [P, NB * L], F32R)
        xlo = sb("xlo", [P, NB * L], F32R)
        xn = sb("xn", [P, TT, P])
        stats = sb("stats", [P, TT, 6])
        mv = sb("mv", [P, TT, 2])
        veps = sb("veps", [P, TT])
        rstd = sb("rstd", [P, TT])
        mhalf = sb("mhalf", [P, TT])
        yT = sb("yT", [P, L])

        ident = sb("ident_s", [P, P])
        before = sb("before_s", [P, NE, NE])
        target = sb("target_s", [P, 2])
        rope_k = sb("rope_k_s", [P, L])
        rope_q = sb("rope_q_s", [P, L])
        low = sb("low_s", [P, 5])
        cap = sb("cap_s", [P, 2, P])
        ebias = sb("ebias_s", [P, NE])
        gb = sb("gb_s", [P, 2, P])
        tb = sb("tb_s", [P, NCH])
        down = sb("down_s", [P, NX, P])
        tout = sb("tout_s", [P, NCH, P])
        wo = sb("wo_s", [P, P])
        raw = sb("raw", [P, 19 * P])
        up_hi = sb("up_hi", [P, NX * 2, P], F32R)
        up_lo = sb("up_lo", [P, NX * 2, P], F32R)
        raw_r = sb("raw_r", [P, P])
        router_hi = sb("router_hi", [P, P], F32R)
        router_lo = sb("router_lo", [P, P], F32R)
        sel = sb("sel_s", [P, NE, P], F32R)
        lat_hi = sb("lat_hi", [P, 2, P], F32R)
        lat_lo = sb("lat_lo", [P, 2, P], F32R)
        pair_w = sb("pair_w", [P, 17, P], F32R)
        tin_hi = sb("tin_hi", [P, NCH, P], F32R)
        tin_lo = sb("tin_lo", [P, NCH, P], F32R)
        path = sb("path_s", [P, 2, P], BF16)
        mix_hi = sb("mix_hi", [P, 10, P], F32R)
        mix_lo = sb("mix_lo", [P, 10, P], F32R)

        work = sb("work", [P, 12, L])
        pb = work[:].rearrange("p (a g j) l -> p a g j l", a=2, g=3)
        act_s = work[:, 0:4, :]
        h_s = work[:, 4:8, :]
        acc_v, prod_v, acc_p = work[:, 4:6, :], work[:, 6:8, :], work[:, 8:10, :]
        prod_p = work[:, 10, :]
        sel_raw = work[:, 8:10, :].rearrange("p a l -> p (a l)")
        path_raw = work[:, 10, 0:2 * P]
        lgT = sb("lgT", [P, L])
        rt = sb("rt", [P, 8, TT, NE])
        rcmp = sb("rcmp", [P, 2, TT, NE, NE])
        rsum = sb("rsum", [P, 4, TT])
        ghl = sb("ghl", [P, TT, P])
        g_hi = sb("g_hi", [P, TT, NE], F32R)
        gT = sb("gT", [P, NB * L], F32R)
        dec = sb("dec", [P, 2, L], BF16)
        cqk = sb("cqk", [P, 2 * NB * L], F32R)
        CQ, CK = cqk[:, 0:NB * L], cqk[:, NB * L:2 * NB * L]
        pair_tmp = cqk[:, 0:17 * P]
        ck_x = sb("ck_x", [P, L])
        c_hi = sb("c_hi", [P, L], F32R)
        ck_now = sb("ck_now", [P, L], F32R)
        v_aug = sb("v_aug", [P, TT, NH, 32])
        q_x = sb("q_x", [P, L])
        q_hi = sb("q_hi", [P, L], F32R)
        k_hi = sb("k_hi", [P, L], F32R)
        QS = sb("QS", [P, 2, L], F32R)
        KS = sb("KS", [P, 2, L], F32R)
        avT = sb("avT", [P, L])
        rden = sb("rden", [P, TT, 4])
        att = sb("att", [P, TT, NH, DH])
        attT = yT
        vpad = v_aug[:].rearrange("p t h e -> p (t h e)")[:, 0:L + 2 * PADV]
        ln2 = ck_x[:].rearrange("p (c d) -> p c d", c=TT)

        bank = ctx.enter_context(nc.psum_tensor("bank", [P, 8, L], F32))
        psO, psT, psR, psG = 4, 5, 6, 7

        s_x = [sem(f"x_loaded_{b}") for b in range(NB)]
        s_const = sem("consts_loaded")
        s_up = sem("up_loaded")
        s_moe = sem("moe_consts_loaded")
        s_down = sem("down_loaded")
        s_pairs = sem("pairs_loaded")
        s_raw = {k: sem(k + "_raw_loaded") for k in ("latent", "tin", "mixw")}
        s_late = sem("late_consts_loaded")
        s_out = sem("out_stored")
        x_new = sem("x_new")
        ln_stat, ln_agg, ln_eps, ln_rstd, ln_xn = (sem("ln_" + k) for k in ("stat", "agg", "eps", "rstd", "xn"))
        xn_ps, x_hi_ready, x_lo_ready = sem("xn_transposed"), sem("x_hi_ready"), sem("x_lo_ready")
        y_sb, y_ps = sem("y_in_sbuf"), sem("y_token_major")
        w_hi = {k: sem(k + "_hi_ready") for k in ("up", "pairs")}
        w_ready = {k: sem(k + "_split") for k in ("up", "router", "sel", "latent", "pairs", "tin", "mixw", "path")}
        setup_v, setup_p = sem("vector_setup"), sem("pool_setup")
        S = {}
        for ph in PHASES:
            kind = ph[:-1] if ph[-1].isdigit() else ph
            names = {
                "moe": ("gate_ps", "up_ps", "bc_ps", "silu", "sg", "h", "down", "lg_ps", "lg_sb", "lgt_ps",
                        "r_exp_in", "r_exp", "r_chain", "ghl", "ghl_ps", "gT"),
                "attn": ("lat_ps", "ck_x", "c_hi", "c_done", "ck_now", "v_ps", "v_sb", "qp_ps", "qx", "qhi", "qs",
                         "kp_ps", "khi", "ks", "scores", "exp", "clip", "av", "avT", "avt_ps", "rden", "att",
                         "att_ps", "attT"),
                "tree": ("logit_ps", "silu", "dec", "cnt", "mask", "outp"),
                "mix": ("v_ps", "v_sb", "v_wrap", "gate_ps", "gate", "prod_v", "sum_v", "prod_p", "sum_p",
                        "l_stat", "l_agg", "l_eps", "l_rstd", "l_n", "l_g"),
            }[kind]
            S[ph] = {n: sem(f"{ph}_{n}") for n in names}

        def phases():
            for p, name in enumerate(PHASES[:n_phases]):
                yield p, name

        def wait_apart(eng, s, value):
            eng.wait_ge(s, value)
            eng.nop(nofuse=True)

        def over_batches(eng, p, body):
            more = p < n_phases - 1
            body(0, False, True)
            with eng.Fori(1, NB - 1) as b:
                body(b, False, more)
            body(NB - 1, True, more)

        block = ctx.enter_context(nc.Block())

        @block.sync
        def _(sp):
            for b in range(NB):
                sp.dma_start(X[:, TT * b:TT * (b + 1), :], d["x"][b].rearrange("(c p) d -> p c d", p=P)).then_inc(s_x[b], 16)
                if b == 0:
                    sp.dma_start(ident[:], d["ident"]).then_inc(s_const, 16)
                    sp.dma_start(raw_r[:], d["router"]).then_inc(s_moe, 16)
                    sp.dma_start(before[:].rearrange("p a b -> p (a b)"), d["before"]).then_inc(s_moe, 16)
                    sp.dma_start(ebias[:], d["ebias"]).then_inc(s_moe, 16)
                    sp.dma_start(sel_raw, d["sel"]).then_inc(s_moe, 16)
            sp.dma_start(raw[:, 0:NX * 2 * P], d["up"]).then_inc(s_up, 16)
            sp.dma_start(down[:].rearrange("p a b -> p (a b)"), d["down"]).then_inc(s_down, 16)
            for t, name in ((low, "low"), (rope_k, "rope_k"), (rope_q, "rope_q"), (target, "target"), (tb, "tb"), (wo, "wo")):
                sp.dma_start(t[:], d[name]).then_inc(s_late, 16)
            for t, name in ((cap, "cap"), (gb, "gb"), (tout, "tout")):
                sp.dma_start(t[:].rearrange("p a b -> p (a b)"), d[name]).then_inc(s_late, 16)
            sp.dma_start(path_raw, d["path"]).then_inc(s_late, 16)
            sp.wait_ge(w_ready["up"], 1)
            sp.dma_start(raw[:, 0:2 * P], d["latent"]).then_inc(s_raw["latent"], 16)
            sp.dma_start(raw[:, 2 * P:19 * P], d["pairs"]).then_inc(s_pairs, 16)
            sp.wait_ge(w_ready["latent"], 1)
            if n_phases > 1:
                sp.wait_ge(w_ready["pairs"], 1)
                sp.dma_start(raw[:, 0:NCH * P], d["tin"]).then_inc(s_raw["tin"], 16)
            if n_phases > 2:
                sp.wait_ge(w_ready["tin"], 1)
                sp.dma_start(raw[:, 0:10 * P], d["mixw"]).then_inc(s_raw["mixw"], 16)
            base = NB * (n_phases - 1)
            for b in range(NB):
                sp.wait_ge(x_new, base + b + 1)
                sp.dma_start(out[b].rearrange("(c p) d -> p c d", p=P), X[:, TT * b:TT * (b + 1), :]).then_inc(s_out, 16)
            sp.wait_ge(s_out, 16 * NB)

        @block.gpsimd
        def _(pool):
            nc.gpsimd.memset(mhalf[:], -0.5).then_inc(setup_p, 1)
            nc.gpsimd.memset(ghl[:], 0.0).then_inc(setup_p, 1)
            nc.gpsimd.memset(v_aug[:], 0.0).then_inc(setup_p, 1)
            pool.wait_ge(setup_p, 3)
            nc.gpsimd.memset(v_aug[:, :, :, DH:DH + 1], 1.0).then_inc(setup_p, 1)

            def rstd_of(n):
                pool.wait_ge(ln_eps, n + 1)
                nc.gpsimd.tensor_tensor(rstd[:], veps[:], mhalf[:], ALU.pow).then_inc(ln_rstd, 1)

            def split(hi, lo, src, ready):
                nc.gpsimd.tensor_copy(hi, src).then_inc(ready[0], 1)
                pool.wait_ge(ready[0], ready[1])
                nc.gpsimd.tensor_tensor(lo, src, hi.bitcast(F32), ALU.subtract).then_inc(ready[2], 1)

            for b in range(NB - 1):
                rstd_of(b)
            pool_hi = setup_p
            count = [4]

            def split_weights(name, hi, lo, src):
                count[0] += 1
                split(hi, lo, src, (pool_hi, count[0], w_ready[name]))

            for p, ph in phases():
                s = S[ph]
                if ph == "moe0":
                    rstd_of(NB * (p + 1) - 1)
                    pool.wait_ge(s_raw["latent"], 16)
                    split_weights("latent", lat_hi[:], lat_lo[:], raw[:, 0:2 * P].rearrange("p (a b) -> p a b", a=2))
                    pool.wait_ge(s_pairs, 16)
                    nc.gpsimd.tensor_copy(pair_tmp, raw[:, 2 * P:19 * P]).then_inc(w_hi["pairs"], 1)
                    pool.wait_ge(s_late, 160)
                    nc.gpsimd.tensor_copy(path[:].rearrange("p a b -> p (a b)"), path_raw).then_inc(w_ready["path"], 1)
                    if p < n_phases - 1:
                        with pool.Fori(1, NB) as b:
                            rstd_of(NB * (p + 1) + b - 1)
                elif ph == "attn":
                    def body(b, last, renorm):
                        if renorm:
                            rstd_of(NB * (p + 1) + b - 1)
                        for pr in range(NPAIR):
                            if last and pr == NPAIR - 1:
                                break
                            i = NPAIR * b + pr + 1
                            wait_apart(pool, s["qx"], i + 1)
                            nc.gpsimd.tensor_copy(q_hi[:], q_x[:]).then_inc(s["qhi"], 1)
                    pool.wait_ge(s["qx"], 1)
                    nc.gpsimd.tensor_copy(q_hi[:], q_x[:]).then_inc(s["qhi"], 1)
                    over_batches(pool, p, body)
                elif ph == "mix":
                    def body(b, last, renorm):
                        if renorm:
                            rstd_of(NB * (p + 1) + b - 1)
                        pool.wait_ge(s["v_wrap"], b + 1)
                        for i, g in enumerate((2, 5, 8)):
                            pool.wait_ge(s["gate"], 9 * b + g + 1)
                            dst = acc_p[:, 0, :] if i == 0 else prod_p[:]
                            if i == 0:
                                pool.wait_ge(s["sum_v"], 6 * b)
                            sh = PADV + SHIFTS[g]
                            nc.gpsimd.tensor_tensor(dst, act_s[:, g % 3, :], vpad[:, sh:sh + L], ALU.mult).then_inc(s["prod_p"], 1)
                            pool.wait_ge(s["prod_p"], 3 * b + i + 1)
                            if i:
                                nc.gpsimd.tensor_tensor(acc_p[:, i % 2, :], acc_p[:, 1 - i % 2, :], prod_p[:], ALU.add).then_inc(s["sum_p"], 1)
                                pool.wait_ge(s["sum_p"], 2 * b + i)
                        pool.wait_ge(s["l_eps"], b + 1)
                        nc.gpsimd.tensor_tensor(rstd[:], veps[:], mhalf[:], ALU.pow).then_inc(s["l_rstd"], 1)
                    over_batches(pool, p, body)
                else:
                    rstd_of(NB * (p + 1) - 1)
                    if ph == "moe1":
                        pool.wait_ge(s_raw["tin"], 16)
                        split_weights("tin", tin_hi[:], tin_lo[:], raw[:, 0:NCH * P].rearrange("p (a b) -> p a b", a=NCH))
                        pool.wait_ge(s_raw["mixw"], 16)
                        split_weights("mixw", mix_hi[:], mix_lo[:], raw[:, 0:10 * P].rearrange("p (a b) -> p a b", a=10))
                    if p < n_phases - 1:
                        with pool.Fori(1, NB) as b:
                            rstd_of(NB * (p + 1) + b - 1)

        @block.scalar
        def _(act):
            def copy(dst, src, **kw):
                return nc.scalar.activation(dst, src, ACT.Copy, **kw)

            def x_high(n, b, bk=psT):
                act.wait_ge(xn_ps, n + 1)
                copy(xhi[:, bass.ds(b * L, L)], bank[:, bk, :]).then_inc(x_hi_ready, 1)

            def y_copy(n, done, count):
                act.wait_ge(done, count)
                act.wait_ge(y_ps, n - NB)
                copy(yT[:], bank[:, psO, :], scale=0.5).then_inc(y_sb, 1)

            for b in range(NB - 1):
                x_high(b, b)
            act.wait_ge(s_up, 16)
            copy(up_hi[:].rearrange("p a b -> p (a b)"), raw[:, 0:NX * 2 * P]).then_inc(w_hi["up"], 1)

            n_y = 0
            for p, ph in phases():
                s = S[ph]
                n0 = NB * (p + 1)
                if ph.startswith("moe"):
                    def router_logits(b):
                        act.wait_ge(s["lg_ps"], b + 1)
                        copy(lgT[:], bank[:, psR, :]).then_inc(s["lg_sb"], 1)

                    def router_exp(b):
                        act.wait_ge(s["r_exp_in"], b + 1)
                        nc.scalar.activation(rt[:, 2], rt[:, 1], ACT.Exp).then_inc(s["r_exp"], 1)

                    def weights_T(b):
                        act.wait_ge(s["ghl_ps"], b + 1)
                        copy(gT[:, bass.ds(b * L, L)], bank[:, psR, :]).then_inc(s["gT"], 1)

                    def body(b, last, renorm):
                        for i in range(NX):
                            act.wait_ge(s["gate_ps"], NX * b + i + 1)
                            act.wait_ge(s["h"], NX * b + max(i - 1, 0))
                            nc.scalar.activation(act_s[:, i % 2, :], bank[:, i % 2, :], ACT.Silu).then_inc(s["silu"], 1)
                            if i == 3 and renorm:
                                x_high(n0 + b - 1, (b + NB - 1) % NB)
                            if i == 4 and not last:
                                router_logits(b + 1)
                            if i == 7 and not last:
                                router_exp(b + 1)
                        if not last:
                            weights_T(b + 1)
                        y_copy(n0 + b, s["down"], NX * (b + 1))
                    router_logits(0)
                    router_exp(0)
                    weights_T(0)
                    over_batches(act, p, body)
                    n_y += NB
                elif ph == "attn":
                    def latent_high(b):
                        act.wait_ge(s["lat_ps"], 2 * b + 1)
                        copy(c_hi[:], bank[:, psG, :]).then_inc(s["c_hi"], 1)
                        act.wait_ge(s["ck_x"], b + 1)
                        act.wait_ge(s["c_done"], 2 * b + 1)
                        copy(c_hi[:], ck_x[:]).then_inc(s["c_hi"], 1)

                    def keys_high(i):
                        act.wait_ge(s["kp_ps"], i + 1)
                        act.wait_ge(s["ks"], i)
                        copy(k_hi[:], bank[:, psG, :]).then_inc(s["khi"], 1)

                    def av_copy(i):
                        act.wait_ge(s["av"], 2 * (i + 1))
                        act.wait_ge(s["avt_ps"], i)
                        copy(avT[:], bank[:, 6, :]).then_inc(s["avT"], 1)

                    def body(b, last, renorm):
                        if True:
                            act.wait_ge(s["v_ps"], b + 1)
                            act.wait_ge(s["av"], NPAIR * b)
                            copy(v_aug[:, :, :, 0:DH], bank[:, psG, :].rearrange("p (t h e) -> p t h e", t=TT, h=NH)).then_inc(s["v_sb"], 1)
                        for pr in range(NPAIR):
                            if not (last and pr == NPAIR - 1):
                                keys_high(NPAIR * b + pr + 1)
                            for g, w in enumerate((L, L, L // 2)):
                                i = 3 * (NPAIR * b + pr) + g
                                act.wait_ge(s["scores"], i + 1)
                                act.wait_ge(s["av"], NPAIR * b + max(pr - 1, 0))
                                nc.scalar.activation(pb[:, pr % 2, g, :, 0:w], bank[:, 2 * g:2 * g + 2, 0:w], ACT.Exp,
                                                     scale=QK_SCALE).then_inc(s["exp"], 1)
                            if pr == 1 and renorm:
                                x_high(n0 + b - 1, (b + NB - 1) % NB, psG)
                            if pr == 3 and not last:
                                latent_high(b + 1)
                            if pr % 2 == 0 and pr:
                                av_copy(4 * b + pr // 2 - 1)
                        av_copy(4 * b + 3)
                        act.wait_ge(s["att_ps"], b + 1)
                        copy(attT[:], bank[:, psG, :]).then_inc(s["attT"], 1)
                    act.wait_ge(w_ready["path"], 1)
                    latent_high(0)
                    keys_high(0)
                    over_batches(act, p, body)
                elif ph.startswith("tree"):
                    def body(b, last, renorm):
                        for i in range(NCH):
                            act.wait_ge(s["logit_ps"], NCH * b + i + 1)
                            act.wait_ge(s["mask"], NCH * b + max(i - 3, 0))
                            nc.scalar.activation(act_s[:, i % 4, :], bank[:, i % 4, :], ACT.Silu,
                                                 bias=tb[:, i:i + 1]).then_inc(s["silu"], 1)
                            if i == 5 and renorm:
                                x_high(n0 + b - 1, (b + NB - 1) % NB)
                        y_copy(n0 + b, s["outp"], NCH * (b + 1))
                    act.wait_ge(s_late, 160)
                    over_batches(act, p, body)
                elif ph == "mix":
                    def body(b, last, renorm):
                        act.wait_ge(s["v_ps"], b + 1)
                        act.wait_ge(s["sum_v"], 6 * b)
                        act.wait_ge(s["prod_p"], 3 * b)
                        copy(vpad[:, PADV:PADV + L], bank[:, psO, :]).then_inc(s["v_sb"], 1)
                        act.wait_ge(s["v_sb"], b + 1)
                        copy(vpad[:, 0:PADV], vpad[:, L:L + PADV])
                        copy(vpad[:, L + PADV:], vpad[:, PADV:2 * PADV]).then_inc(s["v_wrap"], 1)
                        for g in range(9):
                            act.wait_ge(s["gate_ps"], 9 * b + g + 1)
                            if g >= 3:
                                if g % 3 == 2:
                                    act.wait_ge(s["prod_p"], 3 * b + (g - 3) // 3 + 1)
                                else:
                                    act.wait_ge(s["prod_v"], 6 * b + 2 * ((g - 3) // 3) + (g - 3) % 3 + 1)
                            else:
                                act.wait_ge(s["prod_p"], 3 * b)
                                act.wait_ge(s["prod_v"], 6 * b)
                            nc.scalar.activation(act_s[:, g % 3, :], bank[:, g % 3, :], ACT.Sigmoid).then_inc(s["gate"], 1)
                            if g == 3 and renorm:
                                x_high(n0 + b - 1, (b + NB - 1) % NB)
                        act.wait_ge(s["sum_v"], 6 * b + 6)
                        act.wait_ge(y_ps, n0 - NB + b)
                        copy(yT[:], acc_v[:, 1, :]).then_inc(y_sb, 1)
                    over_batches(act, p, body)

        @block.vector
        def _(dve):
            V = nc.vector

            def normalise(n, b):
                for c in range(TT):
                    i = V.bn_stats(stats[:, c, :], X[:, bass.ds(b * TT + c, 1), :])
                i.then_inc(ln_stat, 1)
                wait_apart(dve, ln_stat, n + 1)
                for c in range(TT):
                    i = V.bn_aggr(mv[:, c, :], stats[:, c, :])
                i.then_inc(ln_agg, 1)
                dve.wait_ge(ln_agg, n + 1)
                V.tensor_scalar(veps[:], mv[:, :, 1], EPS, None, ALU.add).then_inc(ln_eps, 1)

            def normalised(n, b):
                dve.wait_ge(ln_rstd, n + 1)
                dve.wait_ge(xn_ps, n)
                for c in range(TT):
                    i = V.tensor_scalar(xn[:, c, :].rearrange("p (o d) -> p o d", o=1), X[:, bass.ds(b * TT + c, 1), :], mv[:, c, 0:1], rstd[:, c:c + 1],
                                        ALU.subtract, ALU.mult)
                i.then_inc(ln_xn, 1)

            def x_low(n, b, bk=psT):
                dve.wait_ge(x_hi_ready, n + 1)
                V.tensor_tensor(xlo[:, bass.ds(b * L, L)], bank[:, bk, :], xhi[:, bass.ds(b * L, L)].bitcast(F32),
                                ALU.subtract).then_inc(x_lo_ready, 1)

            def add_y(n, b, src, done, count):
                dve.wait_ge(done, count)
                dst = X[:, bass.ds(b * TT, TT), :]
                V.tensor_tensor(dst, dst, src, ALU.add).then_inc(x_new, 1)
                wait_apart(dve, x_new, n - NB + 1)

            def tok(bk):
                return bank[:, bk, :].rearrange("p (c d) -> p c d", c=TT)

            for b in range(NB - 1):
                dve.wait_ge(s_x[b], 16)
                normalise(b, b)
                normalised(b, b)
                if b == 0:
                    dve.wait_ge(s_moe, 64)
                    V.tensor_copy(router_hi[:], raw_r[:]).then_inc(setup_v, 1)
                    dve.wait_ge(setup_v, 1)
                    V.tensor_tensor(router_lo[:], raw_r[:], router_hi[:].bitcast(F32), ALU.subtract).then_inc(w_ready["router"], 1)
                    V.tensor_copy(sel[:].rearrange("p a b -> p (a b)"), sel_raw).then_inc(w_ready["sel"], 1)
                x_low(b, b)
            dve.wait_ge(w_hi["up"], 1)
            V.tensor_tensor(up_lo[:].rearrange("p a b -> p (a b)"), raw[:, 0:NX * 2 * P], up_hi[:].bitcast(F32).rearrange("p a b -> p (a b)"),
                            ALU.subtract).then_inc(w_ready["up"], 1)
            dve.wait_ge(s_x[NB - 1], 16)
            normalise(NB - 1, NB - 1)
            dve.wait_ge(setup_p, 4)

            yc = 0
            for p, ph in phases():
                s = S[ph]
                n0 = NB * (p + 1)

                if ph.startswith("moe"):
                    KR = 12

                    def router_1(b):
                        c = KR * b
                        dve.wait_ge(s["lgt_ps"], b + 1)
                        V.tensor_copy(rt[:, 0], tok(psR)[:, :, 0:NE]).then_inc(s["r_chain"], 1)
                        dve.wait_ge(s["r_chain"], c + 1)
                        V.tensor_reduce(rsum[:, 0, :], rt[:, 0], AX.X, ALU.max).then_inc(s["r_chain"], 1)
                        dve.wait_ge(s["r_chain"], c + 2)
                        V.tensor_tensor(rt[:, 1], rt[:, 0], rsum[:, 0, :].unsqueeze(2).to_broadcast([P, TT, NE]), ALU.subtract).then_inc(s["r_exp_in"], 1)

                    def router_2(b):
                        c = KR * b + 2
                        dve.wait_ge(s["r_exp"], b + 1)
                        k = [0]

                        def step(ins):
                            ins.then_inc(s["r_chain"], 1)
                            k[0] += 1
                            dve.wait_ge(s["r_chain"], c + k[0])
                        step(V.tensor_reduce(rsum[:, 1, :], rt[:, 2], AX.X, ALU.add))
                        step(V.reciprocal(rsum[:, 2, :], rsum[:, 1, :]))
                        step(V.tensor_tensor(rt[:, 3], rt[:, 2], rsum[:, 2, :].unsqueeze(2).to_broadcast([P, TT, NE]), ALU.mult))
                        step(V.tensor_tensor(rt[:, 4], rt[:, 3], ebias[:].unsqueeze(1).to_broadcast([P, TT, NE]), ALU.add))
                        mine = rt[:, 4].unsqueeze(3).to_broadcast([P, TT, NE, NE])
                        theirs = rt[:, 4].unsqueeze(2).to_broadcast([P, TT, NE, NE])
                        V.tensor_tensor(rcmp[:, 0], theirs, mine, ALU.is_gt)
                        step(V.tensor_tensor(rcmp[:, 1], theirs, mine, ALU.is_equal))
                        step(V.tensor_tensor(rcmp[:, 1], rcmp[:, 1], before[:].unsqueeze(1).to_broadcast([P, TT, NE, NE]), ALU.mult))
                        step(V.tensor_tensor(rcmp[:, 0], rcmp[:, 0], rcmp[:, 1], ALU.add))
                        step(V.tensor_reduce(rt[:, 5], rcmp[:, 0], AX.X, ALU.add))
                        step(V.scalar_tensor_tensor(rt[:, 6], rt[:, 5], 2.0, rt[:, 3], ALU.is_lt, ALU.mult))
                        step(V.tensor_copy(g_hi[:], rt[:, 6]))
                        assert k[0] + 2 == KR
                        dve.wait_ge(s["ghl_ps"], b)
                        V.tensor_copy(ghl[:, :, 0:NE], g_hi[:].bitcast(F32))
                        V.tensor_tensor(ghl[:, :, NE:2 * NE], rt[:, 6], g_hi[:].bitcast(F32), ALU.subtract).then_inc(s["ghl"], 1)

                    def body(b, last, renorm):
                        for i in range(NX):
                            if i == 2 and renorm:
                                normalised(n0 + b - 1, (b + NB - 1) % NB)
                            if i == 4 and renorm:
                                x_low(n0 + b - 1, (b + NB - 1) % NB)
                            if i == 7 and not last:
                                router_1(b + 1)
                            if i == 8 and not last:
                                router_2(b + 1)
                            j = NX * b + i
                            dve.wait_ge(s["silu"], j + 1)
                            dve.wait_ge(s["down"], NX * b + max(i - 1, 0))
                            a = act_s[:, i % 2, :]
                            if i:
                                dve.wait_ge(s["bc_ps"], NE * b + i)
                                V.tensor_tensor(a, a, bank[:, psG, :], ALU.mult).then_inc(s["sg"], 1)
                                dve.wait_ge(s["sg"], NE * b + i)
                            dve.wait_ge(s["up_ps"], j + 1)
                            V.tensor_tensor(h_s[:, i % 2, :], a, bank[:, 2 + i % 2, :], ALU.mult).then_inc(s["h"], 1)
                        add_y(n0 + b, b, tok(psT), y_ps, yc + b + 1)
                        if p < n_phases - 1:
                            normalise(n0 + b, b)

                    router_1(0)
                    router_2(0)
                    over_batches(dve, p, body)
                    yc += NB
                elif ph == "attn":
                    def latent(b):
                        dst = bass.ds(b * L, L)
                        dve.wait_ge(s["c_hi"], 2 * b + 1)
                        V.scalar_tensor_tensor(CQ[:, dst], c_hi[:].bitcast(F32), low[:, 0:1], bank[:, psG, :], ALU.mult, ALU.add).then_inc(s["c_done"], 1)
                        dve.wait_ge(s["lat_ps"], 2 * b + 2)
                        V.tensor_tensor(ck_x[:], bank[:, psG, :], rope_k[:], ALU.mult).then_inc(s["ck_x"], 1)
                        dve.wait_ge(s["c_hi"], 2 * b + 2)
                        V.scalar_tensor_tensor(CK[:, dst], c_hi[:].bitcast(F32), low[:, 1:2], ck_x[:], ALU.mult, ALU.add).then_inc(s["c_done"], 1)

                    def latent_now(b):
                        dve.wait_ge(s["c_done"], 2 * b + 2)
                        dve.wait_ge(s["v_ps"], b)
                        V.tensor_copy(ck_now[:], CK[:, bass.ds(b * L, L)].bitcast(F32)).then_inc(s["ck_now"], 1)

                    def queries_x(i):
                        dve.wait_ge(s["qp_ps"], i + 1)
                        dve.wait_ge(s["qs"], i)
                        V.tensor_tensor(q_x[:], bank[:, psG, :], rope_q[:], ALU.mult).then_inc(s["qx"], 1)

                    def prev(i):
                        return max(3 * (i - 1), 0) if isinstance(i, int) else 3 * (i - 1)

                    def queries(i, par):
                        dve.wait_ge(s["qhi"], i + 1)
                        dve.wait_ge(s["scores"], prev(i))
                        V.scalar_tensor_tensor(QS[:, par, :], q_hi[:].bitcast(F32), low[:, 3:4], q_x[:], ALU.mult, ALU.add).then_inc(s["qs"], 1)

                    def keys(i, par):
                        dve.wait_ge(s["khi"], i + 1)
                        dve.wait_ge(s["scores"], prev(i))
                        V.scalar_tensor_tensor(KS[:, par, :], k_hi[:].bitcast(F32), low[:, 4:5], bank[:, psG, :], ALU.mult, ALU.add).then_inc(s["ks"], 1)

                    def clip(b, pr, g):
                        i = 3 * (NPAIR * b + pr) + g
                        dve.wait_ge(s["exp"], i + 1)
                        t = pb[:, pr % 2, g]
                        diag = (0,) if g != 1 else (0, 384)
                        for c in diag:
                            V.scalar_tensor_tensor(t[:, :, c:c + P], t[:, :, c:c + P], P_LOW, cap[:], ALU.max, ALU.min)
                        rest = t[:, :, P:(L, 384, 256)[g]]
                        V.tensor_scalar(rest, rest, P_LOW, P_HIGH, ALU.max, ALU.min).then_inc(s["clip"], 1)

                    def heads(i, g):
                        dve.wait_ge(s["avt_ps"], i + 1)
                        o = bank[:, psG, :].rearrange("p (t h e) -> p t h e", t=TT, h=4)
                        V.reciprocal(rden[:], o[:, :, :, DH]).then_inc(s["rden"], 1)
                        dve.wait_ge(s["rden"], i + 1)
                        V.tensor_tensor(att[:, :, 4 * g:4 * g + 4, :], o[:, :, :, 0:DH],
                                        rden[:].unsqueeze(3).to_broadcast([P, TT, 4, DH]), ALU.mult).then_inc(s["att"], 1)

                    def body(b, last, renorm):
                        latent_now(b)
                        for pr in range(NPAIR):
                            nxt = not (last and pr == NPAIR - 1)
                            i = NPAIR * b + pr + 1
                            if nxt:
                                queries_x(i)
                                keys(i, (pr + 1) % 2)
                            clip(b, pr, 0)
                            if nxt:
                                queries(i, (pr + 1) % 2)
                            clip(b, pr, 1)
                            clip(b, pr, 2)
                            if pr == 0 and renorm:
                                normalised(n0 + b - 1, (b + NB - 1) % NB)
                            if pr == 1 and renorm:
                                x_low(n0 + b - 1, (b + NB - 1) % NB, psG)
                            if pr == 3 and not last:
                                latent(b + 1)
                            if pr % 2 == 0 and pr:
                                heads(4 * b + pr // 2 - 1, pr // 2 - 1)
                        heads(4 * b + 3, 3)
                        add_y(n0 + b, b, tok(psG), y_ps, yc + b + 1)
                        if p < n_phases - 1:
                            normalise(n0 + b, b)

                    dve.wait_ge(s_late, 160)
                    dve.wait_ge(w_hi["pairs"], 1)
                    V.scalar_tensor_tensor(pair_w[:].rearrange("p a b -> p (a b)"), pair_tmp.bitcast(F32), low[:, 2:3],
                                           raw[:, 2 * P:19 * P], ALU.mult, ALU.add).then_inc(w_ready["pairs"], 1)
                    dve.wait_ge(w_ready["pairs"], 1)
                    latent(0)
                    queries_x(0)
                    keys(0, 0)
                    queries(0, 0)
                    over_batches(dve, p, body)
                    yc += NB
                elif ph.startswith("tree"):
                    def body(b, last, renorm):
                        for t in range(TREES):
                            if t == 1 and renorm:
                                normalised(n0 + b - 1, (b + NB - 1) % NB)
                            if t == 3 and renorm:
                                x_low(n0 + b - 1, (b + NB - 1) % NB)
                            i = 2 * t
                            dve.wait_ge(s["silu"], NCH * b + i + 1)
                            dve.wait_ge(s["cnt"], NCH * b + max(i - 2, 0))
                            V.tensor_scalar(dec[:, t % 2, :], bank[:, i % 4, :], tb[:, i:i + 1], 0.0, ALU.add, ALU.is_gt).then_inc(s["dec"], 1)
                            for c in range(2):
                                j = NCH * b + i + c
                                dve.wait_ge(s["silu"], j + 1)
                                dve.wait_ge(s["cnt"], j + 1)
                                dve.wait_ge(s["outp"], NCH * b + max(i + c - 3, 0))
                                V.scalar_tensor_tensor(h_s[:, (i + c) % 4, :], bank[:, 6 + c, :], target[:, c:c + 1],
                                                       act_s[:, (i + c) % 4, :], ALU.is_equal, ALU.mult).then_inc(s["mask"], 1)
                        add_y(n0 + b, b, tok(psT), y_ps, yc + b + 1)
                        if p < n_phases - 1:
                            normalise(n0 + b, b)
                    over_batches(dve, p, body)
                    yc += NB
                elif ph == "mix":
                    def body(b, last, renorm):
                        if renorm:
                            normalised(n0 + b - 1, (b + NB - 1) % NB)
                        dve.wait_ge(s["v_wrap"], b + 1)
                        for i, g in enumerate((0, 1, 3, 4, 6, 7)):
                            j = 6 * b + i
                            dve.wait_ge(s["gate"], 9 * b + g + 1)
                            sh = PADV + SHIFTS[g]
                            dst = acc_v[:, 0, :] if i == 0 else prod_v[:, i % 2, :]
                            if i == 0:
                                dve.wait_ge(y_sb, NB * p - NB + b)
                            V.tensor_tensor(dst, act_s[:, g % 3, :], vpad[:, sh:sh + L], ALU.mult).then_inc(s["prod_v"], 1)
                            dve.wait_ge(s["prod_v"], j + 1)
                            if i:
                                V.tensor_tensor(acc_v[:, i % 2, :], acc_v[:, 1 - i % 2, :], prod_v[:, i % 2, :], ALU.add).then_inc(s["sum_v"], 1)
                                dve.wait_ge(s["sum_v"], 6 * b + i)
                            if i == 3 and renorm:
                                x_low(n0 + b - 1, (b + NB - 1) % NB)
                        dve.wait_ge(s["sum_p"], 2 * b + 2)
                        V.tensor_tensor(acc_v[:, 1, :], acc_v[:, 1, :], acc_p[:, 0, :], ALU.add).then_inc(s["sum_v"], 1)
                        dve.wait_ge(y_ps, yc + b + 1)
                        for c in range(TT):
                            i = V.bn_stats(stats[:, c, :], bank[:, psT, c * P:(c + 1) * P])
                        i.then_inc(s["l_stat"], 1)
                        wait_apart(dve, s["l_stat"], b + 1)
                        for c in range(TT):
                            i = V.bn_aggr(mv[:, c, :], stats[:, c, :])
                        i.then_inc(s["l_agg"], 1)
                        dve.wait_ge(s["l_agg"], b + 1)
                        V.tensor_scalar(veps[:], mv[:, :, 1], EPS, None, ALU.add).then_inc(s["l_eps"], 1)
                        dve.wait_ge(s["l_rstd"], b + 1)
                        for c in range(TT):
                            i = V.tensor_scalar(ln2[:, c, :], bank[:, psT, c * P:(c + 1) * P], mv[:, c, 0:1], rstd[:, c:c + 1],
                                                ALU.subtract, ALU.mult)
                        i.then_inc(s["l_n"], 1)
                        dve.wait_ge(s["l_n"], b + 1)
                        V.tensor_tensor(ln2[:], ln2[:], gb[:, 0, :].unsqueeze(1).to_broadcast([P, TT, P]), ALU.mult).then_inc(s["l_g"], 1)
                        dve.wait_ge(s["l_g"], 2 * b + 1)
                        V.tensor_tensor(ln2[:], ln2[:], gb[:, 1, :].unsqueeze(1).to_broadcast([P, TT, P]), ALU.add).then_inc(s["l_g"], 1)
                        add_y(n0 + b, b, ln2[:], s["l_g"], 2 * b + 2)
                        if p < n_phases - 1:
                            normalise(n0 + b, b)
                    over_batches(dve, p, body)
                    yc += NB

        @block.tensor
        def _(pe):
            mm = nc.tensor.matmul

            def xpose(dst, src):
                return nc.tensor.transpose(dst, src, ident[:])

            def three(dst, whi, wlo, b):
                hi, lo = xhi[:, bass.ds(b * L, L)], xlo[:, bass.ds(b * L, L)]
                mm(dst, whi, hi, start=True, stop=False)
                mm(dst, whi, lo, start=False, stop=False)
                return mm(dst, wlo, hi, start=False, stop=True)

            def xn_T(n, bk=psT):
                pe.wait_ge(ln_xn, n + 1)
                pe.wait_ge(x_lo_ready, n)
                for c in range(TT):
                    i = xpose(bank[:, bk, c * P:(c + 1) * P], xn[:, c, :])
                i.then_inc(xn_ps, 1)

            def y_T(m, n, renorm):
                pe.wait_ge(y_sb, m)
                pe.wait_ge(x_new, n - NB)
                if renorm:
                    pe.wait_ge(x_lo_ready, n)
                for c in range(TT):
                    i = xpose(bank[:, psT, c * P:(c + 1) * P], yT[:, c * P:(c + 1) * P])
                i.then_inc(y_ps, 1)

            pe.wait_ge(s_const, 16)
            for b in range(NB - 1):
                xn_T(b)
            pe.wait_ge(x_lo_ready, NB - 1)
            ysb = 0
            for p, ph in phases():
                s = S[ph]
                n0 = NB * (p + 1)
                if ph.startswith("moe"):
                    def router_mm(b):
                        pe.wait_ge(x_hi_ready, NB * p + b + 1)
                        pe.wait_ge(x_lo_ready, NB * p + b + 1)
                        pe.wait_ge(s["gT"], b)
                        three(bank[:, psR, :], router_hi[:], router_lo[:], b).then_inc(s["lg_ps"], 1)

                    def router_T(b):
                        pe.wait_ge(s["lg_sb"], b + 1)
                        for c in range(TT):
                            i = xpose(bank[:, psR, c * P:(c + 1) * P], lgT[:, c * P:(c + 1) * P])
                        i.then_inc(s["lgt_ps"], 1)

                    def weights_T(b):
                        pe.wait_ge(s["ghl"], b + 1)
                        for c in range(TT):
                            i = xpose(bank[:, psR, c * P:(c + 1) * P], ghl[:, c, :])
                        i.then_inc(s["ghl_ps"], 1)

                    def down_mm(b, i):
                        pe.wait_ge(s["h"], NX * b + i + 1)
                        if i == 0:
                            pe.wait_ge(y_sb, ysb + b)
                        mm(bank[:, psO, :], down[:, i, :], h_s[:, i % 2, :], start=(i == 0), stop=(i == NX - 1)).then_inc(s["down"], 1)

                    def body(b, last, renorm):
                        for i in range(NX):
                            pe.wait_ge(s["silu"], NX * b + max(i - 1, 0))
                            three(bank[:, i % 2, :], up_hi[:, 2 * i, :], up_lo[:, 2 * i, :], b).then_inc(s["gate_ps"], 1)
                            pe.wait_ge(s["h"], NX * b + max(i - 1, 0))
                            three(bank[:, 2 + i % 2, :], up_hi[:, 2 * i + 1, :], up_lo[:, 2 * i + 1, :], b).then_inc(s["up_ps"], 1)
                            if i:
                                pe.wait_ge(s["gT"], b + 1)
                                pe.wait_ge(s["sg"], NE * b + i - 1)
                                mm(bank[:, psG, :], sel[:, i - 1, :], gT[:, bass.ds(b * L, L)], start=True, stop=True).then_inc(s["bc_ps"], 1)
                                down_mm(b, i - 1)
                            if i == 3 and renorm:
                                xn_T(n0 + b - 1)
                            if i == 4 and not last:
                                router_mm(b + 1)
                            if i == 5 and not last:
                                router_T(b + 1)
                        down_mm(b, NX - 1)
                        if not last:
                            weights_T(b + 1)
                        y_T(ysb + b + 1, n0 + b, renorm)

                    pe.wait_ge(w_ready["router"], 1)
                    router_mm(0)
                    router_T(0)
                    weights_T(0)
                    pe.wait_ge(w_ready["up"], 1)
                    pe.wait_ge(w_ready["sel"], 1)
                    pe.wait_ge(s_down, 16)
                    over_batches(pe, p, body)
                    ysb += NB
                elif ph == "attn":
                    def latent(b):
                        pe.wait_ge(x_lo_ready, NB * p + b + 1)
                        three(bank[:, psG, :], lat_hi[:, 0, :], lat_lo[:, 0, :], b).then_inc(s["lat_ps"], 1)
                        pe.wait_ge(s["c_done"], 2 * b + 1)
                        three(bank[:, psG, :], lat_hi[:, 1, :], lat_lo[:, 1, :], b).then_inc(s["lat_ps"], 1)

                    def project(b, pr, i):
                        mm(bank[:, psG, :], pair_w[:, pr, :], CQ[:, bass.ds(b * L, L)], start=True, stop=True).then_inc(s["qp_ps"], 1)
                        pe.wait_ge(s["qx"], i + 1)
                        mm(bank[:, psG, :], pair_w[:, NPAIR + pr, :], CK[:, bass.ds(b * L, L)], start=True, stop=True).then_inc(s["kp_ps"], 1)

                    def scores(b, pr):
                        i = NPAIR * b + pr
                        pe.wait_ge(s["qs"], i + 1)
                        pe.wait_ge(s["ks"], i + 1)
                        for g, tiles in enumerate((((0, 0),), ((1, 0), (3, 384)), ((2, 0),))):
                            pe.wait_ge(s["exp"], 3 * NPAIR * b + max(3 * (pr - 1) + g + 1, 0))
                            for kt, col in tiles:
                                for j in range(2):
                                    r = slice(64 * j, 64 * j + 64)
                                    ins = mm(bank[:, 2 * g + j, col:col + L - P * kt], KS[r, pr % 2, kt * P:(kt + 1) * P],
                                             QS[r, pr % 2, kt * P:L], start=True, stop=True)
                            ins.then_inc(s["scores"], 1)

                    def values(b, pr):
                        i = NPAIR * b + pr
                        if pr % 2 == 0:
                            pe.wait_ge(s["avT"], 4 * b + pr // 2)
                        for g, tiles in enumerate((((0, 0),), ((1, 0), (3, 384)), ((2, 0),))):
                            pe.wait_ge(s["clip"], 3 * i + g + 1)
                            for kt, col in tiles:
                                for j in range(2):
                                    q = 32 * (2 * (pr % 2) + j)
                                    ins = mm(bank[q:q + 32, 6, kt * P:L], v_aug[:, kt, 2 * pr + j, :],
                                             pb[:, pr % 2, g, j, col:col + L - P * kt], start=(kt == 0), stop=(kt == 2))
                        ins.then_inc(s["av"], 1)

                    def heads_T(b, g):
                        pe.wait_ge(s["avT"], 4 * b + g + 1)
                        for c in range(TT):
                            ins = xpose(bank[:, psG, c * P:(c + 1) * P], avT[:, c * P:(c + 1) * P])
                        ins.then_inc(s["avt_ps"], 1)

                    def body(b, last, renorm):
                        pe.wait_ge(s["ck_now"], b + 1)
                        for c in range(TT):
                            ins = mm(bank[:, psG, c * P:(c + 1) * P], ck_now[:, c * P:(c + 1) * P], pair_w[:, 2 * NPAIR, :], start=True, stop=True)
                        ins.then_inc(s["v_ps"], 1)
                        pe.wait_ge(s["v_sb"], b + 1)
                        for pr in range(NPAIR):
                            if pr < NPAIR - 1:
                                project(b, pr + 1, NPAIR * b + pr + 1)
                            elif not last:
                                project(b + 1, 0, NPAIR * b + pr + 1)
                            scores(b, pr)
                            if pr:
                                values(b, pr - 1)
                            if not (last and pr == NPAIR - 1):
                                pe.wait_ge(s["ks"], NPAIR * b + pr + 2)
                            if pr == 1 and renorm:
                                xn_T(n0 + b - 1, psG)
                                pe.wait_ge(x_lo_ready, n0 + b)
                            if pr == 3 and not last:
                                latent(b + 1)
                                pe.wait_ge(s["ck_x"], b + 2)
                            if pr % 2 == 0 and pr:
                                heads_T(b, pr // 2 - 1)
                                pe.wait_ge(s["att"], 4 * b + pr // 2)
                        values(b, NPAIR - 1)
                        heads_T(b, 3)
                        pe.wait_ge(s["att"], 4 * b + 4)
                        for c in range(TT):
                            ins = xpose(bank[:, psG, c * P:(c + 1) * P], att[:, c].rearrange("p h e -> p (h e)"))
                        ins.then_inc(s["att_ps"], 1)
                        pe.wait_ge(s["attT"], b + 1)
                        for c in range(TT):
                            ins = mm(bank[:, psG, c * P:(c + 1) * P], attT[:, c * P:(c + 1) * P], wo[:], start=True, stop=True)
                        ins.then_inc(y_ps, 1)
                        pe.wait_ge(x_new, NB * p + b + 1)

                    pe.wait_ge(w_ready["latent"], 1)
                    pe.wait_ge(w_ready["pairs"], 1)
                    pe.wait_ge(setup_p, 4)
                    latent(0)
                    pe.wait_ge(s["c_done"], 2)
                    project(0, 0, 0)
                    pe.wait_ge(s["ks"], 1)
                    over_batches(pe, p, body)
                elif ph.startswith("tree"):
                    def logits(b, i):
                        pe.wait_ge(s["silu"], NCH * b + max(i - 3, 0))
                        if i % 2 == 0:
                            pe.wait_ge(s["dec"], TREES * b + max(i // 2 - 1, 0))
                        three(bank[:, i % 4, :], tin_hi[:, i, :], tin_lo[:, i, :], b).then_inc(s["logit_ps"], 1)

                    def count(b, t):
                        pe.wait_ge(s["dec"], TREES * b + t + 1)
                        for c in range(2):
                            pe.wait_ge(s["mask"], NCH * b + max(2 * t + c - 1, 0))
                            mm(bank[:, 6 + c, :], path[:, c, :], dec[:, t % 2, :], start=True, stop=True).then_inc(s["cnt"], 1)

                    def out_mm(b, i):
                        pe.wait_ge(s["mask"], NCH * b + i + 1)
                        if i == 0:
                            pe.wait_ge(y_sb, ysb + b)
                        mm(bank[:, psO, :], tout[:, i, :], h_s[:, i % 4, :], start=(i == 0), stop=(i == NCH - 1)).then_inc(s["outp"], 1)

                    def body(b, last, renorm):
                        pe.wait_ge(x_lo_ready, NB * p + b + 1)
                        logits(b, 0)
                        logits(b, 1)
                        for t in range(TREES):
                            if t < TREES - 1:
                                logits(b, 2 * t + 2)
                            count(b, t)
                            if t < TREES - 1:
                                logits(b, 2 * t + 3)
                            if t == 2 and renorm:
                                xn_T(n0 + b - 1)
                            out_mm(b, 2 * t)
                            out_mm(b, 2 * t + 1)
                        y_T(ysb + b + 1, n0 + b, renorm)

                    pe.wait_ge(w_ready["tin"], 1)
                    pe.wait_ge(w_ready["path"], 1)
                    pe.wait_ge(s_late, 160)
                    over_batches(pe, p, body)
                    ysb += NB
                elif ph == "mix":
                    def body(b, last, renorm):
                        pe.wait_ge(x_lo_ready, NB * p + b + 1)
                        three(bank[:, psO, :], mix_hi[:, 0, :], mix_lo[:, 0, :], b).then_inc(s["v_ps"], 1)
                        for g in range(9):
                            pe.wait_ge(s["gate"], 9 * b + max(g - 2, 0))
                            three(bank[:, g % 3, :], mix_hi[:, g + 1, :], mix_lo[:, g + 1, :], b).then_inc(s["gate_ps"], 1)
                            if g == 2 and renorm:
                                xn_T(n0 + b - 1)
                        y_T(ysb + b + 1, n0 + b, renorm)
                    pe.wait_ge(w_ready["mixw"], 1)
                    over_batches(pe, p, body)
                    ysb += NB


def kernel(**inputs):
    import concourse.bacc as _bacc
    from concourse import mybir as _mybir
    from concourse.bass_utils import run_bass_kernel_spmd as _run

    nc = _bacc.Bacc("TRN2", target_bir_lowering=False, num_devices=1)
    arrays = lay_out(inputs)
    d = {name: nc.dram_tensor("in_" + name, a.shape, _mybir.dt.float32, kind="ExternalInput").ap() for name, a in arrays.items()}
    out = nc.dram_tensor("out", arrays["x"].shape, _mybir.dt.float32, kind="ExternalOutput").ap()
    macaron(nc, d, out, N_PHASES)
    r = _run(nc, [{"in_" + k: v for k, v in arrays.items()}], core_ids=[0])
    return r.results[0]["out"]
```

```python
from contextlib import ExitStack

import numpy as np

import concourse.bass as bass
from concourse import mybir

F32 = mybir.dt.float32
F32R = mybir.dt.float32r
BF16 = mybir.dt.bfloat16
ALU = mybir.AluOpType
ACT = mybir.ActivationFunctionType
AX = mybir.AxisListType

P = 128
NB = 4
L = 512
TT = L // P
NE = 8
NX = NE + 1
NH = 16
NPAIR = NH // 2
DL = 32
DH, DR = 8, 4
TREES = 8
DEPTH = 7
NCH = 2 * TREES
SHIFTS = (0, -32, -16, -4, -1, 1, 4, 16, 32)
PADV = 32
EPS = 1e-5
QK_SCALE = float(1.0 / np.sqrt(np.float32(DH + DR)))
P_LOW = float(np.exp(-80.0 * QK_SCALE))
P_HIGH = float(np.exp(80.0 * QK_SCALE))
N_PHASES = 6
PHASES = ("moe0", "attn", "moe1", "tree0", "mix", "tree1")


def shape_constants():
    ident = np.eye(P, dtype=np.float32)
    sel = np.zeros((P, NE, P), np.float32)
    for e in range(NE):
        sel[e, e] = 1.0
        sel[NE + e, e] = 1.0
    before = np.broadcast_to(np.tril(np.ones((NE, NE), np.float32), -1).reshape(1, -1), (P, NE * NE))
    path = np.zeros((P, 2, P), np.float32)
    target = np.full((P, 2), 99.0, np.float32)
    for n in range(2 ** (DEPTH + 1) - 1):
        c, i = (0, n) if n < 127 else (1, n - 127)
        target[i, c] = 0.0
        m = n
        while m > 0:
            parent = (m - 1) // 2
            right = m == 2 * parent + 2
            path[parent, c, i] = -1.0 if right else 1.0
            target[i, c] -= 1.0 if right else 0.0
            m = parent
    inv = np.float32(10000.0) ** (-np.arange(0, DR, 2, dtype=np.float32) / np.float32(DR))
    ang = np.arange(L, dtype=np.float32)[:, None] * inv.astype(np.float32)
    cos = np.repeat(np.cos(ang).astype(np.float32), 2, axis=1).T
    sin = np.repeat(np.sin(ang).astype(np.float32), 2, axis=1).T * np.array([-1, 1, -1, 1], np.float32)[:, None]
    rope_k = np.ones((P, L), np.float32)
    for r in (3 * DL, 3 * DL + 8):
        rope_k[r:r + 4] = cos
        rope_k[r + 4:r + 8] = sin
    rope_q = np.concatenate([np.tile(cos, (NH, 1)), np.tile(sin, (NH, 1))])
    rot_sel = np.zeros((P, NPAIR, 2, 4, 16), np.float32)
    for h in range(NH):
        for r in range(DR):
            rot_sel[DR * h + r, h // 2, h % 2, 0:3, DH + r] = 1.0
            rot_sel[P // 2 + DR * h + r, h // 2, h % 2, 0:3, DH + r] = 1.0
    low = np.zeros((P, 5), np.float32)
    low[DL:2 * DL, 0] = -1
    low[DL:2 * DL, 1] = -1
    low[3 * DL + 8:3 * DL + 16, 1] = -1
    low[2 * DL:3 * DL, 2] = -1
    for half in (0, 64):
        low[half + 16:half + 32, 3] = -1
        low[half + 32:half + 48, 4] = -1
    k, q = np.arange(P)[:, None], np.arange(P)[None, :]
    tri = np.tile((k <= q).astype(np.float32), (1, 4))
    return [("ident", ident), ("sel", sel.reshape(P, -1)), ("before", np.ascontiguousarray(before)),
            ("path", path.reshape(P, -1)), ("target", target), ("rope_k", rope_k), ("rope_q", rope_q),
            ("low", low), ("tri", tri), ("rot_sel", rot_sel.reshape(P, -1))]


def lay_out(x):
    g = {k: np.asarray(v) for k, v in x.items()}
    f = np.float32
    out = {}
    out["x"] = g["L0_attn_x"]
    up = np.zeros((P, NX, 2, P), f)
    down = np.zeros((P, NX, P), f)
    up[:, 0, 0], up[:, 0, 1], down[:, 0] = g["L0_ffn_sw1"], g["L0_ffn_sw3"], g["L0_ffn_sw2"]
    up[:, 1:, 0] = g["L0_ffn_w1"].transpose(1, 0, 2)
    up[:, 1:, 1] = g["L0_ffn_w3"].transpose(1, 0, 2)
    down[:, 1:] = g["L0_ffn_w2"].transpose(1, 0, 2)
    out["up"], out["down"] = up.reshape(P, -1), down.reshape(P, -1)
    router = np.zeros((P, P), f)
    router[:, :NE] = g["L0_ffn_router_w"]
    out["router"] = router
    out["ebias"] = np.tile(g["L0_ffn_expert_bias"][None, :], (P, 1))
    kr = g["L0_attn_W_KR"]
    swap = [1, 0, 3, 2]
    wc = np.zeros((P, 2, P), f)
    for i in range(3):
        wc[:, 0, DL * i:DL * i + DL] = g["L0_attn_W_DQ"]
        wc[:, 1, DL * i:DL * i + DL] = g["L0_attn_W_DKV"]
    for r in (3 * DL, 3 * DL + 8):
        wc[:, 1, r:r + 4] = kr
        wc[:, 1, r + 4:r + 8] = kr[:, swap]
    out["latent"] = wc.reshape(P, -1)
    uq = g["L0_attn_W_UQ"].reshape(DL, NH, DH)
    qr = g["L0_attn_W_QR"].reshape(DL, NH, DR)
    uk = g["L0_attn_W_UK"].reshape(DL, NH, DH)
    wq = np.zeros((P, NPAIR, 2, 4, 16), f)
    wk = np.zeros((P, NPAIR, 2, 4, 16), f)
    wv = np.zeros((P, P), f)
    wr = np.zeros((P, P), f)
    for i in range(3):
        r = slice(DL * i, DL * i + DL)
        wv[r] = g["L0_attn_W_UV"]
        wr[r, :P // 2] = qr.reshape(DL, NH * DR)
        wr[r, P // 2:] = qr[:, :, swap].reshape(DL, NH * DR)
        for h in range(NH):
            for blk in range(3):
                wq[r, h // 2, h % 2, blk, 0:8] = uq[:, h]
                wk[r, h // 2, h % 2, blk, 0:8] = uk[:, h]
    for r in range(16):
        wk[3 * DL + r, :, :, 0:3, 8 + r % 4] = 1.0
    out["pairs"] = np.concatenate([wq.reshape(P, -1), wk.reshape(P, -1), wv, wr], axis=1)
    out["wo"] = g["L0_attn_W_O"]
    win = g["L1_ffn_W_in"].reshape(TREES, 255, P)
    b = g["L1_ffn_b_in"].reshape(TREES, 255)
    wout = g["L1_ffn_W_out"].reshape(P, TREES, 255)
    tin = np.zeros((P, TREES, 2, P), f)
    tout = np.zeros((P, TREES, 2, P), f)
    tb = np.zeros((P, TREES, 2), f)
    for c, (a, n) in enumerate(((0, 127), (127, 128))):
        tin[:, :, c, :n] = win[:, a:a + n].transpose(2, 0, 1)
        tout[:n, :, c, :] = wout[:, :, a:a + n].transpose(2, 1, 0)
        tb[:n, :, c] = b[:, a:a + n].T
    out["tin"], out["tout"], out["tb"] = tin.reshape(P, -1), tout.reshape(P, -1), tb.reshape(P, -1)
    mw = np.zeros((P, 10, P), f)
    mw[:, 0] = g["L1_attn_value_W"].T
    mw[:, 1:] = g["L1_attn_gate_W"].reshape(9, P, P).transpose(2, 0, 1)
    out["mixw"] = mw.reshape(P, -1)
    out["gb"] = np.tile(np.concatenate([g["L1_attn_gamma"], g["L1_attn_beta"]])[None, :], (P, 1))
    for name, a in shape_constants():
        out[name] = a
    return {k: np.ascontiguousarray(v) for k, v in out.items()}


def macaron(nc, d, out, n_phases=6):
    with ExitStack() as ctx:
        def sb(name, shape, dt=F32):
            return ctx.enter_context(nc.sbuf_tensor(name, shape, dt))

        def sem(name):
            return ctx.enter_context(nc.semaphore(name))

        X = sb("X", [P, NB * TT, P])
        xhi = sb("xhi", [P, NB * L], F32R)
        xlo = sb("xlo", [P, NB * L], F32R)
        xn = sb("xn", [P, TT, P])
        stats = sb("stats", [P, TT, 6])
        mv = sb("mv", [P, TT, 2])
        veps = sb("veps", [P, TT])
        rstd = sb("rstd", [P, TT])
        mhalf = sb("mhalf", [P, TT])
        yT = sb("yT", [P, L])

        UP_A, UP_B = slice(0, 4 * P), slice(4 * P, NX * 2 * P)
        ident = sb("ident_s", [P, P])
        before = sb("before_s", [P, NE, NE])
        target = sb("target_s", [P, 2])
        rope_k = sb("rope_k_s", [P, L])
        rope_q = sb("rope_q_s", [P, L])
        low = sb("low_s", [P, 5])
        tri = sb("tri_s", [P, 2, 2 * P])
        ebias = sb("ebias_s", [P, NE])
        gb = sb("gb_s", [P, 2, P])
        tb = sb("tb_s", [P, NCH])
        down = sb("down_s", [P, NX, P])
        wo = sb("wo_s", [P, P])
        up_hi = sb("up_hi", [P, NX * 2, P], F32R)
        up_lo = sb("up_lo", [P, NX * 2, P], F32R)
        raw_r = sb("raw_r", [P, P])
        router_hi = sb("router_hi", [P, P], F32R)
        router_lo = sb("router_lo", [P, P], F32R)
        sel = sb("sel_s", [P, NE, P], F32R)
        lat_hi = sb("lat_hi", [P, 2, P], F32R)
        lat_lo = sb("lat_lo", [P, 2, P], F32R)
        pair_w = sb("pair_w", [P, 18, P], F32R)
        tin = sb("tin_s", [P, 2, NCH * P], F32R)
        tin_hi, tin_lo = (tin[:, i, :].rearrange("p (a b) -> p a b", a=NCH) for i in range(2))
        CQ, CK = tin[:, 0, :], tin[:, 1, :]
        pair_tmp = tin[:].rearrange("p a b -> p (a b)")[:, 0:18 * P]
        path = sb("path_s", [P, 2, P], BF16)
        mix_w = sb("mix_w", [P, 20 * P], F32R)
        mix_hi = mix_w[:, 0:10 * P].rearrange("p (a b) -> p a b", a=10)
        mix_lo = mix_w[:, 10 * P:20 * P].rearrange("p (a b) -> p a b", a=10)
        rot_hi, rot_lo = mix_w[:, 0:2 * L], mix_w[:, 2 * L:4 * L]
        rot_sel = sb("rot_sel_s", [P, NPAIR, P], F32R)

        work = sb("work", [P, 20 * L])
        pb = work[:].rearrange("p (a w) -> p a w", a=4)

        def rows(at, n):
            return work[:, at * L:(at + n) * L].rearrange("p (a l) -> p a l", a=n)

        act_s = rows(0, 4)
        h_s = rows(4, 4)
        acc_v, prod_v, acc_p = rows(4, 2), rows(6, 2), rows(8, 2)
        prod_p = work[:, 10 * L:11 * L]
        raw = work[:, 8 * L:8 * L + 20 * P]
        sel_raw = work[:, 13 * L:15 * L]
        path_raw = work[:, 15 * L:15 * L + 2 * P]
        rot_raw = work[:, 16 * L:18 * L]
        tout = work[:, 16 * L:20 * L].rearrange("p (a b) -> p a b", a=NCH)
        lgT = sb("lgT", [P, L])
        rt = sb("rt", [P, 8, TT, NE])
        rcmp = sb("rcmp", [P, 2, TT, NE, NE])
        rsum = sb("rsum", [P, 4, TT])
        ghl = sb("ghl", [P, TT, P])
        g_hi = sb("g_hi", [P, TT, NE], F32R)
        gT = sb("gT", [P, NB * L], F32R)
        dec = sb("dec", [P, 2, L], BF16)
        ck_x = sb("ck_x", [P, L])
        c_hi = sb("c_hi", [P, L], F32R)
        ck_now = sb("ck_now", [P, L], F32R)
        v_aug = sb("v_aug", [P, TT, NH, 32])
        q_hi = sb("q_hi", [P, L], F32R)
        k_hi = sb("k_hi", [P, L], F32R)
        QS = sb("QS", [P, 2, L], F32R)
        KS = sb("KS", [P, 2, 2, L], F32R)
        avT = sb("avT", [P, L])
        rden = sb("rden", [P, TT, 4])
        att = sb("att", [P, TT, NH, DH])
        attT = yT
        vpad = v_aug[:].rearrange("p t h e -> p (t h e)")[:, 0:L + 2 * PADV]
        ln2 = ck_x[:].rearrange("p (c d) -> p c d", c=TT)

        bank = ctx.enter_context(nc.psum_tensor("bank", [P, 8, L], F32))
        psO, psT, psR, psG = 4, 5, 6, 7
        psA = psT

        s_x = [sem(f"x_loaded_{b}") for b in range(NB)]
        s_const = sem("consts_loaded")
        s_up = [sem("first_up_loaded"), sem("up_loaded")]
        s_moe = sem("moe_consts_loaded")
        s_down = sem("down_loaded")
        s_tout = sem("tout_loaded")
        s_pairs = sem("pairs_loaded")
        s_raw = {k: sem(k + "_raw_loaded") for k in ("latent", "tin", "mixw")}
        s_late = sem("late_consts_loaded")
        s_out = sem("out_stored")
        x_new = sem("x_new")
        ln_stat, ln_agg, ln_eps, ln_rstd, ln_xn = (sem("ln_" + k) for k in ("stat", "agg", "eps", "rstd", "xn"))
        xn_ps, x_hi_ready, x_lo_ready = sem("xn_transposed"), sem("x_hi_ready"), sem("x_lo_ready")
        y_sb, y_ps = sem("y_in_sbuf"), sem("y_token_major")
        w_hi = {k: sem(k + "_hi_ready") for k in ("up", "pairs")}
        w_ready = {k: sem(k + "_split") for k in ("up", "router", "sel", "latent", "pairs", "tin", "mixw", "path", "rot")}
        setup_v, setup_p = sem("vector_setup"), sem("pool_setup")
        S = {}
        for ph in PHASES:
            kind = ph[:-1] if ph[-1].isdigit() else ph
            names = {
                "moe": ("gate_ps", "up_ps", "bc_ps", "silu", "sg", "h", "down", "lg_ps", "lg_sb", "lgt_ps",
                        "r_exp_in", "r_exp", "r_chain", "ghl", "ghl_ps", "gT"),
                "attn": ("lat_ps", "ck_x", "c_hi", "c_done", "rot_ps", "rot_x", "rot_hi", "rot", "ck_now", "v_ps", "v_sb",
                         "qp_ps", "qhi", "qs", "kp_ps", "khi", "ks", "scores", "exp", "clip", "masked", "av", "avT",
                         "avt_ps", "rden", "att", "att_ps", "attT"),
                "tree": ("logit_ps", "silu", "dec", "cnt", "mask", "outp"),
                "mix": ("v_ps", "v_sb", "v_wrap", "gate_ps", "gate", "prod_v", "sum_v", "prod_p", "sum_p",
                        "l_stat", "l_agg", "l_eps", "l_rstd", "l_n", "l_g"),
            }[kind]
            S[ph] = {n: sem(f"{ph}_{n}") for n in names}

        def phases():
            for p, name in enumerate(PHASES[:n_phases]):
                yield p, name

        def wait_apart(eng, s, value):
            eng.wait_ge(s, value)
            eng.nop(nofuse=True)

        def over_batches(eng, p, body):
            more = p < n_phases - 1
            body(0, False, True)
            with eng.Fori(1, NB - 1) as b:
                body(b, False, more)
            body(NB - 1, True, more)

        def summed(p, b):
            q = p - 1 if isinstance(b, int) and b == 0 else p
            if q < 0 or (q != p and PHASES[q] == "attn"):
                return None
            return "mix" if PHASES[q] == "mix" else "y"

        def at_least(value):
            return max(value, 0) if isinstance(value, int) else value

        A = PHASES.index("attn")

        def before_of(b):
            return (b + NB - 1) % NB

        block = ctx.enter_context(nc.Block())

        @block.sync
        def _(sp):
            def load_x(b):
                sp.dma_start(X[:, TT * b:TT * (b + 1), :], d["x"][b].rearrange("(c p) d -> p c d", p=P)).then_inc(s_x[b], 16)

            load_x(0)
            sp.dma_start(ident[:], d["ident"]).then_inc(s_const, 16)
            sp.dma_start(raw_r[:], d["router"]).then_inc(s_moe, 16)
            sp.dma_start(raw[:, UP_A], d["up"][:, UP_A]).then_inc(s_up[0], 16)
            load_x(1)
            sp.dma_start(before[:].rearrange("p a b -> p (a b)"), d["before"]).then_inc(s_moe, 16)
            sp.dma_start(ebias[:], d["ebias"]).then_inc(s_moe, 16)
            sp.dma_start(sel_raw, d["sel"]).then_inc(s_moe, 16)
            sp.dma_start(raw[:, UP_B], d["up"][:, UP_B]).then_inc(s_up[1], 16)
            sp.dma_start(down[:].rearrange("p a b -> p (a b)"), d["down"]).then_inc(s_down, 16)
            load_x(2)
            load_x(3)
            for t, name in ((low, "low"), (rope_k, "rope_k"), (rope_q, "rope_q"), (target, "target"), (tb, "tb"), (wo, "wo")):
                sp.dma_start(t[:], d[name]).then_inc(s_late, 16)
            for t, name in ((tri, "tri"), (gb, "gb")):
                sp.dma_start(t[:].rearrange("p a b -> p (a b)"), d[name]).then_inc(s_late, 16)
            sp.dma_start(rot_raw, d["rot_sel"]).then_inc(s_late, 16)
            sp.dma_start(path_raw, d["path"]).then_inc(s_late, 16)
            sp.wait_ge(w_ready["up"], 2)
            sp.dma_start(raw[:, 0:2 * P], d["latent"]).then_inc(s_raw["latent"], 16)
            sp.dma_start(raw[:, 2 * P:20 * P], d["pairs"]).then_inc(s_pairs, 16)
            if n_phases > 2:
                sp.wait_ge(x_new, 2 * NB)
                sp.dma_start(tout.rearrange("p a b -> p (a b)"), d["tout"]).then_inc(s_tout, 16)
                sp.dma_start(raw[:, 0:NCH * P], d["tin"]).then_inc(s_raw["tin"], 16)
                sp.wait_ge(w_ready["tin"], 1)
                sp.dma_start(raw[:, 0:10 * P], d["mixw"]).then_inc(s_raw["mixw"], 16)
            base = NB * (n_phases - 1)
            for b in range(NB):
                sp.wait_ge(x_new, base + b + 1)
                sp.dma_start(out[b].rearrange("(c p) d -> p c d", p=P), X[:, TT * b:TT * (b + 1), :]).then_inc(s_out, 16)
            sp.wait_ge(s_out, 16 * NB)

        @block.gpsimd
        def _(pool):
            def rstd_of(n):
                pool.wait_ge(ln_eps, n + 1)
                nc.gpsimd.tensor_tensor(rstd[:], veps[:], mhalf[:], ALU.pow).then_inc(ln_rstd, 1)

            nc.gpsimd.memset(mhalf[:], -0.5).then_inc(setup_p, 1)
            nc.gpsimd.memset(ghl[:], 0.0).then_inc(setup_p, 1)
            nc.gpsimd.memset(v_aug[:], 0.0).then_inc(setup_p, 1)
            pool.wait_ge(setup_p, 3)
            nc.gpsimd.memset(v_aug[:, :, :, DH:DH + 1], 1.0).then_inc(setup_p, 1)
            rstd_of(0)
            rstd_of(1)
            nc.gpsimd.memset(KS[:].bitcast(F32), 0.0).then_inc(setup_p, 1)

            def split(hi, lo, src, ready):
                nc.gpsimd.tensor_copy(hi, src).then_inc(ready[0], 1)
                pool.wait_ge(ready[0], ready[1])
                nc.gpsimd.tensor_tensor(lo, src, hi.bitcast(F32), ALU.subtract).then_inc(ready[2], 1)

            rstd_of(2)
            pool_hi = setup_p
            count = [5]

            def split_weights(name, hi, lo, src):
                count[0] += 1
                split(hi, lo, src, (pool_hi, count[0], w_ready[name]))

            for p, ph in phases():
                s = S[ph]
                if ph == "moe0":
                    rstd_of(NB * (p + 1) - 1)
                    pool.wait_ge(s_raw["latent"], 16)
                    split_weights("latent", lat_hi[:], lat_lo[:], raw[:, 0:2 * P].rearrange("p (a b) -> p a b", a=2))
                    pool.wait_ge(s_pairs, 16)
                    nc.gpsimd.tensor_copy(pair_tmp, raw[:, 2 * P:20 * P]).then_inc(w_hi["pairs"], 1)
                    pool.wait_ge(s_late, 160)
                    nc.gpsimd.tensor_copy(path[:].rearrange("p a b -> p (a b)"), path_raw).then_inc(w_ready["path"], 1)
                    nc.gpsimd.tensor_copy(rot_sel[:].rearrange("p a b -> p (a b)"), rot_raw).then_inc(w_ready["rot"], 1)
                    if p < n_phases - 1:
                        with pool.Fori(1, NB) as b:
                            rstd_of(NB * (p + 1) + b - 1)
                elif ph == "attn":
                    def body(b, last, renorm):
                        for pr in range(NPAIR):
                            t = pb[:, pr % 4, :]
                            for g, (at, w) in enumerate(((0, P), (2 * L, 2 * P), (4 * L, P))):
                                if pr == 5 and g == 2 and renorm:
                                    rstd_of(NB * (p + 1) + b - 1)
                                pool.wait_ge(s["clip"], 3 * (NPAIR * b + pr) + g + 1)
                                v = t[:, at:at + 2 * (L if g < 2 else L // 2)].rearrange("p (j l) -> p j l", j=2)[:, :, 0:w]
                                nc.gpsimd.tensor_tensor(v, v, tri[:, :, 0:w], ALU.mult).then_inc(s["masked"], 1)
                    over_batches(pool, p, body)
                elif ph == "mix":
                    def mixture_rstd(b):
                        if isinstance(b, int) and b == 0:
                            return
                        pool.wait_ge(S["mix"]["l_eps"], b)
                        nc.gpsimd.tensor_tensor(rstd[:], veps[:], mhalf[:], ALU.pow).then_inc(S["mix"]["l_rstd"], 1)

                    def body(b, last, renorm):
                        mixture_rstd(b)
                        if renorm:
                            rstd_of(NB * (p + 1) + b - 1)
                        pool.wait_ge(s["v_wrap"], b + 1)
                        for i, g in enumerate((2, 5, 8)):
                            pool.wait_ge(s["gate"], 9 * b + g + 1)
                            dst = acc_p[:, 0, :] if i == 0 else prod_p[:]
                            if i == 0:
                                pool.wait_ge(s["sum_v"], 5 * b)
                            sh = PADV + SHIFTS[g]
                            nc.gpsimd.tensor_tensor(dst, act_s[:, g % 3, :], vpad[:, sh:sh + L], ALU.mult).then_inc(s["prod_p"], 1)
                            pool.wait_ge(s["prod_p"], 3 * b + i + 1)
                            if i:
                                nc.gpsimd.tensor_tensor(acc_p[:, i % 2, :], acc_p[:, 1 - i % 2, :], prod_p[:], ALU.add).then_inc(s["sum_p"], 1)
                                pool.wait_ge(s["sum_p"], 2 * b + i)
                    over_batches(pool, p, body)
                else:
                    if ph == "tree1":
                        mixture_rstd(NB)
                    rstd_of(NB * (p + 1) - 1)
                    if ph == "moe1":
                        pool.wait_ge(s_raw["tin"], 16)
                        split_weights("tin", tin_hi[:], tin_lo[:], raw[:, 0:NCH * P].rearrange("p (a b) -> p a b", a=NCH))
                        pool.wait_ge(s_raw["mixw"], 16)
                        split_weights("mixw", mix_hi[:], mix_lo[:], raw[:, 0:10 * P].rearrange("p (a b) -> p a b", a=10))
                    if p < n_phases - 1:
                        with pool.Fori(1, NB) as b:
                            rstd_of(NB * (p + 1) + b - 1)

        @block.scalar
        def _(act):
            def copy(dst, src, **kw):
                return nc.scalar.activation(dst, src, ACT.Copy, **kw)

            def x_high(n, b, bk=psT):
                act.wait_ge(xn_ps, n + 1)
                copy(xhi[:, bass.ds(b * L, L)], bank[:, bk, :]).then_inc(x_hi_ready, 1)

            def y_copy(n, done, count):
                act.wait_ge(done, count)
                act.wait_ge(y_ps, n - NB)
                copy(yT[:], bank[:, psO, :], scale=0.5).then_inc(y_sb, 1)

            def tail_copy(p, b):
                first = isinstance(b, int) and b == 0
                q = PHASES[p - 1] if first else PHASES[p]
                if (first and p == 0) or q in ("attn", "mix"):
                    return
                done, per = (S[q]["down"], NX) if q.startswith("moe") else (S[q]["outp"], NCH)
                y_copy(NB * (p + 1) + b - 1, done, per * (NB if first else b))

            def up_high(k, cols):
                act.wait_ge(s_up[k], 16)
                copy(up_hi[:].rearrange("p a b -> p (a b)")[:, cols], raw[:, cols]).then_inc(w_hi["up"], 1)

            def router_logits(sM, b, bk=psR):
                act.wait_ge(sM["lg_ps"], b + 1)
                copy(lgT[:], bank[:, bk, :]).then_inc(sM["lg_sb"], 1)

            def router_exp(sM, b, bk=psR):
                act.wait_ge(sM["r_exp_in"], b + 1)
                nc.scalar.activation(rt[:, 2], rt[:, 1], ACT.Exp).then_inc(sM["r_exp"], 1)

            def weights_T(sM, b, bk=psR):
                act.wait_ge(sM["ghl_ps"], b + 1)
                copy(gT[:, bass.ds(b * L, L)], bank[:, bk, :]).then_inc(sM["gT"], 1)

            def latent_high(b, k, bk=psA):
                act.wait_ge(S["attn"]["lat_ps"] if k == 0 else S["attn"]["ck_x"], 2 * b + 1 if k == 0 else b + 1)
                act.wait_ge(S["attn"]["c_done"], 2 * b + k)
                copy(c_hi[:], bank[:, bk, :] if k == 0 else ck_x[:]).then_inc(S["attn"]["c_hi"], 1)

            def rot_high(b):
                act.wait_ge(S["attn"]["rot_x"], b + 1)
                copy(rot_hi[:, bass.ds((b % 2) * L, L)], ck_x[:]).then_inc(S["attn"]["rot_hi"], 1)

            def queries_high(i, bk):
                act.wait_ge(S["attn"]["qp_ps"], i + 1)
                act.wait_ge(S["attn"]["qs"], i)
                copy(q_hi[:], bank[:, bk, :]).then_inc(S["attn"]["qhi"], 1)

            def keys_high(i, bk):
                act.wait_ge(S["attn"]["kp_ps"], i + 1)
                act.wait_ge(S["attn"]["ks"], i)
                copy(k_hi[:], bank[:, bk, :]).then_inc(S["attn"]["khi"], 1)

            for p, ph in phases():
                s = S[ph]
                n0 = NB * (p + 1)
                if ph.startswith("moe"):
                    ahead = p + 1 == A and p < n_phases - 1

                    def body(b, last, renorm):
                        first = isinstance(b, int) and b == 0
                        tail_copy(p, b)
                        for i in range(NX):
                            act.wait_ge(s["gate_ps"], NX * b + i + 1)
                            act.wait_ge(s["h"], NX * b + max(i - 1, 0))
                            nc.scalar.activation(act_s[:, i % 2, :], bank[:, i % 2, :], ACT.Silu).then_inc(s["silu"], 1)
                            if first and i == 0:
                                if p == 0:
                                    weights_T(s, 0)
                                    up_high(1, UP_B)
                                    x_high(1, 1)
                            if first and i == 2 and p == 0:
                                x_high(2, 2)
                            if i == 5 and renorm:
                                x_high(n0 + b - 1, before_of(b))
                            if not last:
                                if i == 1:
                                    router_logits(s, b + 1)
                                if i == 3:
                                    router_exp(s, b + 1)
                                if i == 8:
                                    weights_T(s, b + 1)
                            elif ahead:
                                if i in (1, 2):
                                    latent_high(0, i - 1, psR)
                                if i == 3:
                                    rot_high(0)
                                if i == 5:
                                    queries_high(0, psR)
                                if i == 6:
                                    keys_high(0, psR)
                    if p == 0:
                        x_high(0, 0)
                        up_high(0, UP_A)
                        router_logits(s, 0)
                        router_exp(s, 0)
                    over_batches(act, p, body)
                elif ph == "attn":
                    def av_copy(i):
                        act.wait_ge(s["av"], i + 1)
                        act.wait_ge(s["avt_ps"], i)
                        copy(avT[:], bank[:, psR, :]).then_inc(s["avT"], 1)

                    def att_copy(b):
                        act.wait_ge(s["att_ps"], b + 1)
                        copy(attT[:], bank[:, psG, :]).then_inc(s["attT"], 1)

                    def exp(b, pr, g):
                        act.wait_ge(s["scores"], 3 * (NPAIR * b + pr) + g + 1)
                        act.wait_ge(s["av"], at_least(4 * b + pr // 2 - 1))
                        at, w = (0, L) if g == 0 else (2 * L, L) if g == 1 else (4 * L, L // 2)
                        dst = pb[:, pr % 4, at:at + 2 * w]
                        if g < 2:
                            dst, src = dst.rearrange("p (j l) -> p j l", j=2), bank[:, 2 * g:2 * g + 2, :]
                        else:
                            src = bank[:, 4, :]
                        nc.scalar.activation(dst, src, ACT.Exp, scale=QK_SCALE).then_inc(s["exp"], 1)

                    def body(b, last, renorm):
                        first = isinstance(b, int) and b == 0
                        for pr in range(NPAIR):
                            nxt = not (last and pr == NPAIR - 1)
                            if nxt:
                                queries_high(NPAIR * b + pr + 1, psA)
                            exp(b, pr, 0)
                            if pr == 3 and not first:
                                att_copy(b - 1)
                            if nxt:
                                keys_high(NPAIR * b + pr + 1, psG)
                            if pr == 2 and not last:
                                latent_high(b + 1, 0)
                            if pr == 3 and not last:
                                latent_high(b + 1, 1)
                            if pr == 4 and not last:
                                rot_high(b + 1)
                            if last and p < n_phases - 1:
                                if pr == 2:
                                    router_logits(S["moe1"], 0, psA)
                                if pr == 3:
                                    router_exp(S["moe1"], 0)
                                if pr == 6:
                                    weights_T(S["moe1"], 0, psA)
                            if pr == 7 and renorm:
                                x_high(n0 + b - 1, before_of(b), psA)
                            exp(b, pr, 1)
                            if pr == 1:
                                act.wait_ge(s["v_ps"], b + 1)
                                act.wait_ge(s["av"], 4 * b)
                                copy(v_aug[:, :, :, 0:DH], bank[:, psG, :].rearrange("p (t h e) -> p t h e", t=TT, h=NH)).then_inc(s["v_sb"], 1)
                            exp(b, pr, 2)
                            if pr % 2 == 1 and not (first and pr == 1):
                                av_copy(4 * b + (pr - 1) // 2 - 1)
                    tail_copy(p, 0)
                    for w in ("path", "rot", "sel", "latent", "pairs"):
                        act.wait_ge(w_ready[w], 1)
                    over_batches(act, p, body)
                    av_copy(4 * NB - 1)
                    att_copy(NB - 1)
                elif ph.startswith("tree"):
                    def body(b, last, renorm):
                        tail_copy(p, b)
                        for i in range(NCH):
                            act.wait_ge(s["logit_ps"], NCH * b + i + 1)
                            act.wait_ge(s["mask"], NCH * b + max(i - 3, 0))
                            nc.scalar.activation(act_s[:, i % 4, :], bank[:, i % 4, :], ACT.Silu,
                                                 bias=tb[:, i:i + 1]).then_inc(s["silu"], 1)
                            if i == 9 and renorm:
                                x_high(n0 + b - 1, before_of(b))
                    act.wait_ge(s_late, 160)
                    over_batches(act, p, body)
                elif ph == "mix":
                    def body(b, last, renorm):
                        if isinstance(b, int) and b == 0:
                            tail_copy(p, b)
                        act.wait_ge(s["v_ps"], b + 1)
                        act.wait_ge(s["sum_v"], 5 * b)
                        act.wait_ge(s["prod_p"], 3 * b)
                        copy(vpad[:, PADV:PADV + L], bank[:, psO, :]).then_inc(s["v_sb"], 1)
                        act.wait_ge(s["v_sb"], b + 1)
                        copy(vpad[:, 0:PADV], vpad[:, L:L + PADV])
                        copy(vpad[:, L + PADV:], vpad[:, PADV:2 * PADV]).then_inc(s["v_wrap"], 1)
                        for g in range(9):
                            act.wait_ge(s["gate_ps"], 9 * b + g + 1)
                            if g >= 3:
                                if g % 3 == 2:
                                    act.wait_ge(s["prod_p"], 3 * b + (g - 3) // 3 + 1)
                                else:
                                    act.wait_ge(s["prod_v"], 6 * b + 2 * ((g - 3) // 3) + (g - 3) % 3 + 1)
                            else:
                                act.wait_ge(s["prod_p"], 3 * b)
                                act.wait_ge(s["prod_v"], 6 * b)
                            nc.scalar.activation(act_s[:, g % 3, :], bank[:, g % 3, :], ACT.Sigmoid).then_inc(s["gate"], 1)
                            if g == 7 and renorm:
                                x_high(n0 + b - 1, before_of(b))
                    over_batches(act, p, body)
                    act.wait_ge(s["prod_v"], 6 * NB)
                    act.wait_ge(s["prod_p"], 3 * NB)
            if PHASES[n_phases - 1] not in ("attn", "mix"):
                last = S[PHASES[n_phases - 1]]
                done, count = (last["down"], NX * NB) if "down" in last else (last["outp"], NCH * NB)
                y_copy(NB * (n_phases + 1) - 1, done, count)

        @block.vector
        def _(dve):
            V = nc.vector

            def normalise(n, b):
                for c in range(TT):
                    i = V.bn_stats(stats[:, c, :], X[:, bass.ds(b * TT + c, 1), :])
                i.then_inc(ln_stat, 1)
                wait_apart(dve, ln_stat, n + 1)
                for c in range(TT):
                    i = V.bn_aggr(mv[:, c, :], stats[:, c, :])
                i.then_inc(ln_agg, 1)
                dve.wait_ge(ln_agg, n + 1)
                V.tensor_scalar(veps[:], mv[:, :, 1], EPS, None, ALU.add).then_inc(ln_eps, 1)

            def normalised(n, b):
                dve.wait_ge(ln_rstd, n + 1)
                dve.wait_ge(xn_ps, n)
                for c in range(TT):
                    i = V.tensor_scalar(xn[:, c, :].rearrange("p (o d) -> p o d", o=1), X[:, bass.ds(b * TT + c, 1), :], mv[:, c, 0:1], rstd[:, c:c + 1],
                                        ALU.subtract, ALU.mult)
                i.then_inc(ln_xn, 1)

            def x_low(n, b, bk=psT):
                dve.wait_ge(x_hi_ready, n + 1)
                V.tensor_tensor(xlo[:, bass.ds(b * L, L)], bank[:, bk, :], xhi[:, bass.ds(b * L, L)].bitcast(F32),
                                ALU.subtract).then_inc(x_lo_ready, 1)

            def add_y(n, b, src, done, count):
                dve.wait_ge(done, count)
                dst = X[:, bass.ds(b * TT, TT), :]
                V.tensor_tensor(dst, dst, src, ALU.add).then_inc(x_new, 1)
                wait_apart(dve, x_new, n - NB + 1)

            def tok(bk):
                return bank[:, bk, :].rearrange("p (c d) -> p c d", c=TT)

            def mixture_norm(lb):
                m = S["mix"]
                for c in range(TT):
                    i = V.bn_stats(stats[:, c, :], bank[:, psT, c * P:(c + 1) * P])
                i.then_inc(m["l_stat"], 1)
                wait_apart(dve, m["l_stat"], lb + 1)
                for c in range(TT):
                    i = V.bn_aggr(mv[:, c, :], stats[:, c, :])
                i.then_inc(m["l_agg"], 1)
                dve.wait_ge(m["l_agg"], lb + 1)
                V.tensor_scalar(veps[:], mv[:, :, 1], EPS, None, ALU.add).then_inc(m["l_eps"], 1)
                dve.wait_ge(m["l_rstd"], lb + 1)
                for c in range(TT):
                    i = V.tensor_scalar(ln2[:, c, :], bank[:, psT, c * P:(c + 1) * P], mv[:, c, 0:1], rstd[:, c:c + 1],
                                        ALU.subtract, ALU.mult)
                i.then_inc(m["l_n"], 1)
                dve.wait_ge(m["l_n"], lb + 1)
                V.tensor_tensor(ln2[:], ln2[:], gb[:, 0, :].unsqueeze(1).to_broadcast([P, TT, P]), ALU.mult).then_inc(m["l_g"], 1)
                dve.wait_ge(m["l_g"], 2 * lb + 1)
                V.tensor_tensor(ln2[:], ln2[:], gb[:, 1, :].unsqueeze(1).to_broadcast([P, TT, P]), ALU.add).then_inc(m["l_g"], 1)
                dve.wait_ge(m["l_g"], 2 * lb + 2)

            def tail_add(p, b, renorm, bk=psT):
                kind = summed(p, b)
                n = NB * (p + 1) + b - 1
                if kind is None:
                    return
                if kind == "mix":
                    wait_apart(dve, y_ps, n - NB + 1)
                    mixture_norm(NB - 1 if PHASES[p] != "mix" else b - 1)
                    add_y(n, before_of(b), ln2[:], y_ps, n - NB + 1)
                else:
                    add_y(n, before_of(b), tok(bk), y_ps, n - NB + 1)
                if renorm:
                    normalise(n, before_of(b))

            def up_low(k, cols):
                dve.wait_ge(w_hi["up"], k + 1)
                V.tensor_tensor(up_lo[:].rearrange("p a b -> p (a b)")[:, cols], raw[:, cols], up_hi[:].bitcast(F32).rearrange("p a b -> p (a b)")[:, cols],
                                ALU.subtract).then_inc(w_ready["up"], 1)

            KR = 12

            def router_1(sM, b, bk):
                c = KR * b
                dve.wait_ge(sM["lgt_ps"], b + 1)
                V.tensor_copy(rt[:, 0], tok(bk)[:, :, 0:NE]).then_inc(sM["r_chain"], 1)
                dve.wait_ge(sM["r_chain"], c + 1)
                V.tensor_reduce(rsum[:, 0, :], rt[:, 0], AX.X, ALU.max).then_inc(sM["r_chain"], 1)
                dve.wait_ge(sM["r_chain"], c + 2)
                V.tensor_tensor(rt[:, 1], rt[:, 0], rsum[:, 0, :].unsqueeze(2).to_broadcast([P, TT, NE]), ALU.subtract).then_inc(sM["r_exp_in"], 1)

            def router_2(sM, b, part):
                c = KR * b + 2
                k = [(0, 4, 6)[part]]

                def step(ins):
                    ins.then_inc(sM["r_chain"], 1)
                    k[0] += 1
                    dve.wait_ge(sM["r_chain"], c + k[0])
                mine = rt[:, 4].unsqueeze(3).to_broadcast([P, TT, NE, NE])
                theirs = rt[:, 4].unsqueeze(2).to_broadcast([P, TT, NE, NE])
                if part == 0:
                    dve.wait_ge(sM["r_exp"], b + 1)
                    step(V.tensor_reduce(rsum[:, 1, :], rt[:, 2], AX.X, ALU.add))
                    step(V.reciprocal(rsum[:, 2, :], rsum[:, 1, :]))
                    step(V.tensor_tensor(rt[:, 3], rt[:, 2], rsum[:, 2, :].unsqueeze(2).to_broadcast([P, TT, NE]), ALU.mult))
                    step(V.tensor_tensor(rt[:, 4], rt[:, 3], ebias[:].unsqueeze(1).to_broadcast([P, TT, NE]), ALU.add))
                    return
                if part == 1:
                    V.tensor_tensor(rcmp[:, 0], theirs, mine, ALU.is_gt)
                    step(V.tensor_tensor(rcmp[:, 1], theirs, mine, ALU.is_equal))
                    step(V.tensor_tensor(rcmp[:, 1], rcmp[:, 1], before[:].unsqueeze(1).to_broadcast([P, TT, NE, NE]), ALU.mult))
                    return
                step(V.tensor_tensor(rcmp[:, 0], rcmp[:, 0], rcmp[:, 1], ALU.add))
                step(V.tensor_reduce(rt[:, 5], rcmp[:, 0], AX.X, ALU.add))
                step(V.scalar_tensor_tensor(rt[:, 6], rt[:, 5], 2.0, rt[:, 3], ALU.is_lt, ALU.mult))
                step(V.tensor_copy(g_hi[:], rt[:, 6]))
                assert k[0] + 2 == KR
                dve.wait_ge(sM["ghl_ps"], b)
                V.tensor_copy(ghl[:, :, 0:NE], g_hi[:].bitcast(F32))
                V.tensor_tensor(ghl[:, :, NE:2 * NE], rt[:, 6], g_hi[:].bitcast(F32), ALU.subtract).then_inc(sM["ghl"], 1)

            def latent(b, k, bk=psA):
                dst = bass.ds(b * L, L)
                if k == 0:
                    dve.wait_ge(S["attn"]["c_hi"], 2 * b + 1)
                    V.scalar_tensor_tensor(CQ[:, dst], c_hi[:].bitcast(F32), low[:, 0:1], bank[:, bk, :], ALU.mult, ALU.add).then_inc(S["attn"]["c_done"], 1)
                    return
                dve.wait_ge(S["attn"]["lat_ps"], 2 * b + 2)
                V.tensor_tensor(ck_x[:], bank[:, bk, :], rope_k[:], ALU.mult).then_inc(S["attn"]["ck_x"], 1)
                dve.wait_ge(S["attn"]["c_hi"], 2 * b + 2)
                V.scalar_tensor_tensor(CK[:, dst], c_hi[:].bitcast(F32), low[:, 1:2], ck_x[:], ALU.mult, ALU.add).then_inc(S["attn"]["c_done"], 1)

            def rotated(b, bk=psA):
                dve.wait_ge(S["attn"]["rot_ps"], b + 1)
                dve.wait_ge(S["attn"]["c_done"], 2 * b + 2)
                V.tensor_tensor(ck_x[:], bank[:, bk, :], rope_q[:], ALU.mult).then_inc(S["attn"]["rot_x"], 1)
                dve.wait_ge(S["attn"]["rot_hi"], b + 1)
                dst = bass.ds((b % 2) * L, L)
                V.tensor_tensor(rot_lo[:, dst], ck_x[:], rot_hi[:, dst].bitcast(F32), ALU.subtract).then_inc(S["attn"]["rot"], 1)

            def latent_now(b):
                dve.wait_ge(S["attn"]["c_done"], 2 * b + 2)
                wait_apart(dve, S["attn"]["v_ps"], b)
                V.tensor_copy(ck_now[:], CK[:, bass.ds(b * L, L)].bitcast(F32)).then_inc(S["attn"]["ck_now"], 1)

            def queries(i, par, bk):
                dve.wait_ge(S["attn"]["qhi"], i + 1)
                dve.wait_ge(S["attn"]["scores"], at_least(3 * (i - 1)))
                V.scalar_tensor_tensor(QS[:, par, :], q_hi[:].bitcast(F32), low[:, 3:4], bank[:, bk, :], ALU.mult, ALU.add).then_inc(S["attn"]["qs"], 1)

            def keys(i, par, bk):
                dve.wait_ge(S["attn"]["khi"], i + 1)
                dve.wait_ge(S["attn"]["scores"], at_least(3 * (i - 1)))
                for j in range(2):
                    r = slice(64 * j, 64 * j + 64)
                    ins = V.scalar_tensor_tensor(KS[r, par, j, :], k_hi[r].bitcast(F32), low[r, 4:5], bank[r, bk, :], ALU.mult, ALU.add)
                ins.then_inc(S["attn"]["ks"], 1)

            for p, ph in phases():
                s = S[ph]
                n0 = NB * (p + 1)

                if ph.startswith("moe"):
                    ahead = p + 1 == A and p < n_phases - 1

                    def body(b, last, renorm):
                        first = isinstance(b, int) and b == 0
                        for i in range(NX):
                            if first and p == 0:
                                if i == 1:
                                    up_low(1, UP_B)
                                    normalised(1, 1)
                                    x_low(1, 1)
                                if i in (2, 3):
                                    dve.wait_ge(s_x[i], 16)
                                    normalise(i, i)
                                if i == 2:
                                    normalised(2, 2)
                                if i == 3:
                                    x_low(2, 2)
                            if i == 2:
                                tail_add(p, b, renorm)
                            if i == 4 and renorm:
                                normalised(n0 + b - 1, before_of(b))
                            if i == 6 and renorm:
                                x_low(n0 + b - 1, before_of(b))
                            if not last:
                                if i == 3:
                                    router_1(s, b + 1, psR)
                                if i in (5, 6, 7):
                                    router_2(s, b + 1, i - 5)
                            elif ahead:
                                if i == 1:
                                    dve.wait_ge(s_late, 160)
                                    dve.wait_ge(w_hi["pairs"], 1)
                                    V.scalar_tensor_tensor(pair_w[:].rearrange("p a b -> p (a b)"), pair_tmp.bitcast(F32), low[:, 2:3],
                                                           raw[:, 2 * P:20 * P], ALU.mult, ALU.add).then_inc(w_ready["pairs"], 1)
                                    dve.wait_ge(w_ready["pairs"], 1)
                                    dve.wait_ge(setup_p, 5)
                                if i in (2, 3):
                                    latent(0, i - 2, psR)
                                if i == 4:
                                    rotated(0, psR)
                                    latent_now(0)
                                if i == 6:
                                    queries(0, 0, psR)
                                if i == 7:
                                    keys(0, 0, psR)
                            j = NX * b + i
                            dve.wait_ge(s["silu"], j + 1)
                            dve.wait_ge(s["down"], NX * b + max(i - 1, 0))
                            a = act_s[:, i % 2, :]
                            if i:
                                dve.wait_ge(s["bc_ps"], NE * b + i)
                                V.tensor_tensor(a, a, bank[:, psG, :], ALU.mult).then_inc(s["sg"], 1)
                                dve.wait_ge(s["sg"], NE * b + i)
                            dve.wait_ge(s["up_ps"], j + 1)
                            V.tensor_tensor(h_s[:, i % 2, :], a, bank[:, 2 + i % 2, :], ALU.mult).then_inc(s["h"], 1)

                    if p == 0:
                        dve.wait_ge(s_x[0], 16)
                        normalise(0, 0)
                        normalised(0, 0)
                        dve.wait_ge(s_moe, 64)
                        V.tensor_copy(router_hi[:], raw_r[:]).then_inc(setup_v, 1)
                        dve.wait_ge(setup_v, 1)
                        V.tensor_tensor(router_lo[:], raw_r[:], router_hi[:].bitcast(F32), ALU.subtract).then_inc(w_ready["router"], 1)
                        x_low(0, 0)
                        up_low(0, UP_A)
                        V.tensor_copy(sel[:].rearrange("p a b -> p (a b)"), sel_raw).then_inc(w_ready["sel"], 1)
                        router_1(s, 0, psR)
                        dve.wait_ge(s_x[1], 16)
                        normalise(1, 1)
                        dve.wait_ge(setup_p, 4)
                        for part in range(3):
                            router_2(s, 0, part)
                    over_batches(dve, p, body)
                elif ph == "attn":
                    def clip(b, pr, g):
                        dve.wait_ge(s["exp"], 3 * (NPAIR * b + pr) + g + 1)
                        at, n = (0, 2 * L) if g == 0 else (2 * L, 2 * L) if g == 1 else (4 * L, L)
                        t = pb[:, pr % 4, at:at + n]
                        V.tensor_scalar(t, t, P_LOW, P_HIGH, ALU.max, ALU.min).then_inc(s["clip"], 1)

                    def heads(i, g):
                        dve.wait_ge(s["avt_ps"], i + 1)
                        o = bank[:, psG, :].rearrange("p (t h e) -> p t h e", t=TT, h=4)
                        V.reciprocal(rden[:], o[:, :, :, DH]).then_inc(s["rden"], 1)
                        dve.wait_ge(s["rden"], i + 1)
                        V.tensor_tensor(att[:, :, 4 * g:4 * g + 4, :], o[:, :, :, 0:DH],
                                        rden[:].unsqueeze(3).to_broadcast([P, TT, 4, DH]), ALU.mult).then_inc(s["att"], 1)

                    def body(b, last, renorm):
                        first = isinstance(b, int) and b == 0
                        for pr in range(NPAIR):
                            nxt = not (last and pr == NPAIR - 1)
                            i = NPAIR * b + pr + 1
                            if nxt:
                                queries(i, (pr + 1) % 2, psA)
                            if pr in (4, 6) or pr in (0, 2) and not first:
                                heads(4 * b + (pr - 4) // 2, (pr // 2 + 2) % 4)
                            clip(b, pr, 0)
                            if nxt:
                                keys(i, (pr + 1) % 2, psG)
                            if pr == 2 and not last:
                                latent(b + 1, 0)
                            if pr == 3 and not last:
                                latent(b + 1, 1)
                            if pr == 4 and not last:
                                rotated(b + 1)
                                latent_now(b + 1)
                            if pr == 5:
                                tail_add(p, b, renorm, psA)
                            if pr == 6 and renorm:
                                normalised(n0 + b - 1, before_of(b))
                            if last and p < n_phases - 1:
                                if pr == 3:
                                    router_1(S["moe1"], 0, psA)
                                if pr in (4, 5, 6):
                                    router_2(S["moe1"], 0, pr - 4)
                            if pr == 7 and renorm:
                                x_low(n0 + b - 1, before_of(b), psA)
                            clip(b, pr, 1)
                            clip(b, pr, 2)

                    over_batches(dve, p, body)
                    heads(4 * NB - 2, 2)
                    heads(4 * NB - 1, 3)
                    add_y(n0 + NB - 1, NB - 1, tok(psA), y_ps, NB * (p + 1))
                    if p < n_phases - 1:
                        normalise(n0 + NB - 1, NB - 1)
                elif ph.startswith("tree"):
                    def body(b, last, renorm):
                        for t in range(TREES):
                            if t == 1:
                                tail_add(p, b, renorm)
                            if t == 3 and renorm:
                                normalised(n0 + b - 1, before_of(b))
                            if t == 5 and renorm:
                                x_low(n0 + b - 1, before_of(b))
                            i = 2 * t
                            dve.wait_ge(s["silu"], NCH * b + i + 1)
                            dve.wait_ge(s["cnt"], NCH * b + max(i - 2, 0))
                            V.tensor_scalar(dec[:, t % 2, :], bank[:, i % 4, :], tb[:, i:i + 1], 0.0, ALU.add, ALU.is_gt).then_inc(s["dec"], 1)
                            for c in range(2):
                                j = NCH * b + i + c
                                dve.wait_ge(s["silu"], j + 1)
                                dve.wait_ge(s["cnt"], j + 1)
                                dve.wait_ge(s["outp"], NCH * b + max(i + c - 3, 0))
                                V.scalar_tensor_tensor(h_s[:, (i + c) % 4, :], bank[:, 6 + c, :], target[:, c:c + 1],
                                                       act_s[:, (i + c) % 4, :], ALU.is_equal, ALU.mult).then_inc(s["mask"], 1)
                    over_batches(dve, p, body)
                elif ph == "mix":
                    def body(b, last, renorm):
                        dve.wait_ge(s["v_wrap"], b + 1)
                        for i, g in enumerate((0, 1, 3, 4, 6, 7)):
                            j = 6 * b + i
                            dve.wait_ge(s["gate"], 9 * b + g + 1)
                            sh = PADV + SHIFTS[g]
                            dst = acc_v[:, 0, :] if i == 0 else prod_v[:, i % 2, :]
                            V.tensor_tensor(dst, act_s[:, g % 3, :], vpad[:, sh:sh + L], ALU.mult).then_inc(s["prod_v"], 1)
                            dve.wait_ge(s["prod_v"], j + 1)
                            if i:
                                V.tensor_tensor(acc_v[:, i % 2, :], acc_v[:, 1 - i % 2, :], prod_v[:, i % 2, :], ALU.add).then_inc(s["sum_v"], 1)
                                dve.wait_ge(s["sum_v"], 5 * b + i)
                            if i == 1:
                                tail_add(p, b, renorm)
                            if i == 3 and renorm:
                                normalised(n0 + b - 1, before_of(b))
                            if i == 5 and renorm:
                                x_low(n0 + b - 1, before_of(b))
                        dve.wait_ge(s["sum_p"], 2 * b + 2)
                        dve.wait_ge(y_ps, NB * p + b)
                        V.tensor_tensor(yT[:], acc_v[:, 1, :], acc_p[:, 0, :], ALU.add).then_inc(y_sb, 1)
                    over_batches(dve, p, body)
            if PHASES[n_phases - 1] != "attn":
                tail_add(n_phases - 1, NB, False)

        @block.tensor
        def _(pe):
            mm = nc.tensor.matmul

            def xpose(dst, src):
                return nc.tensor.transpose(dst, src, ident[:])

            def three(dst, whi, wlo, b):
                hi, lo = xhi[:, bass.ds(b * L, L)], xlo[:, bass.ds(b * L, L)]
                mm(dst, whi, hi, start=True, stop=False)
                mm(dst, whi, lo, start=False, stop=False)
                return mm(dst, wlo, hi, start=False, stop=True)

            def xn_T(n, bk=psT):
                pe.wait_ge(ln_xn, n + 1)
                pe.wait_ge(x_lo_ready, n)
                for c in range(TT):
                    i = xpose(bank[:, bk, c * P:(c + 1) * P], xn[:, c, :])
                i.then_inc(xn_ps, 1)

            def tail_T(p, b, renorm, bk=psT):
                if summed(p, b):
                    y_T(NB * sum(q != "attn" for q in PHASES[:p]) + b, NB * (p + 1) + b - 1, renorm, bk)

            def y_T(m, n, renorm, bk=psT):
                pe.wait_ge(y_sb, m)
                pe.wait_ge(x_new, n - NB)
                if renorm:
                    pe.wait_ge(x_lo_ready, n)
                for c in range(TT):
                    i = xpose(bank[:, bk, c * P:(c + 1) * P], yT[:, c * P:(c + 1) * P])
                i.then_inc(y_ps, 1)

            pe.wait_ge(s_const, 16)
            free = {psA: None, psG: None, psR: None}

            ysb = 0
            def router_mm(sM, b, n, bk=psR):
                pe.wait_ge(x_hi_ready, n)
                pe.wait_ge(x_lo_ready, n)
                pe.wait_ge(sM["gT"], b)
                three(bank[:, bk, :], router_hi[:], router_lo[:], b).then_inc(sM["lg_ps"], 1)

            def router_T(sM, b, bk=psR):
                pe.wait_ge(sM["lg_sb"], b + 1)
                for c in range(TT):
                    i = xpose(bank[:, bk, c * P:(c + 1) * P], lgT[:, c * P:(c + 1) * P])
                i.then_inc(sM["lgt_ps"], 1)

            def weights_T(sM, b, bk=psR):
                pe.wait_ge(sM["ghl"], b + 1)
                for c in range(TT):
                    i = xpose(bank[:, bk, c * P:(c + 1) * P], ghl[:, c, :])
                i.then_inc(sM["ghl_ps"], 1)

            def shared(sem_, value, bk=psG):
                if free[bk] is not None:
                    pe.wait_ge(*free[bk])
                free[bk] = (sem_, value)

            def latent(b, k, bk=psA):
                pe.wait_ge(x_lo_ready, NB * A + b + 1)
                shared(S["attn"]["c_done"] if k == 0 else S["attn"]["ck_x"], 2 * b + 1 if k == 0 else b + 1, bk)
                three(bank[:, bk, :], lat_hi[:, k, :], lat_lo[:, k, :], b).then_inc(S["attn"]["lat_ps"], 1)

            def rotary(b, bk=psA):
                pe.wait_ge(S["attn"]["c_done"], 2 * b + 1)
                shared(S["attn"]["rot_x"], b + 1, bk)
                mm(bank[:, bk, :], pair_w[:, 2 * NPAIR + 1, :], CQ[:, bass.ds(b * L, L)], start=True, stop=True).then_inc(S["attn"]["rot_ps"], 1)

            def queries(b, pr, i, bk=psA):
                rot = bass.ds((b % 2) * L, L)
                pe.wait_ge(S["attn"]["rot"], b + 1)
                shared(S["attn"]["qs"], i + 1, bk)
                mm(bank[:, bk, :], pair_w[:, pr, :], CQ[:, bass.ds(b * L, L)], start=True, stop=False)
                mm(bank[:, bk, :], rot_sel[:, pr, :], rot_hi[:, rot], start=False, stop=False)
                mm(bank[:, bk, :], rot_sel[:, pr, :], rot_lo[:, rot], start=False, stop=True).then_inc(S["attn"]["qp_ps"], 1)

            def keys(b, pr, i, bk=psG):
                shared(S["attn"]["ks"], i + 1, bk)
                mm(bank[:, bk, :], pair_w[:, NPAIR + pr, :], CK[:, bass.ds(b * L, L)], start=True, stop=True).then_inc(S["attn"]["kp_ps"], 1)

            for p, ph in phases():
                s = S[ph]
                n0 = NB * (p + 1)
                if ph.startswith("moe"):
                    def down_mm(b, i):
                        pe.wait_ge(s["h"], NX * b + i + 1)
                        if i == 0:
                            pe.wait_ge(y_sb, ysb + b)
                        mm(bank[:, psO, :], down[:, i, :], h_s[:, i % 2, :], start=(i == 0), stop=(i == NX - 1)).then_inc(s["down"], 1)

                    ahead = p + 1 == A and p < n_phases - 1

                    def body(b, last, renorm):
                        first = isinstance(b, int) and b == 0
                        for i in range(NX):
                            if first and p == 0 and i == 1:
                                pe.wait_ge(w_ready["sel"], 1)
                                pe.wait_ge(s_down, 16)
                            if first and p == 0 and i == 2:
                                pe.wait_ge(w_ready["up"], 2)
                            pe.wait_ge(s["silu"], NX * b + max(i - 1, 0))
                            three(bank[:, i % 2, :], up_hi[:, 2 * i, :], up_lo[:, 2 * i, :], b).then_inc(s["gate_ps"], 1)
                            pe.wait_ge(s["h"], NX * b + max(i - 1, 0))
                            three(bank[:, 2 + i % 2, :], up_hi[:, 2 * i + 1, :], up_lo[:, 2 * i + 1, :], b).then_inc(s["up_ps"], 1)
                            if i:
                                pe.wait_ge(s["gT"], b + 1)
                                pe.wait_ge(s["sg"], NE * b + i - 1)
                                mm(bank[:, psG, :], sel[:, i - 1, :], gT[:, bass.ds(b * L, L)], start=True, stop=True).then_inc(s["bc_ps"], 1)
                                down_mm(b, i - 1)
                            if first and p == 0:
                                if i == 0:
                                    weights_T(s, 0)
                                    xn_T(1)
                                if i == 2:
                                    xn_T(2)
                            if i == 1:
                                tail_T(p, b, renorm)
                            if i == 4 and renorm:
                                xn_T(n0 + b - 1)
                            if not last:
                                if i == 1:
                                    router_mm(s, b + 1, NB * p + b + 2)
                                if i == 2:
                                    router_T(s, b + 1)
                                if i == 8:
                                    weights_T(s, b + 1)
                            elif ahead:
                                if i == 1:
                                    for w in ("latent", "pairs", "rot"):
                                        pe.wait_ge(w_ready[w], 1)
                                    free[psR] = (s["gT"], NB)
                                if i in (1, 2):
                                    latent(0, i - 1, psR)
                                if i == 3:
                                    rotary(0, psR)
                                if i == 5:
                                    queries(0, 0, 0, psR)
                                if i == 6:
                                    keys(0, 0, 0, psR)
                        down_mm(b, NX - 1)

                    if p == 0:
                        xn_T(0)
                        pe.wait_ge(w_ready["router"], 1)
                        router_mm(s, 0, 1)
                        router_T(s, 0)
                        pe.wait_ge(w_ready["up"], 1)
                    over_batches(pe, p, body)
                    ysb += NB
                elif ph == "attn":
                    def scores(b, pr, g):
                        pe.wait_ge(s["qs"], NPAIR * b + pr + 1)
                        pe.wait_ge(s["ks"], NPAIR * b + pr + 1)
                        pe.wait_ge(s["exp"], at_least(3 * (NPAIR * b + pr - 1) + g + 1))
                        for kt, col in (((0, 0),), ((3, 0), (1, P)), ((2, 0),))[g]:
                            for j in range(2):
                                bk, at = (2 * g + j, col) if g < 2 else (4, j * (L // 2))
                                ins = mm(bank[:, bk, at:at + L - P * kt], KS[:, pr % 2, j, kt * P:(kt + 1) * P],
                                         QS[:, pr % 2, kt * P:L], start=True, stop=True)
                        ins.then_inc(s["scores"], 1)

                    def values(b, pr, part):
                        b, g = (b - 1, 3) if pr < 2 else (b, (pr - 2) // 2)
                        kt, at, stride, slot = ((0, 0, L, 0), (1, 2 * L + P, L, 1), (3, 2 * L, L, 1), (2, 4 * L, L // 2, 2))[2 * (pr % 2) + part]
                        pe.wait_ge(s["masked"], 3 * (NPAIR * b + 2 * g + 1) + slot + 1)
                        if kt == 0:
                            pe.wait_ge(s["v_sb"], b + 1)
                            pe.wait_ge(s["avT"], at_least(4 * b + g))
                        for q in range(4):
                            c = at + stride * (q % 2)
                            ins = mm(bank[32 * q:32 * q + 32, psR, kt * P:L], v_aug[:, kt, 4 * g + q, :],
                                     pb[:, (2 * g + q // 2) % 4, c:c + L - P * kt], start=(kt == 0), stop=(kt == 2))
                        if kt == 2:
                            ins.then_inc(s["av"], 1)

                    def heads_T(i):
                        pe.wait_ge(s["avT"], i + 1)
                        shared(s["att"], i + 1)
                        for c in range(TT):
                            ins = xpose(bank[:, psG, c * P:(c + 1) * P], avT[:, c * P:(c + 1) * P])
                        ins.then_inc(s["avt_ps"], 1)

                    def att_T(b):
                        pe.wait_ge(s["att"], 4 * b + 4)
                        shared(s["attT"], b + 1)
                        for c in range(TT):
                            ins = xpose(bank[:, psG, c * P:(c + 1) * P], att[:, c].rearrange("p h e -> p (h e)"))
                        ins.then_inc(s["att_ps"], 1)

                    def output(b):
                        pe.wait_ge(s["attT"], b + 1)
                        shared(x_new, NB * p + b + 1, psA)
                        for c in range(TT):
                            ins = mm(bank[:, psA, c * P:(c + 1) * P], attT[:, c * P:(c + 1) * P], wo[:], start=True, stop=True)
                        ins.then_inc(y_ps, 1)

                    def batch_values(b):
                        pe.wait_ge(s["ck_now"], b + 1)
                        shared(s["v_sb"], b + 1)
                        for c in range(TT):
                            ins = mm(bank[:, psG, c * P:(c + 1) * P], ck_now[:, c * P:(c + 1) * P], pair_w[:, 2 * NPAIR, :], start=True, stop=True)
                        ins.then_inc(s["v_ps"], 1)

                    def body(b, last, renorm):
                        first = isinstance(b, int) and b == 0
                        if not first:
                            free[psA], free[psG] = (x_lo_ready, n0 + b - 1), (s["ks"], NPAIR * b + 1)
                        for pr in range(NPAIR):
                            i = NPAIR * b + pr + 1
                            nb, npr = (b, pr + 1) if pr < NPAIR - 1 else (b + 1, 0)
                            nxt = not (last and pr == NPAIR - 1)
                            if nxt:
                                queries(nb, npr, i)
                            scores(b, pr, 0)
                            if pr in (4, 6) or pr in (0, 2) and not first:
                                heads_T(4 * b + (pr - 4) // 2)
                            if pr == 3 and not first:
                                att_T(b - 1)
                            if pr > 1 or not first:
                                values(b, pr, 0)
                            if nxt:
                                keys(nb, npr, i)
                            if pr == 2 and not last:
                                latent(b + 1, 0)
                            if pr == 3 and not last:
                                latent(b + 1, 1)
                            if pr == 4 and not last:
                                rotary(b + 1)
                            if pr == 5:
                                if first:
                                    shared(x_new, NB * p, psA)
                                    tail_T(p, b, renorm, psA)
                                else:
                                    output(b - 1)
                            if last and p < n_phases - 1:
                                if pr == 2:
                                    shared(S["moe1"]["lg_sb"], 1, psA)
                                    router_mm(S["moe1"], 0, NB * (p + 1) + 1, psA)
                                if pr == 3:
                                    shared(S["moe1"]["r_chain"], 1, psA)
                                    router_T(S["moe1"], 0, psA)
                                if pr == 6:
                                    shared(S["moe1"]["gT"], 1, psA)
                                    weights_T(S["moe1"], 0, psA)
                            if pr == 7 and renorm:
                                shared(x_lo_ready, n0 + b, psA)
                                xn_T(n0 + b - 1, psA)
                            scores(b, pr, 1)
                            if pr > 1 or not first:
                                values(b, pr, 1)
                            if pr == 1:
                                batch_values(b)
                            scores(b, pr, 2)

                    pe.wait_ge(setup_p, 4)
                    pe.wait_ge(y_sb, ysb)
                    pe.wait_ge(x_lo_ready, n0 - 1)
                    over_batches(pe, p, body)
                    heads_T(4 * NB - 2)
                    for part in range(4):
                        values(NB, part // 2, part % 2)
                    heads_T(4 * NB - 1)
                    att_T(NB - 1)
                    output(NB - 1)
                    pe.wait_ge(*free[psA])
                elif ph.startswith("tree"):
                    def logits(b, i):
                        pe.wait_ge(s["silu"], NCH * b + max(i - 3, 0))
                        if i % 2 == 0:
                            pe.wait_ge(s["dec"], TREES * b + max(i // 2 - 1, 0))
                        three(bank[:, i % 4, :], tin_hi[:, i, :], tin_lo[:, i, :], b).then_inc(s["logit_ps"], 1)

                    def count(b, t):
                        pe.wait_ge(s["dec"], TREES * b + t + 1)
                        for c in range(2):
                            pe.wait_ge(s["mask"], NCH * b + max(2 * t + c - 1, 0))
                            mm(bank[:, 6 + c, :], path[:, c, :], dec[:, t % 2, :], start=True, stop=True).then_inc(s["cnt"], 1)

                    def out_mm(b, i):
                        pe.wait_ge(s["mask"], NCH * b + i + 1)
                        if i == 0:
                            pe.wait_ge(y_sb, ysb + b)
                        mm(bank[:, psO, :], tout[:, i, :], h_s[:, i % 4, :], start=(i == 0), stop=(i == NCH - 1)).then_inc(s["outp"], 1)

                    def body(b, last, renorm):
                        pe.wait_ge(x_lo_ready, NB * p + b + 1)
                        logits(b, 0)
                        logits(b, 1)
                        for t in range(TREES):
                            if t < TREES - 1:
                                logits(b, 2 * t + 2)
                            count(b, t)
                            if t < TREES - 1:
                                logits(b, 2 * t + 3)
                            if t == 0:
                                tail_T(p, b, renorm)
                            if t == 4 and renorm:
                                xn_T(n0 + b - 1)
                            out_mm(b, 2 * t)
                            out_mm(b, 2 * t + 1)

                    pe.wait_ge(w_ready["tin"], 1)
                    pe.wait_ge(w_ready["path"], 1)
                    pe.wait_ge(s_tout, 16)
                    pe.wait_ge(s_late, 160)
                    over_batches(pe, p, body)
                    ysb += NB
                elif ph == "mix":
                    def body(b, last, renorm):
                        pe.wait_ge(x_lo_ready, NB * p + b + 1)
                        if isinstance(b, int) and b == 0:
                            pe.wait_ge(y_sb, ysb)
                        else:
                            pe.wait_ge(s["v_sb"], b)
                        three(bank[:, psO, :], mix_hi[:, 0, :], mix_lo[:, 0, :], b).then_inc(s["v_ps"], 1)
                        for g in range(9):
                            pe.wait_ge(s["gate"], 9 * b + max(g - 2, 0))
                            three(bank[:, g % 3, :], mix_hi[:, g + 1, :], mix_lo[:, g + 1, :], b).then_inc(s["gate_ps"], 1)
                            if g == 1:
                                tail_T(p, b, renorm)
                            if g == 6 and renorm:
                                xn_T(n0 + b - 1)
                    pe.wait_ge(w_ready["mixw"], 1)
                    over_batches(pe, p, body)
                    pe.wait_ge(s["gate"], 9 * NB)
                    ysb += NB
            if PHASES[n_phases - 1] != "attn":
                tail_T(n_phases - 1, NB, False)


def kernel(**inputs):
    import concourse.bacc as _bacc
    from concourse import mybir as _mybir
    from concourse.bass_utils import run_bass_kernel_spmd as _run

    nc = _bacc.Bacc("TRN2", target_bir_lowering=False, num_devices=1)
    arrays = lay_out(inputs)
    d = {name: nc.dram_tensor("in_" + name, a.shape, _mybir.dt.float32, kind="ExternalInput").ap() for name, a in arrays.items()}
    out = nc.dram_tensor("out", arrays["x"].shape, _mybir.dt.float32, kind="ExternalOutput").ap()
    macaron(nc, d, out, N_PHASES)
    r = _run(nc, [{"in_" + k: v for k, v in arrays.items()}], core_ids=[0])
    return r.results[0]["out"]
```

```python
from contextlib import ExitStack

import numpy as np

import concourse.bass as bass
from concourse import mybir

F32 = mybir.dt.float32
F32R = mybir.dt.float32r
BF16 = mybir.dt.bfloat16
ALU = mybir.AluOpType
ACT = mybir.ActivationFunctionType
AX = mybir.AxisListType

P = 128
NB = 4
L = 512
TT = L // P
NE = 8
NX = NE + 1
NH = 16
NPAIR = NH // 2
DL = 32
DH, DR = 8, 4
TREES = 8
DEPTH = 7
NCH = 2 * TREES
SHIFTS = (0, -32, -16, -4, -1, 1, 4, 16, 32)
PADV = 32
EPS = 1e-5
QK_SCALE = float(1.0 / np.sqrt(np.float32(DH + DR)))
P_LOW = float(np.exp(-80.0 * QK_SCALE))
P_HIGH = float(np.exp(80.0 * QK_SCALE))
PHASES = ("moe0", "attn", "moe1", "tree0", "mix", "tree1")


def shape_constants():
    ident = np.eye(P, dtype=np.float32)
    sel = np.zeros((P, NE, P), np.float32)
    for e in range(NE):
        sel[e, e] = 1.0
        sel[NE + e, e] = 1.0
    before = np.broadcast_to(np.tril(np.ones((NE, NE), np.float32), -1).reshape(1, -1), (P, NE * NE))
    path = np.zeros((P, 2, P), np.float32)
    target = np.full((P, 2), 99.0, np.float32)
    for n in range(2 ** (DEPTH + 1) - 1):
        c, i = (0, n) if n < 127 else (1, n - 127)
        target[i, c] = 0.0
        m = n
        while m > 0:
            parent = (m - 1) // 2
            right = m == 2 * parent + 2
            path[parent, c, i] = -1.0 if right else 1.0
            target[i, c] -= 1.0 if right else 0.0
            m = parent
    inv = np.float32(10000.0) ** (-np.arange(0, DR, 2, dtype=np.float32) / np.float32(DR))
    ang = np.arange(L, dtype=np.float32)[:, None] * inv.astype(np.float32)
    cos = np.repeat(np.cos(ang).astype(np.float32), 2, axis=1).T
    sin = np.repeat(np.sin(ang).astype(np.float32), 2, axis=1).T * np.array([-1, 1, -1, 1], np.float32)[:, None]
    rope_k = np.ones((P, L), np.float32)
    for r in (3 * DL, 3 * DL + 8):
        rope_k[r:r + 4] = cos
        rope_k[r + 4:r + 8] = sin
    rope_q = np.concatenate([np.tile(cos, (NH, 1)), np.tile(sin, (NH, 1))])
    rot_sel = np.zeros((P, NPAIR, 2, 4, 16), np.float32)
    for h in range(NH):
        for r in range(DR):
            rot_sel[DR * h + r, h // 2, h % 2, 0:3, DH + r] = 1.0
            rot_sel[P // 2 + DR * h + r, h // 2, h % 2, 0:3, DH + r] = 1.0
    low = np.zeros((P, 5), np.float32)
    low[DL:2 * DL, 0] = -1
    low[DL:2 * DL, 1] = -1
    low[3 * DL + 8:3 * DL + 16, 1] = -1
    low[2 * DL:3 * DL, 2] = -1
    for half in (0, 64):
        low[half + 16:half + 32, 3] = -1
        low[half + 32:half + 48, 4] = -1
    k, q = np.arange(P)[:, None], np.arange(P)[None, :]
    tri = np.tile((k <= q).astype(np.float32), (1, 4))
    return [("ident", ident), ("sel", sel.reshape(P, -1)), ("before", np.ascontiguousarray(before)),
            ("path", path.reshape(P, -1)), ("target", target), ("rope_k", rope_k), ("rope_q", rope_q),
            ("low", low), ("tri", tri), ("rot_sel", rot_sel.reshape(P, -1))]


def lay_out(x):
    g = {k: np.asarray(v) for k, v in x.items()}
    f = np.float32
    out = {}
    out["x"] = g["L0_attn_x"]
    up = np.zeros((P, NX, 2, P), f)
    down = np.zeros((P, NX, P), f)
    up[:, 0, 0], up[:, 0, 1], down[:, 0] = g["L0_ffn_sw1"], g["L0_ffn_sw3"], g["L0_ffn_sw2"]
    up[:, 1:, 0] = g["L0_ffn_w1"].transpose(1, 0, 2)
    up[:, 1:, 1] = g["L0_ffn_w3"].transpose(1, 0, 2)
    down[:, 1:] = g["L0_ffn_w2"].transpose(1, 0, 2)
    out["up"], out["down"] = up.reshape(P, -1), down.reshape(P, -1)
    router = np.zeros((P, P), f)
    router[:, :NE] = g["L0_ffn_router_w"]
    out["router"] = router
    out["ebias"] = np.tile(g["L0_ffn_expert_bias"][None, :], (P, 1))
    kr = g["L0_attn_W_KR"]
    swap = [1, 0, 3, 2]
    wc = np.zeros((P, 2, P), f)
    for i in range(3):
        wc[:, 0, DL * i:DL * i + DL] = g["L0_attn_W_DQ"]
        wc[:, 1, DL * i:DL * i + DL] = g["L0_attn_W_DKV"]
    for r in (3 * DL, 3 * DL + 8):
        wc[:, 1, r:r + 4] = kr
        wc[:, 1, r + 4:r + 8] = kr[:, swap]
    out["latent"] = wc.reshape(P, -1)
    uq = g["L0_attn_W_UQ"].reshape(DL, NH, DH)
    qr = g["L0_attn_W_QR"].reshape(DL, NH, DR)
    uk = g["L0_attn_W_UK"].reshape(DL, NH, DH)
    wq = np.zeros((P, NPAIR, 2, 4, 16), f)
    wk = np.zeros((P, NPAIR, 2, 4, 16), f)
    wv = np.zeros((P, P), f)
    wr = np.zeros((P, P), f)
    for i in range(3):
        r = slice(DL * i, DL * i + DL)
        wv[r] = g["L0_attn_W_UV"]
        wr[r, :P // 2] = qr.reshape(DL, NH * DR)
        wr[r, P // 2:] = qr[:, :, swap].reshape(DL, NH * DR)
        for h in range(NH):
            for blk in range(3):
                wq[r, h // 2, h % 2, blk, 0:8] = uq[:, h]
                wk[r, h // 2, h % 2, blk, 0:8] = uk[:, h]
    for r in range(16):
        wk[3 * DL + r, :, :, 0:3, 8 + r % 4] = 1.0
    out["pairs"] = np.concatenate([wq.reshape(P, -1), wk.reshape(P, -1), wv, wr], axis=1)
    out["wo"] = g["L0_attn_W_O"]
    win = g["L1_ffn_W_in"].reshape(TREES, 255, P)
    b = g["L1_ffn_b_in"].reshape(TREES, 255)
    wout = g["L1_ffn_W_out"].reshape(P, TREES, 255)
    tin = np.zeros((P, TREES, 2, P), f)
    tout = np.zeros((P, TREES, 2, P), f)
    tb = np.zeros((P, TREES, 2), f)
    for c, (a, n) in enumerate(((0, 127), (127, 128))):
        tin[:, :, c, :n] = win[:, a:a + n].transpose(2, 0, 1)
        tout[:n, :, c, :] = wout[:, :, a:a + n].transpose(2, 1, 0)
        tb[:n, :, c] = b[:, a:a + n].T
    out["tin"], out["tout"], out["tb"] = tin.reshape(P, -1), tout.reshape(P, -1), tb.reshape(P, -1)
    mw = np.zeros((P, 10, P), f)
    mw[:, 0] = g["L1_attn_value_W"].T
    mw[:, 1:] = g["L1_attn_gate_W"].reshape(9, P, P).transpose(2, 0, 1)
    out["mixw"] = mw.reshape(P, -1)
    out["gb"] = np.tile(np.concatenate([g["L1_attn_gamma"], g["L1_attn_beta"]])[None, :], (P, 1))
    for name, a in shape_constants():
        out[name] = a
    return {k: np.ascontiguousarray(v) for k, v in out.items()}


def macaron(nc, d, out):
    n_phases = len(PHASES)
    with ExitStack() as ctx:
        def sb(name, shape, dt=F32):
            return ctx.enter_context(nc.sbuf_tensor(name, shape, dt))

        def sem(name):
            return ctx.enter_context(nc.semaphore(name))

        X = sb("X", [P, NB * TT, P])
        xhi = sb("xhi", [P, NB * L], F32R)
        xlo = sb("xlo", [P, NB * L], F32R)
        xn = sb("xn", [P, TT, P])
        stats = sb("stats", [P, TT, 6])
        mv = sb("mv", [P, TT, 2])
        veps = sb("veps", [P, TT])
        rstd = sb("rstd", [P, TT])
        mhalf = sb("mhalf", [P, TT])
        yT = sb("yT", [P, L])

        UP_A, UP_B = slice(0, 4 * P), slice(4 * P, NX * 2 * P)
        ident = sb("ident_s", [P, P])
        before = sb("before_s", [P, NE, NE])
        target = sb("target_s", [P, 2])
        rope_k = sb("rope_k_s", [P, L])
        rope_q = sb("rope_q_s", [P, L])
        low = sb("low_s", [P, 5])
        tri = sb("tri_s", [P, 2, 2 * P])
        ebias = sb("ebias_s", [P, NE])
        gb = sb("gb_s", [P, 2, P])
        tb = sb("tb_s", [P, NCH])
        down = sb("down_s", [P, NX, P])
        wo = sb("wo_s", [P, P])
        up_hi = sb("up_hi", [P, NX * 2, P], F32R)
        up_lo = sb("up_lo", [P, NX * 2, P], F32R)
        router_raw = sb("router_raw", [P, P])
        router_hi = sb("router_hi", [P, P], F32R)
        router_lo = sb("router_lo", [P, P], F32R)
        sel = sb("sel_s", [P, NE, P], F32R)
        lat_hi = sb("lat_hi", [P, 2, P], F32R)
        lat_lo = sb("lat_lo", [P, 2, P], F32R)
        pair_w = sb("pair_w", [P, 18, P], F32R)
        tin = sb("tin_s", [P, 2, NCH * P], F32R)
        tin_hi, tin_lo = (tin[:, i, :].rearrange("p (a b) -> p a b", a=NCH) for i in range(2))
        CQ, CK = tin[:, 0, :], tin[:, 1, :]
        pair_tmp = tin[:].rearrange("p a b -> p (a b)")[:, 0:18 * P]
        path = sb("path_s", [P, 2, P], BF16)
        mix_w = sb("mix_w", [P, 20 * P], F32R)
        mix_hi = mix_w[:, 0:10 * P].rearrange("p (a b) -> p a b", a=10)
        mix_lo = mix_w[:, 10 * P:20 * P].rearrange("p (a b) -> p a b", a=10)
        rot_hi, rot_lo = mix_w[:, 0:2 * L], mix_w[:, 2 * L:4 * L]
        rot_sel = sb("rot_sel_s", [P, NPAIR, P], F32R)

        work = sb("work", [P, 20 * L])
        pb = work[:].rearrange("p (a w) -> p a w", a=4)

        def rows(at, n):
            return work[:, at * L:(at + n) * L].rearrange("p (a l) -> p a l", a=n)

        act_s = rows(0, 4)
        h_s = rows(4, 4)
        prod_v, prod_v2, prod_p = rows(4, 3), rows(11, 2), rows(7, 3)
        raw = work[:, 8 * L:8 * L + 20 * P]
        sel_raw = work[:, 13 * L:15 * L]
        path_raw = work[:, 15 * L:15 * L + 2 * P]
        rot_raw = work[:, 16 * L:18 * L]
        tout = work[:, 16 * L:20 * L].rearrange("p (a b) -> p a b", a=NCH)
        lgT = sb("lgT", [P, L])
        rt = sb("rt", [P, 8, TT, NE])
        rcmp = sb("rcmp", [P, 2, TT, NE, NE])
        rsum = sb("rsum", [P, 4, TT])
        ghl = sb("ghl", [P, TT, P])
        g_hi = sb("g_hi", [P, TT, NE], F32R)
        gT = sb("gT", [P, NB * L], F32R)
        dec = sb("dec", [P, 2, L], BF16)
        ck_x = sb("ck_x", [P, L])
        c_hi = sb("c_hi", [P, L], F32R)
        ck_now = sb("ck_now", [P, L], F32R)
        v_aug = sb("v_aug", [P, TT, NH, 32])
        q_hi = sb("q_hi", [P, L], F32R)
        k_hi = sb("k_hi", [P, L], F32R)
        QS = sb("QS", [P, 2, L], F32R)
        KS = sb("KS", [P, 2, 2, L], F32R)
        avT = sb("avT", [P, L])
        rden = sb("rden", [P, TT, 4])
        att = sb("att", [P, TT, NH, DH])
        attT = yT
        tout_hi = pair_w[:, 0:NCH, :]
        tout_lo = KS[:].rearrange("p a b l -> p (a b l)").rearrange("p (a b) -> p a b", a=NCH)
        rot_rows = rot_sel[:].rearrange("p a b -> p (a b)")
        node_hi = (QS[:, 0, :], QS[:, 1, :], q_hi[:], k_hi[:])
        node_lo = (rot_rows[:, 0:L], rot_rows[:, L:2 * L], c_hi[:], ck_now[:])
        vpad = v_aug[:].rearrange("p t h e -> p (t h e)")[:, 0:L + 2 * PADV]
        ln2 = ck_x[:].rearrange("p (c d) -> p c d", c=TT)

        bank = ctx.enter_context(nc.psum_tensor("bank", [P, 8, L], F32))
        psO, psT, psR, psG = 4, 5, 6, 7
        psQ, psK, psH = psT, psG, psO

        s_x = [sem(f"x_loaded_{b}") for b in range(NB)]
        s_const = sem("consts_loaded")
        s_up = [sem("first_up_loaded"), sem("up_loaded")]
        s_moe = sem("moe_consts_loaded")
        s_down = sem("down_loaded")
        s_tout = sem("tout_loaded")
        s_pairs = sem("pairs_loaded")
        s_raw = {k: sem(k + "_raw_loaded") for k in ("latent", "tin", "mixw")}
        s_late = sem("late_consts_loaded")
        LATE = 16 * 10
        s_out = sem("out_stored")
        x_new = sem("x_new")
        ln_stat, ln_agg, ln_eps, ln_rstd, ln_xn = (sem("ln_" + k) for k in ("stat", "agg", "eps", "rstd", "xn"))
        xn_ps, x_hi_ready, x_lo_ready = sem("xn_transposed"), sem("x_hi_ready"), sem("x_lo_ready")
        y_sb, y_ps = sem("y_in_sbuf"), sem("y_token_major")
        w_hi = {k: sem(k + "_hi_ready") for k in ("up", "pairs")}
        w_ready = {k: sem(k + "_split") for k in ("up", "router", "sel", "latent", "pairs", "tin", "mixw", "path", "rot", "tout")}
        setup_v, setup_p = sem("vector_setup"), sem("pool_setup")
        S = {}
        for ph in PHASES:
            kind = ph[:-1] if ph[-1].isdigit() else ph
            names = {
                "moe": ("gate_ps", "up_ps", "bc_ps", "silu", "sg", "h", "down", "lg_ps", "lg_sb", "lgt_ps",
                        "r_exp_in", "r_exp", "r_chain", "ghl", "ghl_ps", "gT"),
                "attn": ("lat_ps", "ck_x", "c_hi", "c_done", "rot_ps", "rot_x", "rot_hi", "rot", "ck_now", "v_ps", "v_sb",
                         "qp_ps", "qhi", "qs", "kp_ps", "khi", "ks", "scores", "exp", "clip", "masked", "av", "avT",
                         "avt_ps", "rden", "att", "att_ps", "attT"),
                "tree": ("logit_ps", "silu", "dec", "cnt", "mask", "h_hi", "h_lo", "outp"),
                "mix": ("v_ps", "v_sb", "v_wrap", "gate_ps", "gate", "prod_v", "pair_v", "prod_p", "summed",
                        "l_stat", "l_agg", "l_eps", "l_rstd", "l_g"),
            }[kind]
            S[ph] = {n: sem(f"{ph}_{n}") for n in names}

        def phases():
            for p, name in enumerate(PHASES[:n_phases]):
                yield p, name

        def wait_apart(eng, s, value):
            eng.wait_ge(s, value)
            eng.nop(nofuse=True)

        def over_batches(eng, p, body):
            more = p < n_phases - 1
            body(0, False, True)
            with eng.Fori(1, NB - 1) as b:
                body(b, False, more)
            body(NB - 1, True, more)

        def summed(p, b):
            q = p - 1 if isinstance(b, int) and b == 0 else p
            if q < 0 or (q != p and PHASES[q] == "attn"):
                return None
            return "mix" if PHASES[q] == "mix" else "y"

        def after_mix(p, b):
            return p > 0 and PHASES[p - 1] == "mix" and isinstance(b, int) and b == 0

        def at_least(value):
            return max(value, 0) if isinstance(value, int) else value

        A = PHASES.index("attn")

        def before_of(b):
            return (b + NB - 1) % NB

        block = ctx.enter_context(nc.Block())

        @block.sync
        def _(sp):
            def load_x(b):
                sp.dma_start(X[:, TT * b:TT * (b + 1), :], d["x"][b].rearrange("(c p) d -> p c d", p=P)).then_inc(s_x[b], 16)

            load_x(0)
            sp.dma_start(ident[:], d["ident"]).then_inc(s_const, 16)
            sp.dma_start(router_raw[:], d["router"]).then_inc(s_moe, 16)
            sp.dma_start(raw[:, UP_A], d["up"][:, UP_A]).then_inc(s_up[0], 16)
            load_x(1)
            sp.dma_start(before[:].rearrange("p a b -> p (a b)"), d["before"]).then_inc(s_moe, 16)
            sp.dma_start(ebias[:], d["ebias"]).then_inc(s_moe, 16)
            sp.dma_start(sel_raw, d["sel"]).then_inc(s_moe, 16)
            sp.dma_start(raw[:, UP_B], d["up"][:, UP_B]).then_inc(s_up[1], 16)
            sp.dma_start(down[:].rearrange("p a b -> p (a b)"), d["down"]).then_inc(s_down, 16)
            load_x(2)
            load_x(3)
            for t, name in ((low, "low"), (rope_k, "rope_k"), (rope_q, "rope_q"), (target, "target"), (tb, "tb"), (wo, "wo")):
                sp.dma_start(t[:], d[name]).then_inc(s_late, 16)
            for t, name in ((tri, "tri"), (gb, "gb")):
                sp.dma_start(t[:].rearrange("p a b -> p (a b)"), d[name]).then_inc(s_late, 16)
            sp.dma_start(rot_raw, d["rot_sel"]).then_inc(s_late, 16)
            sp.dma_start(path_raw, d["path"]).then_inc(s_late, 16)
            sp.wait_ge(w_ready["up"], 2)
            sp.dma_start(raw[:, 0:2 * P], d["latent"]).then_inc(s_raw["latent"], 16)
            sp.dma_start(raw[:, 2 * P:20 * P], d["pairs"]).then_inc(s_pairs, 16)
            if n_phases > 2:
                sp.wait_ge(x_new, 2 * NB)
                sp.dma_start(tout.rearrange("p a b -> p (a b)"), d["tout"]).then_inc(s_tout, 16)
                sp.dma_start(raw[:, 0:NCH * P], d["tin"]).then_inc(s_raw["tin"], 16)
                sp.wait_ge(w_ready["tin"], 1)
                sp.dma_start(raw[:, 0:10 * P], d["mixw"]).then_inc(s_raw["mixw"], 16)
            base = NB * (n_phases - 1)
            for b in range(NB):
                sp.wait_ge(x_new, base + b + 1)
                sp.dma_start(out[b].rearrange("(c p) d -> p c d", p=P), X[:, TT * b:TT * (b + 1), :]).then_inc(s_out, 16)
            sp.wait_ge(s_out, 16 * NB)

        @block.gpsimd
        def _(pool):
            def rstd_of(n):
                pool.wait_ge(ln_eps, n + 1)
                nc.gpsimd.tensor_tensor(rstd[:], veps[:], mhalf[:], ALU.pow).then_inc(ln_rstd, 1)

            nc.gpsimd.memset(mhalf[:], -0.5).then_inc(setup_p, 1)
            nc.gpsimd.memset(ghl[:], 0.0).then_inc(setup_p, 1)
            nc.gpsimd.memset(v_aug[:], 0.0).then_inc(setup_p, 1)
            pool.wait_ge(setup_p, 3)
            nc.gpsimd.memset(v_aug[:, :, :, DH:DH + 1], 1.0).then_inc(setup_p, 1)
            rstd_of(0)
            rstd_of(1)
            nc.gpsimd.memset(KS[:].bitcast(F32), 0.0).then_inc(setup_p, 1)

            def split(hi, lo, src, ready):
                nc.gpsimd.tensor_copy(hi, src).then_inc(ready[0], 1)
                pool.wait_ge(ready[0], ready[1])
                nc.gpsimd.tensor_tensor(lo, src, hi.bitcast(F32), ALU.subtract).then_inc(ready[2], 1)

            rstd_of(2)
            pool_hi = setup_p
            count = [5]

            def split_weights(name, hi, lo, src):
                count[0] += 1
                split(hi, lo, src, (pool_hi, count[0], w_ready[name]))

            for p, ph in phases():
                s = S[ph]
                if ph == "moe0":
                    rstd_of(NB * (p + 1) - 1)
                    pool.wait_ge(s_raw["latent"], 16)
                    split_weights("latent", lat_hi[:], lat_lo[:], raw[:, 0:2 * P].rearrange("p (a b) -> p a b", a=2))
                    pool.wait_ge(s_pairs, 16)
                    nc.gpsimd.tensor_copy(pair_tmp, raw[:, 2 * P:20 * P]).then_inc(w_hi["pairs"], 1)
                    pool.wait_ge(s_late, LATE)
                    nc.gpsimd.tensor_copy(path[:].rearrange("p a b -> p (a b)"), path_raw).then_inc(w_ready["path"], 1)
                    nc.gpsimd.tensor_copy(rot_sel[:].rearrange("p a b -> p (a b)"), rot_raw).then_inc(w_ready["rot"], 1)
                    if p < n_phases - 1:
                        with pool.Fori(1, NB) as b:
                            rstd_of(NB * (p + 1) + b - 1)
                elif ph == "attn":
                    def body(b, last, renorm):
                        for pr in range(NPAIR):
                            t = pb[:, pr % 4, :]
                            for g, (at, w) in enumerate(((0, P), (2 * L, 2 * P), (4 * L, P))):
                                if pr == 5 and g == 2 and renorm:
                                    rstd_of(NB * (p + 1) + b - 1)
                                pool.wait_ge(s["clip"], 3 * (NPAIR * b + pr) + g + 1)
                                v = t[:, at:at + 2 * (L if g < 2 else L // 2)].rearrange("p (j l) -> p j l", j=2)[:, :, 0:w]
                                nc.gpsimd.tensor_tensor(v, v, tri[:, :, 0:w], ALU.mult).then_inc(s["masked"], 1)
                    over_batches(pool, p, body)
                elif ph == "mix":
                    def mixture_rstd(b):
                        if isinstance(b, int) and b == 0:
                            return
                        pool.wait_ge(S["mix"]["l_eps"], b)
                        nc.gpsimd.tensor_tensor(rstd[:], veps[:], mhalf[:], ALU.pow).then_inc(S["mix"]["l_rstd"], 1)

                    def body(b, last, renorm):
                        pool.wait_ge(s["v_wrap"], b + 1)
                        for i, g in enumerate((2, 5, 8)):
                            if i == 1:
                                mixture_rstd(b)
                            pool.wait_ge(s["gate"], 9 * b + g + 1)
                            pool.wait_ge(s["summed"], at_least(6 * b + 2 * i - 4))
                            sh = PADV + SHIFTS[g]
                            nc.gpsimd.tensor_tensor(prod_p[:, i, :], act_s[:, g % 3, :], vpad[:, sh:sh + L], ALU.mult).then_inc(s["prod_p"], 1)
                        if renorm:
                            rstd_of(NB * (p + 1) + b - 1)
                    over_batches(pool, p, body)
                else:
                    if ph.startswith("tree"):
                        def body(b, last, renorm):
                            for t in range(TREES):
                                if t == 1 and after_mix(p, b):
                                    mixture_rstd(NB)
                                if t == (1 if isinstance(b, int) and b == 0 and not after_mix(p, b) else 3):
                                    if renorm:
                                        rstd_of(NB * (p + 1) + b - 1)
                                for i in (2 * t, 2 * t + 1):
                                    pool.wait_ge(s["h_hi"], NCH * b + i + 1)
                                    pool.wait_ge(s["outp"], at_least(NCH * b + i - 3))
                                    nc.gpsimd.tensor_tensor(node_lo[i % 4], h_s[:, i % 4, :], node_hi[i % 4].bitcast(F32),
                                                            ALU.subtract).then_inc(s["h_lo"], 1)
                        over_batches(pool, p, body)
                        continue
                    rstd_of(NB * (p + 1) - 1)
                    if ph == "moe1":
                        pool.wait_ge(s_raw["tin"], 16)
                        split_weights("tin", tin_hi[:], tin_lo[:], raw[:, 0:NCH * P].rearrange("p (a b) -> p a b", a=NCH))
                        pool.wait_ge(s_tout, 16)
                        split_weights("tout", tout_hi, tout_lo, tout)
                        if p < n_phases - 1:
                            rstd_of(NB * (p + 1))
                        pool.wait_ge(s_raw["mixw"], 16)
                        split_weights("mixw", mix_hi[:], mix_lo[:], raw[:, 0:10 * P].rearrange("p (a b) -> p a b", a=10))
                        if p < n_phases - 1:
                            with pool.Fori(2, NB) as b:
                                rstd_of(NB * (p + 1) + b - 1)

        @block.scalar
        def _(act):
            def copy(dst, src, **kw):
                return nc.scalar.activation(dst, src, ACT.Copy, **kw)

            def x_high(n, b, bk=psT):
                act.wait_ge(xn_ps, n + 1)
                copy(xhi[:, bass.ds(b * L, L)], bank[:, bk, :]).then_inc(x_hi_ready, 1)

            def y_copy(n, done, count, bk=psO, scale=0.5):
                act.wait_ge(done, count)
                act.wait_ge(y_ps, n - NB)
                copy(yT[:], bank[:, bk, :], scale=scale).then_inc(y_sb, 1)

            def tail_copy(p, b):
                first = isinstance(b, int) and b == 0
                q = PHASES[p - 1] if first else PHASES[p]
                if (first and p == 0) or q == "attn":
                    return
                if q == "mix":
                    y_copy(NB * (p + 1) + b - 1, S[q]["summed"], 6 * (NB if first else b), psG, 1.0)
                    return
                done, per = (S[q]["down"], NX) if q.startswith("moe") else (S[q]["outp"], NCH)
                y_copy(NB * (p + 1) + b - 1, done, per * (NB if first else b))

            def up_high(k, cols):
                act.wait_ge(s_up[k], 16)
                copy(up_hi[:].rearrange("p a b -> p (a b)")[:, cols], raw[:, cols]).then_inc(w_hi["up"], 1)

            def router_logits(sM, b, bk=psR):
                act.wait_ge(sM["lg_ps"], b + 1)
                copy(lgT[:], bank[:, bk, :]).then_inc(sM["lg_sb"], 1)

            def router_exp(sM, b, bk=psR):
                act.wait_ge(sM["r_exp_in"], b + 1)
                nc.scalar.activation(rt[:, 2], rt[:, 1], ACT.Exp).then_inc(sM["r_exp"], 1)

            def weights_T(sM, b, bk=psR):
                act.wait_ge(sM["ghl_ps"], b + 1)
                copy(gT[:, bass.ds(b * L, L)], bank[:, bk, :]).then_inc(sM["gT"], 1)

            def latent_high(b, k, bk=psH):
                act.wait_ge(S["attn"]["lat_ps"] if k == 0 else S["attn"]["ck_x"], 2 * b + 1 if k == 0 else b + 1)
                act.wait_ge(S["attn"]["c_done"], 2 * b + k)
                copy(c_hi[:], bank[:, bk, :] if k == 0 else ck_x[:]).then_inc(S["attn"]["c_hi"], 1)

            def rot_high(b):
                act.wait_ge(S["attn"]["rot_x"], b + 1)
                copy(rot_hi[:, bass.ds((b % 2) * L, L)], ck_x[:]).then_inc(S["attn"]["rot_hi"], 1)

            def queries_high(i, bk):
                act.wait_ge(S["attn"]["qp_ps"], i + 1)
                act.wait_ge(S["attn"]["qs"], i)
                copy(q_hi[:], bank[:, bk, :]).then_inc(S["attn"]["qhi"], 1)

            def keys_high(i, bk):
                act.wait_ge(S["attn"]["kp_ps"], i + 1)
                act.wait_ge(S["attn"]["ks"], i)
                copy(k_hi[:], bank[:, bk, :]).then_inc(S["attn"]["khi"], 1)

            for p, ph in phases():
                s = S[ph]
                n0 = NB * (p + 1)
                if ph.startswith("moe"):
                    ahead = p + 1 == A and p < n_phases - 1

                    def body(b, last, renorm):
                        first = isinstance(b, int) and b == 0
                        tail_copy(p, b)
                        for i in range(NX):
                            act.wait_ge(s["gate_ps"], NX * b + i + 1)
                            act.wait_ge(s["h"], NX * b + max(i - 1, 0))
                            nc.scalar.activation(act_s[:, i % 2, :], bank[:, i % 2, :], ACT.Silu).then_inc(s["silu"], 1)
                            if first and i == 0:
                                if p == 0:
                                    weights_T(s, 0)
                                    up_high(1, UP_B)
                            if first and i in (1, 3) and p == 0:
                                x_high((i + 1) // 2, (i + 1) // 2)
                            if i == 5 and renorm:
                                x_high(n0 + b - 1, before_of(b))
                            if not last:
                                if i == 2:
                                    router_logits(s, b + 1)
                                if i == 4:
                                    router_exp(s, b + 1)
                                if i == 8:
                                    weights_T(s, b + 1)
                            elif ahead:
                                if i in (1, 2):
                                    latent_high(0, i - 1, psR)
                                if i == 3:
                                    rot_high(0)
                                if i == 5:
                                    queries_high(0, psR)
                                if i == 6:
                                    keys_high(0, psR)
                    if p == 0:
                        x_high(0, 0)
                        up_high(0, UP_A)
                        router_logits(s, 0)
                        router_exp(s, 0)
                    over_batches(act, p, body)
                elif ph == "attn":
                    def av_copy(i):
                        act.wait_ge(s["av"], i + 1)
                        act.wait_ge(s["avt_ps"], i)
                        copy(avT[:], bank[:, psR, :]).then_inc(s["avT"], 1)

                    def att_copy(b):
                        act.wait_ge(s["att_ps"], b + 1)
                        copy(attT[:], bank[:, psH, :]).then_inc(s["attT"], 1)

                    def exp(b, pr, ks):
                        act.wait_ge(s["av"], at_least(4 * b + pr // 2 - 1))
                        for k in ks:
                            act.wait_ge(s["scores"], 5 * (NPAIR * b + pr) + k + 1)
                            nc.scalar.activation(pb[:, pr % 4, k * L:(k + 1) * L], bank[:, (5 * pr + k) % 4, :], ACT.Exp,
                                                 scale=QK_SCALE).then_inc(s["exp"], 1)

                    def body(b, last, renorm):
                        first = isinstance(b, int) and b == 0
                        for pr in range(NPAIR):
                            nxt = not (last and pr == NPAIR - 1)
                            if nxt:
                                queries_high(NPAIR * b + pr + 1, psQ)
                            exp(b, pr, (0, 1))
                            if pr == 3 and not first:
                                att_copy(b - 1)
                            if nxt:
                                keys_high(NPAIR * b + pr + 1, psK)
                            exp(b, pr, (2, 3, 4))
                            if pr == 2 and not last:
                                latent_high(b + 1, 0)
                            if pr == 3 and not last:
                                latent_high(b + 1, 1)
                            if pr == 4 and not last:
                                rot_high(b + 1)
                            if last and p < n_phases - 1:
                                if pr == 2:
                                    router_logits(S["moe1"], 0, psH)
                                if pr == 3:
                                    router_exp(S["moe1"], 0)
                                if pr == 7:
                                    weights_T(S["moe1"], 0, psH)
                            if pr == 7 and renorm:
                                x_high(n0 + b - 1, before_of(b), psH)
                            if pr == 1:
                                act.wait_ge(s["v_ps"], b + 1)
                                act.wait_ge(s["av"], 4 * b)
                                copy(v_aug[:, :, :, 0:DH], bank[:, psH, :].rearrange("p (t h e) -> p t h e", t=TT, h=NH)).then_inc(s["v_sb"], 1)
                            if pr % 2 == 1 and not (first and pr == 1):
                                av_copy(4 * b + (pr - 1) // 2 - 1)
                    tail_copy(p, 0)
                    for w in ("path", "rot", "sel", "latent", "pairs"):
                        act.wait_ge(w_ready[w], 1)
                    over_batches(act, p, body)
                    av_copy(4 * NB - 1)
                    att_copy(NB - 1)
                elif ph.startswith("tree"):
                    def body(b, last, renorm):
                        first = isinstance(b, int) and b == 0
                        if first:
                            tail_copy(p, b)
                        for i in range(NCH):
                            act.wait_ge(s["logit_ps"], NCH * b + i + 1)
                            act.wait_ge(s["mask"], at_least(NCH * b + i - 3))
                            nc.scalar.activation(act_s[:, i % 4, :], bank[:, i % 4, :], ACT.Silu,
                                                 bias=tb[:, i:i + 1]).then_inc(s["silu"], 1)
                            if i > 1:
                                node_high(b, i - 2)
                            elif not first:
                                node_high(b - 1, NCH - 2 + i)
                            if i == 0 and after_mix(p, b):
                                x_high(n0 - 2, NB - 2)
                            if i == 3 and not first:
                                tail_copy(p, b)
                            if i == 11 and renorm:
                                x_high(n0 + b - 1, before_of(b))

                    def node_high(b, i):
                        act.wait_ge(s["mask"], NCH * b + i + 1)
                        act.wait_ge(s["outp"], at_least(NCH * b + i - 3))
                        act.wait_ge(s["h_lo"], at_least(NCH * b + i - 3))
                        copy(node_hi[i % 4], h_s[:, i % 4, :]).then_inc(s["h_hi"], 1)

                    act.wait_ge(s_late, LATE)
                    over_batches(act, p, body)
                    for i in (NCH - 2, NCH - 1):
                        node_high(NB - 1, i)
                elif ph == "mix":
                    def body(b, last, renorm):
                        first = isinstance(b, int) and b == 0
                        if first:
                            tail_copy(p, b)
                        act.wait_ge(s["v_ps"], b + 1)
                        act.wait_ge(s["prod_v"], 6 * b)
                        act.wait_ge(s["prod_p"], 3 * b)
                        copy(vpad[:, PADV:PADV + L], bank[:, psO, :]).then_inc(s["v_sb"], 1)
                        act.wait_ge(s["v_sb"], b + 1)
                        copy(vpad[:, 0:PADV], vpad[:, L:L + PADV])
                        copy(vpad[:, L + PADV:], vpad[:, PADV:2 * PADV]).then_inc(s["v_wrap"], 1)
                        for g in range(9):
                            act.wait_ge(s["gate_ps"], 9 * b + g + 1)
                            if g >= 3:
                                if g % 3 == 2:
                                    act.wait_ge(s["prod_p"], 3 * b + (g - 3) // 3 + 1)
                                else:
                                    act.wait_ge(s["prod_v"], 6 * b + 2 * ((g - 3) // 3) + (g - 3) % 3 + 1)
                            else:
                                act.wait_ge(s["prod_p"], 3 * b)
                                act.wait_ge(s["prod_v"], 6 * b)
                            nc.scalar.activation(act_s[:, g % 3, :], bank[:, g % 3, :], ACT.Sigmoid).then_inc(s["gate"], 1)
                            if g == 2 and not first:
                                tail_copy(p, b)
                            if g == 3 and not first:
                                x_high(n0 + b - 2, before_of(b + NB - 1))
                    over_batches(act, p, body)
                    act.wait_ge(s["prod_v"], 6 * NB)
                    act.wait_ge(s["prod_p"], 3 * NB)
            if PHASES[n_phases - 1] not in ("attn", "mix"):
                last = S[PHASES[n_phases - 1]]
                done, count = (last["down"], NX * NB) if "down" in last else (last["outp"], NCH * NB)
                y_copy(NB * (n_phases + 1) - 1, done, count)

        @block.vector
        def _(dve):
            V = nc.vector

            def normalise(n, b):
                for c in range(TT):
                    i = V.bn_stats(stats[:, c, :], X[:, bass.ds(b * TT + c, 1), :])
                i.then_inc(ln_stat, 1)
                wait_apart(dve, ln_stat, n + 1)
                for c in range(TT):
                    i = V.bn_aggr(mv[:, c, :], stats[:, c, :])
                i.then_inc(ln_agg, 1)
                dve.wait_ge(ln_agg, n + 1)
                V.tensor_scalar(veps[:], mv[:, :, 1], EPS, None, ALU.add).then_inc(ln_eps, 1)

            def normalised(n, b):
                dve.wait_ge(ln_rstd, n + 1)
                dve.wait_ge(xn_ps, n)
                for c in range(TT):
                    i = V.tensor_scalar(xn[:, c, :].rearrange("p (o d) -> p o d", o=1), X[:, bass.ds(b * TT + c, 1), :], mv[:, c, 0:1], rstd[:, c:c + 1],
                                        ALU.subtract, ALU.mult)
                i.then_inc(ln_xn, 1)

            def x_low(n, b, bk=psT):
                dve.wait_ge(x_hi_ready, n + 1)
                V.tensor_tensor(xlo[:, bass.ds(b * L, L)], bank[:, bk, :], xhi[:, bass.ds(b * L, L)].bitcast(F32),
                                ALU.subtract).then_inc(x_lo_ready, 1)

            def add_y(n, b, src, done, count):
                dve.wait_ge(done, count)
                dst = X[:, bass.ds(b * TT, TT), :]
                V.tensor_tensor(dst, dst, src, ALU.add).then_inc(x_new, 1)
                wait_apart(dve, x_new, n - NB + 1)

            def tok(bk):
                return bank[:, bk, :].rearrange("p (c d) -> p c d", c=TT)

            def mixture_stats(lb):
                m = S["mix"]
                for c in range(TT):
                    i = V.bn_stats(stats[:, c, :], yT[:, c * P:(c + 1) * P])
                i.then_inc(m["l_stat"], 1)
                wait_apart(dve, m["l_stat"], lb + 1)
                for c in range(TT):
                    i = V.bn_aggr(mv[:, c, :], stats[:, c, :])
                i.then_inc(m["l_agg"], 1)
                dve.wait_ge(m["l_agg"], lb + 1)
                V.tensor_scalar(veps[:], mv[:, :, 1], EPS, None, ALU.add).then_inc(m["l_eps"], 1)

            def mixture_norm(lb):
                m = S["mix"]
                dve.wait_ge(m["l_rstd"], lb + 1)
                for c in range(TT):
                    i = V.tensor_scalar(ln2[:, c, :], yT[:, c * P:(c + 1) * P], mv[:, c, 0:1], rstd[:, c:c + 1],
                                        ALU.subtract, ALU.mult)
                i.then_inc(y_ps, 1)
                dve.wait_ge(y_ps, NB * (PHASES.index("mix")) + lb + 1)
                V.tensor_tensor(ln2[:], ln2[:], gb[:, 0, :].unsqueeze(1).to_broadcast([P, TT, P]), ALU.mult).then_inc(m["l_g"], 1)
                dve.wait_ge(m["l_g"], 2 * lb + 1)
                V.tensor_tensor(ln2[:], ln2[:], gb[:, 1, :].unsqueeze(1).to_broadcast([P, TT, P]), ALU.add).then_inc(m["l_g"], 1)
                dve.wait_ge(m["l_g"], 2 * lb + 2)

            def tail_stats(p, b):
                if summed(p, b) == "mix":
                    wait_apart(dve, y_sb, NB * sum(q != "attn" for q in PHASES[:p]) + b)
                    mixture_stats(NB - 1 if PHASES[p] != "mix" else b - 1)

            def tail_norm(p, b):
                if summed(p, b) == "mix":
                    mixture_norm(NB - 1 if PHASES[p] != "mix" else b - 1)

            def tail_add(p, b, renorm, bk=psT):
                kind = summed(p, b)
                n = NB * (p + 1) + b - 1
                if kind is None:
                    return
                if kind == "mix":
                    add_y(n, before_of(b), ln2[:], y_ps, n - NB + 1)
                else:
                    add_y(n, before_of(b), tok(bk), y_ps, n - NB + 1)
                if renorm:
                    normalise(n, before_of(b))

            def up_low(k, cols):
                dve.wait_ge(w_hi["up"], k + 1)
                V.tensor_tensor(up_lo[:].rearrange("p a b -> p (a b)")[:, cols], raw[:, cols], up_hi[:].bitcast(F32).rearrange("p a b -> p (a b)")[:, cols],
                                ALU.subtract).then_inc(w_ready["up"], 1)

            KR = 12

            def router_1(sM, b, bk):
                c = KR * b
                dve.wait_ge(sM["lgt_ps"], b + 1)
                V.tensor_copy(rt[:, 0], tok(bk)[:, :, 0:NE]).then_inc(sM["r_chain"], 1)
                dve.wait_ge(sM["r_chain"], c + 1)
                V.tensor_reduce(rsum[:, 0, :], rt[:, 0], AX.X, ALU.max).then_inc(sM["r_chain"], 1)
                dve.wait_ge(sM["r_chain"], c + 2)
                V.tensor_tensor(rt[:, 1], rt[:, 0], rsum[:, 0, :].unsqueeze(2).to_broadcast([P, TT, NE]), ALU.subtract).then_inc(sM["r_exp_in"], 1)

            def router_2(sM, b, part):
                c = KR * b + 2
                k = [(0, 4, 6)[part]]

                def step(ins):
                    ins.then_inc(sM["r_chain"], 1)
                    k[0] += 1
                    dve.wait_ge(sM["r_chain"], c + k[0])
                mine = rt[:, 4].unsqueeze(3).to_broadcast([P, TT, NE, NE])
                theirs = rt[:, 4].unsqueeze(2).to_broadcast([P, TT, NE, NE])
                if part == 0:
                    dve.wait_ge(sM["r_exp"], b + 1)
                    step(V.tensor_reduce(rsum[:, 1, :], rt[:, 2], AX.X, ALU.add))
                    step(V.reciprocal(rsum[:, 2, :], rsum[:, 1, :]))
                    step(V.tensor_tensor(rt[:, 3], rt[:, 2], rsum[:, 2, :].unsqueeze(2).to_broadcast([P, TT, NE]), ALU.mult))
                    step(V.tensor_tensor(rt[:, 4], rt[:, 3], ebias[:].unsqueeze(1).to_broadcast([P, TT, NE]), ALU.add))
                    return
                if part == 1:
                    V.tensor_tensor(rcmp[:, 0], theirs, mine, ALU.is_gt)
                    step(V.tensor_tensor(rcmp[:, 1], theirs, mine, ALU.is_equal))
                    step(V.tensor_tensor(rcmp[:, 1], rcmp[:, 1], before[:].unsqueeze(1).to_broadcast([P, TT, NE, NE]), ALU.mult))
                    return
                step(V.tensor_tensor(rcmp[:, 0], rcmp[:, 0], rcmp[:, 1], ALU.add))
                step(V.tensor_reduce(rt[:, 5], rcmp[:, 0], AX.X, ALU.add))
                step(V.scalar_tensor_tensor(rt[:, 6], rt[:, 5], 2.0, rt[:, 3], ALU.is_lt, ALU.mult))
                step(V.tensor_copy(g_hi[:], rt[:, 6]))
                assert k[0] + 2 == KR
                dve.wait_ge(sM["ghl_ps"], b)
                V.tensor_copy(ghl[:, :, 0:NE], g_hi[:].bitcast(F32))
                V.tensor_tensor(ghl[:, :, NE:2 * NE], rt[:, 6], g_hi[:].bitcast(F32), ALU.subtract).then_inc(sM["ghl"], 1)

            def latent(b, k, bk=psH):
                dst = bass.ds(b * L, L)
                if k == 0:
                    dve.wait_ge(S["attn"]["c_hi"], 2 * b + 1)
                    V.scalar_tensor_tensor(CQ[:, dst], c_hi[:].bitcast(F32), low[:, 0:1], bank[:, bk, :], ALU.mult, ALU.add).then_inc(S["attn"]["c_done"], 1)
                    return
                dve.wait_ge(S["attn"]["lat_ps"], 2 * b + 2)
                V.tensor_tensor(ck_x[:], bank[:, bk, :], rope_k[:], ALU.mult).then_inc(S["attn"]["ck_x"], 1)
                dve.wait_ge(S["attn"]["c_hi"], 2 * b + 2)
                V.scalar_tensor_tensor(CK[:, dst], c_hi[:].bitcast(F32), low[:, 1:2], ck_x[:], ALU.mult, ALU.add).then_inc(S["attn"]["c_done"], 1)

            def rotated(b, bk=psH):
                dve.wait_ge(S["attn"]["rot_ps"], b + 1)
                dve.wait_ge(S["attn"]["c_done"], 2 * b + 2)
                V.tensor_tensor(ck_x[:], bank[:, bk, :], rope_q[:], ALU.mult).then_inc(S["attn"]["rot_x"], 1)
                dve.wait_ge(S["attn"]["rot_hi"], b + 1)
                dst = bass.ds((b % 2) * L, L)
                V.tensor_tensor(rot_lo[:, dst], ck_x[:], rot_hi[:, dst].bitcast(F32), ALU.subtract).then_inc(S["attn"]["rot"], 1)

            def latent_now(b):
                dve.wait_ge(S["attn"]["c_done"], 2 * b + 2)
                wait_apart(dve, S["attn"]["v_ps"], b)
                V.tensor_copy(ck_now[:], CK[:, bass.ds(b * L, L)].bitcast(F32)).then_inc(S["attn"]["ck_now"], 1)

            def queries(i, par, bk):
                dve.wait_ge(S["attn"]["qhi"], i + 1)
                dve.wait_ge(S["attn"]["scores"], at_least(5 * (i - 1)))
                V.scalar_tensor_tensor(QS[:, par, :], q_hi[:].bitcast(F32), low[:, 3:4], bank[:, bk, :], ALU.mult, ALU.add).then_inc(S["attn"]["qs"], 1)

            def keys(i, par, bk):
                dve.wait_ge(S["attn"]["khi"], i + 1)
                dve.wait_ge(S["attn"]["scores"], at_least(5 * (i - 1)))
                for j in range(2):
                    r = slice(64 * j, 64 * j + 64)
                    ins = V.scalar_tensor_tensor(KS[r, par, j, :], k_hi[r].bitcast(F32), low[r, 4:5], bank[r, bk, :], ALU.mult, ALU.add)
                ins.then_inc(S["attn"]["ks"], 1)

            for p, ph in phases():
                s = S[ph]
                n0 = NB * (p + 1)

                if ph.startswith("moe"):
                    ahead = p + 1 == A and p < n_phases - 1

                    def body(b, last, renorm):
                        first = isinstance(b, int) and b == 0
                        for i in range(NX):
                            if first and p == 0:
                                if i == 1:
                                    normalised(1, 1)
                                    up_low(1, UP_B)
                                if i == 2:
                                    x_low(1, 1)
                                if i == 3:
                                    normalised(2, 2)
                                if i in (2, 3):
                                    dve.wait_ge(s_x[i], 16)
                                    normalise(i, i)
                            if i == 2:
                                tail_add(p, b, renorm)
                            if first and p == 0 and i == 4:
                                x_low(2, 2)
                            if i == 4 and renorm:
                                normalised(n0 + b - 1, before_of(b))
                            if i == 6 and renorm:
                                x_low(n0 + b - 1, before_of(b))
                            if not last:
                                if i == 4:
                                    router_1(s, b + 1, psR)
                                if i in (5, 6, 7):
                                    router_2(s, b + 1, i - 5)
                            elif ahead:
                                if i == 1:
                                    dve.wait_ge(s_late, LATE)
                                    dve.wait_ge(w_hi["pairs"], 1)
                                    V.scalar_tensor_tensor(pair_w[:].rearrange("p a b -> p (a b)"), pair_tmp.bitcast(F32), low[:, 2:3],
                                                           raw[:, 2 * P:20 * P], ALU.mult, ALU.add).then_inc(w_ready["pairs"], 1)
                                    dve.wait_ge(w_ready["pairs"], 1)
                                    dve.wait_ge(setup_p, 5)
                                if i in (2, 3):
                                    latent(0, i - 2, psR)
                                if i == 4:
                                    rotated(0, psR)
                                    latent_now(0)
                                if i == 6:
                                    queries(0, 0, psR)
                                if i == 7:
                                    keys(0, 0, psR)
                            j = NX * b + i
                            dve.wait_ge(s["silu"], j + 1)
                            dve.wait_ge(s["down"], NX * b + max(i - 1, 0))
                            a = act_s[:, i % 2, :]
                            if i:
                                dve.wait_ge(s["bc_ps"], NE * b + i)
                                V.tensor_tensor(a, a, bank[:, psG, :], ALU.mult).then_inc(s["sg"], 1)
                                dve.wait_ge(s["sg"], NE * b + i)
                            dve.wait_ge(s["up_ps"], j + 1)
                            V.tensor_tensor(h_s[:, i % 2, :], a, bank[:, 2 + i % 2, :], ALU.mult).then_inc(s["h"], 1)

                    if p == 0:
                        dve.wait_ge(s_x[0], 16)
                        normalise(0, 0)
                        normalised(0, 0)
                        dve.wait_ge(s_moe, 64)
                        V.tensor_copy(router_hi[:], router_raw[:]).then_inc(setup_v, 1)
                        dve.wait_ge(setup_v, 1)
                        V.tensor_tensor(router_lo[:], router_raw[:], router_hi[:].bitcast(F32), ALU.subtract).then_inc(w_ready["router"], 1)
                        x_low(0, 0)
                        up_low(0, UP_A)
                        V.tensor_copy(sel[:].rearrange("p a b -> p (a b)"), sel_raw).then_inc(w_ready["sel"], 1)
                        router_1(s, 0, psR)
                        dve.wait_ge(s_x[1], 16)
                        normalise(1, 1)
                        dve.wait_ge(setup_p, 4)
                        for part in range(3):
                            router_2(s, 0, part)
                    over_batches(dve, p, body)
                elif ph == "attn":
                    def clip(b, pr, g):
                        dve.wait_ge(s["exp"], 5 * (NPAIR * b + pr) + (2, 4, 5)[g])
                        at, n = (0, 2 * L) if g == 0 else (2 * L, 2 * L) if g == 1 else (4 * L, L)
                        t = pb[:, pr % 4, at:at + n]
                        V.tensor_scalar(t, t, P_LOW, P_HIGH, ALU.max, ALU.min).then_inc(s["clip"], 1)

                    def heads(i, g):
                        dve.wait_ge(s["avt_ps"], i + 1)
                        o = bank[:, psH, :].rearrange("p (t h e) -> p t h e", t=TT, h=4)
                        V.reciprocal(rden[:], o[:, :, :, DH]).then_inc(s["rden"], 1)
                        dve.wait_ge(s["rden"], i + 1)
                        V.tensor_tensor(att[:, :, 4 * g:4 * g + 4, :], o[:, :, :, 0:DH],
                                        rden[:].unsqueeze(3).to_broadcast([P, TT, 4, DH]), ALU.mult).then_inc(s["att"], 1)

                    def body(b, last, renorm):
                        first = isinstance(b, int) and b == 0
                        for pr in range(NPAIR):
                            nxt = not (last and pr == NPAIR - 1)
                            i = NPAIR * b + pr + 1
                            if nxt:
                                queries(i, (pr + 1) % 2, psQ)
                            if pr in (4, 6) or pr in (0, 2) and not first:
                                heads(4 * b + (pr - 4) // 2, (pr // 2 + 2) % 4)
                            clip(b, pr, 0)
                            if nxt:
                                keys(i, (pr + 1) % 2, psK)
                            if pr == 2 and not last:
                                latent(b + 1, 0)
                            if pr == 3 and not last:
                                latent(b + 1, 1)
                            if pr == 4 and not last:
                                rotated(b + 1)
                                latent_now(b + 1)
                            if pr == 5:
                                tail_add(p, b, renorm, psH)
                            if pr == 6 and renorm:
                                normalised(n0 + b - 1, before_of(b))
                            if last and p < n_phases - 1:
                                if pr == 3:
                                    router_1(S["moe1"], 0, psH)
                                if pr in (4, 5, 6):
                                    router_2(S["moe1"], 0, pr - 4)
                            if pr == 7 and renorm:
                                x_low(n0 + b - 1, before_of(b), psH)
                            clip(b, pr, 1)
                            clip(b, pr, 2)

                    over_batches(dve, p, body)
                    heads(4 * NB - 2, 2)
                    heads(4 * NB - 1, 3)
                    add_y(n0 + NB - 1, NB - 1, tok(psH), y_ps, NB * (p + 1))
                    if p < n_phases - 1:
                        normalise(n0 + NB - 1, NB - 1)
                elif ph.startswith("tree"):
                    def body(b, last, renorm):
                        first = isinstance(b, int) and b == 0
                        late = after_mix(p, b)
                        if late:
                            normalised(n0 - 2, NB - 2)
                        for t in range(TREES):
                            if t == 1 and late:
                                x_low(n0 - 2, NB - 2)
                            if late and t == 1:
                                tail_stats(p, b)
                            if late and t == 2:
                                tail_norm(p, b)
                            if t == (1 if first and not late else 3):
                                tail_add(p, b, renorm)
                            if t == 5 and renorm:
                                normalised(n0 + b - 1, before_of(b))
                            if t == 6 and renorm:
                                x_low(n0 + b - 1, before_of(b))
                            i = 2 * t
                            dve.wait_ge(s["silu"], NCH * b + i + 1)
                            dve.wait_ge(s["cnt"], at_least(NCH * b + i - 2))
                            V.tensor_scalar(dec[:, t % 2, :], bank[:, i % 4, :], tb[:, i:i + 1], 0.0, ALU.add, ALU.is_gt).then_inc(s["dec"], 1)
                            for c in range(2):
                                j = NCH * b + i + c
                                dve.wait_ge(s["silu"], j + 1)
                                dve.wait_ge(s["cnt"], j + 1)
                                dve.wait_ge(s["h_lo"], at_least(NCH * b + i + c - 3))
                                V.scalar_tensor_tensor(h_s[:, (i + c) % 4, :], bank[:, 6 + c, :], target[:, c:c + 1],
                                                       act_s[:, (i + c) % 4, :], ALU.is_equal, ALU.mult).then_inc(s["mask"], 1)
                    over_batches(dve, p, body)
                elif ph == "mix":
                    def body(b, last, renorm):
                        first = isinstance(b, int) and b == 0
                        dve.wait_ge(s["v_wrap"], b + 1)
                        for i, g in enumerate((0, 1, 3, 4, 6, 7)):
                            j = 6 * b + i
                            dve.wait_ge(s["gate"], 9 * b + g + 1)
                            sh = PADV + SHIFTS[g]
                            k = i // 2
                            if i % 2 == 0:
                                dve.wait_ge(s["summed"], at_least(6 * b + 2 * k - 5))
                            dst = prod_v[:, k, :] if i % 2 == 0 else prod_v2[:, k % 2, :]
                            V.tensor_tensor(dst, act_s[:, g % 3, :], vpad[:, sh:sh + L], ALU.mult).then_inc(s["prod_v"], 1)
                            if i % 2:
                                dve.wait_ge(s["prod_v"], 6 * b + i + 1)
                                V.tensor_tensor(prod_v[:, k, :], prod_v[:, k, :], dst, ALU.add).then_inc(s["pair_v"], 1)
                            if i == 2:
                                tail_stats(p, b)
                            if i == 4:
                                tail_norm(p, b)
                                tail_add(p, b, False)
                            if i == 0 and not first:
                                normalised(n0 + b - 2, before_of(b + NB - 1))
                            if i == 3 and not first:
                                x_low(n0 + b - 2, before_of(b + NB - 1))
                        normalise(n0 + b - 1, before_of(b))
                    over_batches(dve, p, body)
            if PHASES[n_phases - 1] != "attn":
                tail_add(n_phases - 1, NB, False)

        @block.tensor
        def _(pe):
            mm = nc.tensor.matmul

            def xpose(dst, src):
                return nc.tensor.transpose(dst, src, ident[:])

            def three(dst, whi, wlo, b):
                hi, lo = xhi[:, bass.ds(b * L, L)], xlo[:, bass.ds(b * L, L)]
                mm(dst, whi, hi, start=True, stop=False)
                mm(dst, whi, lo, start=False, stop=False)
                return mm(dst, wlo, hi, start=False, stop=True)

            def xn_T(n, bk=psT):
                pe.wait_ge(ln_xn, n + 1)
                pe.wait_ge(x_lo_ready, n)
                for c in range(TT):
                    i = xpose(bank[:, bk, c * P:(c + 1) * P], xn[:, c, :])
                i.then_inc(xn_ps, 1)

            def tail_T(p, b, renorm, bk=psT):
                if summed(p, b) == "y":
                    y_T(NB * sum(q != "attn" for q in PHASES[:p]) + b, NB * (p + 1) + b - 1, renorm, bk)

            def y_T(m, n, renorm, bk=psT):
                pe.wait_ge(y_sb, m)
                pe.wait_ge(x_new, n - NB)
                if renorm:
                    pe.wait_ge(x_lo_ready, n)
                for c in range(TT):
                    i = xpose(bank[:, bk, c * P:(c + 1) * P], yT[:, c * P:(c + 1) * P])
                i.then_inc(y_ps, 1)

            pe.wait_ge(s_const, 16)
            free = {psQ: None, psK: None, psH: None, psR: None}

            ysb = 0
            def router_mm(sM, b, n, bk=psR):
                pe.wait_ge(x_hi_ready, n)
                pe.wait_ge(x_lo_ready, n)
                pe.wait_ge(sM["gT"], b)
                three(bank[:, bk, :], router_hi[:], router_lo[:], b).then_inc(sM["lg_ps"], 1)

            def router_T(sM, b, bk=psR):
                pe.wait_ge(sM["lg_sb"], b + 1)
                for c in range(TT):
                    i = xpose(bank[:, bk, c * P:(c + 1) * P], lgT[:, c * P:(c + 1) * P])
                i.then_inc(sM["lgt_ps"], 1)

            def weights_T(sM, b, bk=psR):
                pe.wait_ge(sM["ghl"], b + 1)
                for c in range(TT):
                    i = xpose(bank[:, bk, c * P:(c + 1) * P], ghl[:, c, :])
                i.then_inc(sM["ghl_ps"], 1)

            def shared(sem_, value, bk=psH):
                if free[bk] is not None:
                    pe.wait_ge(*free[bk])
                free[bk] = (sem_, value)

            def latent(b, k, bk=psH):
                pe.wait_ge(x_lo_ready, NB * A + b + 1)
                shared(S["attn"]["c_done"] if k == 0 else S["attn"]["ck_x"], 2 * b + 1 if k == 0 else b + 1, bk)
                three(bank[:, bk, :], lat_hi[:, k, :], lat_lo[:, k, :], b).then_inc(S["attn"]["lat_ps"], 1)

            def rotary(b, bk=psH):
                pe.wait_ge(S["attn"]["c_done"], 2 * b + 1)
                shared(S["attn"]["rot_x"], b + 1, bk)
                mm(bank[:, bk, :], pair_w[:, 2 * NPAIR + 1, :], CQ[:, bass.ds(b * L, L)], start=True, stop=True).then_inc(S["attn"]["rot_ps"], 1)

            def queries(b, pr, i, bk=psQ):
                rot = bass.ds((b % 2) * L, L)
                pe.wait_ge(S["attn"]["rot"], b + 1)
                shared(S["attn"]["qs"], i + 1, bk)
                mm(bank[:, bk, :], pair_w[:, pr, :], CQ[:, bass.ds(b * L, L)], start=True, stop=False)
                mm(bank[:, bk, :], rot_sel[:, pr, :], rot_hi[:, rot], start=False, stop=False)
                mm(bank[:, bk, :], rot_sel[:, pr, :], rot_lo[:, rot], start=False, stop=True).then_inc(S["attn"]["qp_ps"], 1)

            def keys(b, pr, i, bk=psK):
                shared(S["attn"]["ks"], i + 1, bk)
                mm(bank[:, bk, :], pair_w[:, NPAIR + pr, :], CK[:, bass.ds(b * L, L)], start=True, stop=True).then_inc(S["attn"]["kp_ps"], 1)

            def expert(sM, b, i):
                pe.wait_ge(sM["silu"], NX * b + max(i - 1, 0))
                three(bank[:, i % 2, :], up_hi[:, 2 * i, :], up_lo[:, 2 * i, :], b).then_inc(sM["gate_ps"], 1)
                pe.wait_ge(sM["h"], NX * b + max(i - 1, 0))
                three(bank[:, 2 + i % 2, :], up_hi[:, 2 * i + 1, :], up_lo[:, 2 * i + 1, :], b).then_inc(sM["up_ps"], 1)

            for p, ph in phases():
                s = S[ph]
                n0 = NB * (p + 1)
                if ph.startswith("moe"):
                    def down_mm(b, i):
                        pe.wait_ge(s["h"], NX * b + i + 1)
                        if i == 0:
                            pe.wait_ge(y_sb, ysb + b)
                        mm(bank[:, psO, :], down[:, i, :], h_s[:, i % 2, :], start=(i == 0), stop=(i == NX - 1)).then_inc(s["down"], 1)

                    ahead = p + 1 == A and p < n_phases - 1

                    def body(b, last, renorm):
                        first = isinstance(b, int) and b == 0
                        for i in range(NX):
                            if first and p == 0 and i == 1:
                                pe.wait_ge(w_ready["sel"], 1)
                                pe.wait_ge(s_down, 16)
                            if first and p == 0 and i == 2:
                                pe.wait_ge(w_ready["up"], 2)
                            if not (first and p == A + 1 and i < 2):
                                expert(s, b, i)
                            if i:
                                pe.wait_ge(s["gT"], b + 1)
                                pe.wait_ge(s["sg"], NE * b + i - 1)
                                mm(bank[:, psG, :], sel[:, i - 1, :], gT[:, bass.ds(b * L, L)], start=True, stop=True).then_inc(s["bc_ps"], 1)
                                down_mm(b, i - 1)
                            if first and p == 0:
                                if i == 0:
                                    weights_T(s, 0)
                                if i in (1, 3):
                                    xn_T((i + 1) // 2)
                            if i == 1:
                                tail_T(p, b, renorm)
                            if i == 4 and renorm:
                                xn_T(n0 + b - 1)
                            if not last:
                                if i == 2:
                                    router_mm(s, b + 1, NB * p + b + 2)
                                if i == 3:
                                    router_T(s, b + 1)
                                if i == 8:
                                    weights_T(s, b + 1)
                            elif ahead:
                                if i == 1:
                                    for w in ("latent", "pairs", "rot"):
                                        pe.wait_ge(w_ready[w], 1)
                                    free[psR] = (s["gT"], NB)
                                if i in (1, 2):
                                    latent(0, i - 1, psR)
                                if i == 3:
                                    rotary(0, psR)
                                if i == 5:
                                    queries(0, 0, 0, psR)
                                if i == 6:
                                    keys(0, 0, 0, psR)
                        down_mm(b, NX - 1)

                    if p == 0:
                        xn_T(0)
                        pe.wait_ge(w_ready["router"], 1)
                        router_mm(s, 0, 1)
                        router_T(s, 0)
                        pe.wait_ge(w_ready["up"], 1)
                    over_batches(pe, p, body)
                    ysb += NB
                elif ph == "attn":
                    def scores(b, pr, ks):
                        pe.wait_ge(s["qs"], NPAIR * b + pr + 1)
                        pe.wait_ge(s["ks"], NPAIR * b + pr + 1)
                        for k in ks:
                            pe.wait_ge(s["exp"], at_least(5 * (NPAIR * b + pr) + k - 3))
                            heads = (0, 1) if k == 4 else (k % 2,)
                            for kt, col in (((0, 0),), ((3, 0), (1, P)), ((2, 0),))[k // 2]:
                                for j in heads:
                                    at = j * (L // 2) if k == 4 else col
                                    ins = mm(bank[:, (5 * pr + k) % 4, at:at + L - P * kt], KS[:, pr % 2, j, kt * P:(kt + 1) * P],
                                             QS[:, pr % 2, kt * P:L], start=True, stop=True)
                            ins.then_inc(s["scores"], 1)

                    def values(b, pr, part):
                        b, g = (b - 1, 3) if pr < 2 else (b, (pr - 2) // 2)
                        kt, at, stride, slot = ((0, 0, L, 0), (1, 2 * L + P, L, 1), (3, 2 * L, L, 1), (2, 4 * L, L // 2, 2))[2 * (pr % 2) + part]
                        pe.wait_ge(s["masked"], 3 * (NPAIR * b + 2 * g + 1) + slot + 1)
                        if kt == 0:
                            pe.wait_ge(s["v_sb"], b + 1)
                            pe.wait_ge(s["avT"], at_least(4 * b + g))
                        for q in range(4):
                            c = at + stride * (q % 2)
                            ins = mm(bank[32 * q:32 * q + 32, psR, kt * P:L], v_aug[:, kt, 4 * g + q, :],
                                     pb[:, (2 * g + q // 2) % 4, c:c + L - P * kt], start=(kt == 0), stop=(kt == 2))
                        if kt == 2:
                            ins.then_inc(s["av"], 1)

                    def heads_T(i):
                        pe.wait_ge(s["avT"], i + 1)
                        shared(s["att"], i + 1)
                        for c in range(TT):
                            ins = xpose(bank[:, psH, c * P:(c + 1) * P], avT[:, c * P:(c + 1) * P])
                        ins.then_inc(s["avt_ps"], 1)

                    def att_T(b):
                        pe.wait_ge(s["att"], 4 * b + 4)
                        shared(s["attT"], b + 1)
                        for c in range(TT):
                            ins = xpose(bank[:, psH, c * P:(c + 1) * P], att[:, c].rearrange("p h e -> p (h e)"))
                        ins.then_inc(s["att_ps"], 1)

                    def output(b):
                        pe.wait_ge(s["attT"], b + 1)
                        shared(x_new, NB * p + b + 1, psH)
                        for c in range(TT):
                            ins = mm(bank[:, psH, c * P:(c + 1) * P], attT[:, c * P:(c + 1) * P], wo[:], start=True, stop=True)
                        ins.then_inc(y_ps, 1)

                    def batch_values(b):
                        pe.wait_ge(s["ck_now"], b + 1)
                        shared(s["v_sb"], b + 1)
                        for c in range(TT):
                            ins = mm(bank[:, psH, c * P:(c + 1) * P], ck_now[:, c * P:(c + 1) * P], pair_w[:, 2 * NPAIR, :], start=True, stop=True)
                        ins.then_inc(s["v_ps"], 1)

                    def body(b, last, renorm):
                        first = isinstance(b, int) and b == 0
                        if not first:
                            free[psQ], free[psK], free[psH] = (s["qs"], NPAIR * b + 1), (s["ks"], NPAIR * b + 1), (x_lo_ready, n0 + b - 1)
                        for pr in range(NPAIR):
                            i = NPAIR * b + pr + 1
                            nb, npr = (b, pr + 1) if pr < NPAIR - 1 else (b + 1, 0)
                            nxt = not (last and pr == NPAIR - 1)
                            if nxt:
                                queries(nb, npr, i)
                                keys(nb, npr, i)
                            scores(b, pr, (0, 1))
                            if pr in (4, 6) or pr in (0, 2) and not first:
                                heads_T(4 * b + (pr - 4) // 2)
                            if pr == 3 and not first:
                                att_T(b - 1)
                            if pr > 1 or not first:
                                values(b, pr, 0)
                            scores(b, pr, (2, 3, 4))
                            if pr == 2 and not last:
                                latent(b + 1, 0)
                            if pr == 3 and not last:
                                latent(b + 1, 1)
                            if pr == 4 and not last:
                                rotary(b + 1)
                            if pr == 5:
                                if first:
                                    shared(x_new, NB * p, psH)
                                    tail_T(p, b, renorm, psH)
                                else:
                                    output(b - 1)
                            if last and p < n_phases - 1:
                                if pr == 2:
                                    shared(S["moe1"]["lg_sb"], 1, psH)
                                    router_mm(S["moe1"], 0, NB * (p + 1) + 1, psH)
                                if pr == 3:
                                    shared(S["moe1"]["r_chain"], 1, psH)
                                    router_T(S["moe1"], 0, psH)
                                if pr == 7:
                                    shared(S["moe1"]["gT"], 1, psH)
                                    weights_T(S["moe1"], 0, psH)
                            if pr == 7 and renorm:
                                shared(x_lo_ready, n0 + b, psH)
                                xn_T(n0 + b - 1, psH)
                            if pr > 1 or not first:
                                values(b, pr, 1)
                            if pr == 1:
                                batch_values(b)

                    pe.wait_ge(setup_p, 4)
                    pe.wait_ge(y_sb, ysb)
                    pe.wait_ge(x_lo_ready, n0 - 1)
                    over_batches(pe, p, body)
                    heads_T(4 * NB - 2)
                    for part in range(4):
                        values(NB, part // 2, part % 2)
                    if p < n_phases - 1:
                        pe.wait_ge(s["exp"], 5 * NPAIR * NB)
                        expert(S["moe1"], 0, 0)
                    heads_T(4 * NB - 1)
                    att_T(NB - 1)
                    if p < n_phases - 1:
                        expert(S["moe1"], 0, 1)
                    output(NB - 1)
                    pe.wait_ge(*free[psH])
                elif ph.startswith("tree"):
                    def logits(b, i):
                        pe.wait_ge(s["silu"], at_least(NCH * b + i - 3))
                        if i % 2 == 0:
                            pe.wait_ge(s["dec"], at_least(TREES * b + i // 2 - 1))
                        three(bank[:, i % 4, :], tin_hi[:, i, :], tin_lo[:, i, :], b).then_inc(s["logit_ps"], 1)

                    def count(b, t):
                        pe.wait_ge(s["dec"], TREES * b + t + 1)
                        if after_mix(p, b) and t == 0:
                            pe.wait_ge(y_sb, ysb)
                        for c in range(2):
                            pe.wait_ge(s["mask"], at_least(NCH * b + 2 * t + c - 1))
                            mm(bank[:, 6 + c, :], path[:, c, :], dec[:, t % 2, :], start=True, stop=True).then_inc(s["cnt"], 1)

                    def out_mm(b, i):
                        pe.wait_ge(s["h_hi"], NCH * b + i + 1)
                        if i == 0:
                            pe.wait_ge(y_sb, ysb + b)
                        mm(bank[:, psO, :], tout_hi[:, i, :], node_hi[i % 4], start=(i == 0), stop=False)
                        mm(bank[:, psO, :], tout_lo[:, i, :], node_hi[i % 4], start=False, stop=False)
                        pe.wait_ge(s["h_lo"], NCH * b + i + 1)
                        mm(bank[:, psO, :], tout_hi[:, i, :], node_lo[i % 4], start=False, stop=(i == NCH - 1)).then_inc(s["outp"], 1)

                    def body(b, last, renorm):
                        first = isinstance(b, int) and b == 0
                        if first:
                            pe.wait_ge(x_lo_ready, NB * p + 1)
                            logits(0, 0)
                            logits(0, 1)
                        for t in range(TREES):
                            nb, nt = (b, t + 1) if t < TREES - 1 else (b + 1, 0)
                            nxt = not (last and t == TREES - 1)
                            if nxt and nt == 0:
                                pe.wait_ge(x_lo_ready, NB * p + b + 2)
                            if nxt:
                                logits(nb, 2 * nt)
                            count(b, t)
                            if nxt:
                                logits(nb, 2 * nt + 1)
                            if t == 0 and after_mix(p, b):
                                xn_T(n0 - 2)
                            if t == (0 if first else 2):
                                tail_T(p, b, renorm)
                            if t == 5 and renorm:
                                xn_T(n0 + b - 1)
                            if t or not first:
                                for i in (2 * t - 2, 2 * t - 1):
                                    out_mm(b if t else b - 1, i % NCH)

                    pe.wait_ge(w_ready["tin"], 1)
                    pe.wait_ge(w_ready["path"], 1)
                    pe.wait_ge(w_ready["tout"], 1)
                    pe.wait_ge(s_late, LATE)
                    over_batches(pe, p, body)
                    for i in (NCH - 2, NCH - 1):
                        out_mm(NB - 1, i)
                    ysb += NB
                elif ph == "mix":
                    def add_product(b, j):
                        if j == 0:
                            pe.wait_ge(y_sb, ysb + b)
                        if j % 2:
                            pe.wait_ge(s["prod_p"], 3 * b + j // 2 + 1)
                            src = prod_p[:, j // 2, :]
                        else:
                            pe.wait_ge(s["pair_v"], 3 * b + j // 2 + 1)
                            src = prod_v[:, j // 2, :]
                        for c in range(TT):
                            ins = mm(bank[:, psG, c * P:(c + 1) * P], src[:, c * P:(c + 1) * P], ident[:],
                                     start=(j == 0 and c == 0), stop=(j == 5 and c == TT - 1))
                        ins.then_inc(s["summed"], 1)

                    def body(b, last, renorm):
                        pe.wait_ge(x_lo_ready, NB * p + b + 1)
                        if isinstance(b, int) and b == 0:
                            pe.wait_ge(y_sb, ysb)
                        else:
                            pe.wait_ge(s["v_sb"], b)
                        three(bank[:, psO, :], mix_hi[:, 0, :], mix_lo[:, 0, :], b).then_inc(s["v_ps"], 1)
                        for g in range(9):
                            pe.wait_ge(s["gate"], 9 * b + max(g - 2, 0))
                            three(bank[:, g % 3, :], mix_hi[:, g + 1, :], mix_lo[:, g + 1, :], b).then_inc(s["gate_ps"], 1)
                            if g in (3, 4, 6, 8):
                                add_product(b, (3, 4, 6, 8).index(g))
                            elif g < 2 and not (isinstance(b, int) and b == 0):
                                add_product(b - 1, g + 4)
                            if g == 2:
                                tail_T(p, b, renorm)
                            if g == 3 and not (isinstance(b, int) and b == 0):
                                xn_T(n0 + b - 2)
                    pe.wait_ge(w_ready["mixw"], 1)
                    over_batches(pe, p, body)
                    add_product(NB - 1, 4)
                    add_product(NB - 1, 5)
                    pe.wait_ge(s["gate"], 9 * NB)
                    ysb += NB
            if PHASES[n_phases - 1] != "attn":
                tail_T(n_phases - 1, NB, False)


def kernel(**inputs):
    import concourse.bacc as _bacc
    from concourse import mybir as _mybir
    from concourse.bass_utils import run_bass_kernel_spmd as _run

    nc = _bacc.Bacc("TRN2", target_bir_lowering=False, num_devices=1)
    arrays = lay_out(inputs)
    d = {name: nc.dram_tensor("in_" + name, a.shape, _mybir.dt.float32, kind="ExternalInput").ap() for name, a in arrays.items()}
    out = nc.dram_tensor("out", arrays["x"].shape, _mybir.dt.float32, kind="ExternalOutput").ap()
    macaron(nc, d, out)
    r = _run(nc, [{"in_" + k: v for k, v in arrays.items()}], core_ids=[0])
    return r.results[0]["out"]
```
